# Optimizing a Trainium2 kernel written in Bass

```python
import numpy as np
import jax
import jax.numpy as jnp

def _softmax(x, axis=-1):
    return jax.nn.softmax(x, axis=axis)

def _gelu(x):
    return jax.nn.gelu(x, approximate=True)

def _silu(x):
    return jax.nn.silu(x)

def _sigmoid(x):
    return jax.nn.sigmoid(x)

def _layernorm(x, axis=-1, eps=1e-05):
    m = jnp.mean(x, axis=axis, keepdims=True)
    v = jnp.var(x, axis=axis, keepdims=True)
    return (x - m) / jnp.sqrt(v + eps)

def _scatter_add(tgt, idx, src, axis=0):
    return tgt.at[idx].add(src)

def _segment_sum(src, seg, n):
    return jax.ops.segment_sum(src, seg, n)
kernel_name = 'mk_perceiver_d2_seqx_r8_e801e3'

def setup_inputs(seed: int=0):
    np.random.seed(seed)
    _w = jnp.asarray

    def _rec_inputs():
        import jax
        import jax.numpy as jnp
        _rk = jax.random.key(seed)
        x = -0.000125 + 0.9999 * jax.random.normal(jax.random.fold_in(_rk, 1), (1, 64, 128), jnp.float32)
        _lenS = 64 - jax.random.randint(jax.random.fold_in(_rk, 7), (1,), 0, max(1, 64 // 4) + 1, jnp.int32)
        _lenS2 = 6272 - jax.random.randint(jax.random.fold_in(_rk, 8), (1,), 0, max(1, 6272 // 4) + 1, jnp.int32)
        _ctx_1024P = jax.random.normal(jax.random.fold_in(_rk, 11), (1, 16, 128), jnp.float32)
        _ctx_1024c = jax.random.dirichlet(jax.random.fold_in(_rk, 511), 0.3 * jnp.ones((16,), jnp.float32), (1, 6272))
        _ctx_1024t = jnp.einsum('bsk,bkd->bsd', _ctx_1024c, _ctx_1024P)
        _ctx_1024t = _ctx_1024t * jax.lax.rsqrt(jnp.mean(jnp.square(_ctx_1024t)) + 1e-12) * 0.953939
        ctx_1024 = -1.52775e-05 + 0.999936 * (_ctx_1024t + 0.3 * jax.random.normal(jax.random.fold_in(_rk, 611), (1, 6272, 128), jnp.float32))
        return (x, ctx_1024)
    x, ctx_1024 = _rec_inputs()

    def _L0_xattn_setup():
        import jax, jax.numpy as jnp
        import numpy as np
        B, LP, LQ, H = (16, 256, 256, 128)
        key = jax.random.key(seed)
        k1, k2, k3 = jax.random.split(key, 3)
        proj_p = jax.random.normal(k1, (B, LP, H), dtype=jnp.float32)
        proj_q = jax.random.normal(k2, (B, LQ, H), dtype=jnp.float32)
        W = jax.random.normal(k3, (H, H), dtype=jnp.float32) * (1.0 / np.sqrt(H))
        b = jnp.zeros((H,), dtype=jnp.float32)
        return {'proj_p': proj_p, 'proj_q': proj_q, 'W': W, 'b': b}
    _L0_xattn_all = _L0_xattn_setup()
    _L0_xattn_in = {k: v for k, v in _L0_xattn_all.items() if k in ('W', 'b')}
    del _L0_xattn_all

    def _L0_attn_setup():
        import jax, jax.numpy as jnp
        import numpy as np
        B, N, EMBED, HEADS = (1, 256, 128, 16)
        HD = EMBED // HEADS
        BASE = 10000.0
        EPS = 1e-05

        def _rope(t):
            d = t.shape[-1]
            n = t.shape[-2]
            inv_freq = 1.0 / BASE ** (jnp.arange(0, d, 2, dtype=jnp.float32) / d)
            pos = jnp.arange(n, dtype=jnp.float32)
            ang = pos[:, None] * inv_freq[None, :]
            cos = jnp.concatenate([jnp.cos(ang), jnp.cos(ang)], axis=-1)
            sin = jnp.concatenate([jnp.sin(ang), jnp.sin(ang)], axis=-1)
            t1, t2 = (t[..., :d // 2], t[..., d // 2:])
            rot = jnp.concatenate([-t2, t1], axis=-1)
            return t * cos + rot * sin
        key = jax.random.key(seed)
        ks = jax.random.split(key, 7)
        s = EMBED ** (-0.5)
        return {'x': jax.random.normal(ks[0], (B, N, EMBED), dtype=jnp.float32), 'Wq': jax.random.normal(ks[1], (EMBED, EMBED), dtype=jnp.float32) * s, 'Wk': jax.random.normal(ks[2], (EMBED, EMBED), dtype=jnp.float32) * s, 'Wv': jax.random.normal(ks[3], (EMBED, EMBED), dtype=jnp.float32) * s, 'Wo': jax.random.normal(ks[4], (EMBED, EMBED), dtype=jnp.float32) * s, 'Wg1': jax.random.normal(ks[5], (EMBED, HD), dtype=jnp.float32) * s, 'Wg2': jax.random.normal(ks[6], (HD, EMBED), dtype=jnp.float32) * HD ** (-0.5), 'ln_w': jnp.ones((EMBED,), dtype=jnp.float32), 'ln_b': jnp.zeros((EMBED,), dtype=jnp.float32)}
    _L0_attn_all = _L0_attn_setup()
    _L0_attn_in = {k: v for k, v in _L0_attn_all.items() if k in ('Wq', 'Wk', 'Wv', 'Wo', 'Wg1', 'Wg2', 'ln_w', 'ln_b')}
    del _L0_attn_all

    def _L0_ffn_setup():
        import jax, jax.numpy as jnp
        import numpy as np
        S, B, D, H, DH = (512, 8, 128, 16, 64)

        def _forward(x, Wg, Wq, bq, Wkv, bkv, Wo, bo, ln_g, ln_b):
            s_len, bsz, d_model = x.shape
            n_head, _, d_head = Wq.shape
            cap = s_len // n_head
            scale = 1.0 / d_head ** 0.5
            h = jnp.transpose(x, (1, 0, 2))
            t = h
            probs = jax.nn.softmax(h @ Wg, axis=-1)
            scores = jnp.transpose(probs, (0, 2, 1))
            _, idx = jax.lax.top_k(scores, cap)
            idx = jnp.sort(idx, axis=-1)
            hg = jnp.take_along_axis(h[:, None, :, :], idx[..., None], axis=2)
            hg = jnp.transpose(hg, (1, 0, 2, 3))
            q = jnp.einsum('hbcd,hde->hbce', hg, Wq) + bq[:, None, None, :]
            kv = jnp.einsum('hbcd,hde->hbce', hg, Wkv) + bkv[:, None, None, :]
            k, v = jnp.split(kv, 2, axis=-1)
            att = jnp.einsum('hbid,hbjd->hbij', q, k) * scale
            p = jax.nn.softmax(att, axis=1)
            av = jnp.einsum('hbij,hbjd->hbid', p, v)
            ao = jnp.einsum('hbid,hde->hbie', av, Wo) + bo
            tok = jnp.transpose(idx, (1, 0, 2))
            b_ids = jnp.arange(bsz)[None, :, None]
            outs = jnp.zeros_like(t).at[b_ids, tok].add(ao)
            y = t + outs
            mu = jnp.mean(y, axis=-1, keepdims=True)
            var = jnp.var(y, axis=-1, keepdims=True)
            yn = (y - mu) * jax.lax.rsqrt(var + 1e-05) * ln_g + ln_b
            return jnp.transpose(yn, (1, 0, 2))
        key = jax.random.key(seed)
        ks = jax.random.split(key, 6)
        s = 0.02
        return {'x': jax.random.normal(ks[0], (S, B, D), jnp.float32), 'attn_mask': jnp.zeros((S, S), jnp.bool_), 'Wg': jax.random.normal(ks[1], (D, H), jnp.float32) * s, 'Wq': jax.random.normal(ks[2], (H, D, DH), jnp.float32) * s, 'bq': jnp.zeros((H, DH), jnp.float32), 'Wkv': jax.random.normal(ks[3], (H, D, 2 * DH), jnp.float32) * s, 'bkv': jnp.zeros((H, 2 * DH), jnp.float32), 'Wo': jax.random.normal(ks[4], (H, DH, D), jnp.float32) * s, 'bo': jnp.zeros((D,), jnp.float32), 'ln_g': jnp.ones((D,), jnp.float32), 'ln_b': jnp.zeros((D,), jnp.float32)}
    _L0_ffn_all = _L0_ffn_setup()
    _L0_ffn_in = {k: v for k, v in _L0_ffn_all.items() if k in ('attn_mask', 'Wg', 'Wq', 'bq', 'Wkv', 'bkv', 'Wo', 'bo', 'ln_g', 'ln_b')}
    del _L0_ffn_all

    def _L1_xattn_setup():
        import jax, jax.numpy as jnp
        import numpy as np
        B, NT, NM, C, H, FF = (8, 128, 256, 128, 8, 512)

        def _ln(x, g, b):
            m = x.mean(-1, keepdims=True)
            v = jnp.mean((x - m) ** 2, axis=-1, keepdims=True)
            return (x - m) / jnp.sqrt(v + 1e-05) * g + b
        key = jax.random.key(seed)
        ks = jax.random.split(key, 8)
        w = lambda k, shape, s=0.02: jax.random.normal(k, shape, dtype=jnp.float32) * s
        return {'tgt': jax.random.normal(ks[0], (B, NT, C), dtype=jnp.float32), 'memory': jax.random.normal(ks[1], (B, NM, C), dtype=jnp.float32), 'qkv_w': w(ks[2], (3 * C, C)), 'qkv_b': jnp.zeros((3 * C,), jnp.float32), 'sa_out_w': w(ks[3], (C, C)), 'sa_out_b': jnp.zeros((C,), jnp.float32), 'in_proj_w': w(ks[4], (3 * C, C)), 'in_proj_b': jnp.zeros((3 * C,), jnp.float32), 'mha_out_w': w(ks[5], (C, C)), 'mha_out_b': jnp.zeros((C,), jnp.float32), 'lin1_w': w(ks[6], (FF, C)), 'lin1_b': jnp.zeros((FF,), jnp.float32), 'lin2_w': w(ks[7], (C, FF)), 'lin2_b': jnp.zeros((C,), jnp.float32), 'ln1_g': jnp.ones((C,), jnp.float32), 'ln1_b': jnp.zeros((C,), jnp.float32), 'ln2_g': jnp.ones((C,), jnp.float32), 'ln2_b': jnp.zeros((C,), jnp.float32), 'ln3_g': jnp.ones((C,), jnp.float32), 'ln3_b': jnp.zeros((C,), jnp.float32)}
    _L1_xattn_all = _L1_xattn_setup()
    _L1_xattn_in = {k: v for k, v in _L1_xattn_all.items() if k in ('qkv_w', 'qkv_b', 'sa_out_w', 'sa_out_b', 'in_proj_w', 'in_proj_b', 'mha_out_w', 'mha_out_b', 'lin1_w', 'lin1_b', 'lin2_w', 'lin2_b', 'ln1_g', 'ln1_b', 'ln2_g', 'ln2_b', 'ln3_g', 'ln3_b')}
    del _L1_xattn_all

    def _L1_attn_setup():
        import jax, jax.numpy as jnp
        import numpy as np
        DM, EXP, N, K, FRAC = (128, 2, 16, 4, 16)
        D = DM * EXP
        DTR = D // FRAC
        EPS = 1e-06

        def _mamba_block(x, rms_w, in_W, in_b, conv_w, conv_b, A_log, dbc_W, dbc_b, dup_W, dup_b, out_W, out_b):
            residual = x
            h = x * jax.lax.rsqrt(jnp.mean(x * x, axis=-1, keepdims=True) + EPS) * rms_w
            proj = h @ in_W + in_b
            x1, g = (proj[..., :D], proj[..., D:])
            xt = jnp.transpose(x1, (0, 2, 1))
            xc = jax.lax.conv_general_dilated(xt, conv_w[:, None, :], window_strides=(1,), padding=[(K - 1, 0)], feature_group_count=D, dimension_numbers=('NCH', 'OIH', 'NCH'))
            xc = xc + conv_b[:, None]
            x1 = jax.nn.silu(jnp.transpose(xc, (0, 2, 1)))
            A = -jnp.exp(A_log)
            dbc = x1 @ dbc_W + dbc_b
            delta, Bm, Cm = (dbc[..., :DTR], dbc[..., DTR:DTR + N], dbc[..., DTR + N:])
            delta = jax.nn.softplus(delta @ dup_W + dup_b)
            A_disc = jnp.exp(delta[..., None] * A)
            B_x = delta[..., None] * Bm[:, :, None, :] * x1[..., None]
            Ad_t = jnp.transpose(A_disc, (1, 0, 2, 3))
            Bx_t = jnp.transpose(B_x, (1, 0, 2, 3))

            def step(hc, inp):
                a, b = inp
                hc = a * hc + b
                return (hc, hc)
            h0 = jnp.zeros((x.shape[0], D, N), x1.dtype)
            _, hs = jax.lax.scan(step, h0, (Ad_t, Bx_t))
            y = jnp.einsum('tbdn,btn->btd', hs, Cm)
            y = jax.nn.silu(g) * y
            out = y @ out_W + out_b
            return out + residual
        key = jax.random.key(seed)
        ks = jax.random.split(key, 12)
        s = lambda fan: 1.0 / np.sqrt(fan)
        x = jax.random.normal(ks[0], (2, 128, DM), jnp.float32)
        rms_w = jnp.ones((DM,), jnp.float32)
        in_W = jax.random.normal(ks[1], (DM, 2 * D), jnp.float32) * s(DM)
        in_b = jax.random.normal(ks[2], (2 * D,), jnp.float32) * s(DM)
        conv_w = jax.random.normal(ks[3], (D, K), jnp.float32) * s(K)
        conv_b = jax.random.normal(ks[4], (D,), jnp.float32) * s(K)
        A_log = jnp.log(jnp.tile(jnp.arange(1, N + 1, dtype=jnp.float32), (D, 1)))
        dbc_W = jax.random.normal(ks[5], (D, DTR + 2 * N), jnp.float32) * s(D)
        dbc_b = jax.random.normal(ks[6], (DTR + 2 * N,), jnp.float32) * s(D)
        dup_W = jax.random.normal(ks[7], (DTR, D), jnp.float32) * s(DTR)
        dup_b = jax.random.normal(ks[8], (D,), jnp.float32) * s(DTR)
        out_W = jax.random.normal(ks[9], (D, DM), jnp.float32) * s(D)
        out_b = jax.random.normal(ks[10], (DM,), jnp.float32) * s(D)
        return dict(x=x, rms_w=rms_w, in_W=in_W, in_b=in_b, conv_w=conv_w, conv_b=conv_b, A_log=A_log, dbc_W=dbc_W, dbc_b=dbc_b, dup_W=dup_W, dup_b=dup_b, out_W=out_W, out_b=out_b)
    _L1_attn_all = _L1_attn_setup()
    _L1_attn_in = {k: v for k, v in _L1_attn_all.items() if k in ('rms_w', 'in_W', 'in_b', 'conv_w', 'conv_b', 'A_log', 'dbc_W', 'dbc_b', 'dup_W', 'dup_b', 'out_W', 'out_b')}
    del _L1_attn_all

    def _L1_ffn_setup():
        import jax, jax.numpy as jnp
        import numpy as np
        D_MODEL = 128
        EXPANSION = 4
        D_HIDDEN = D_MODEL * EXPANSION
        NUM_STAGES = int(np.log2(D_HIDDEN))

        def butterfly(y, weights, dim):
            lead = y.shape[:-1]
            for stage in range(weights.shape[0]):
                s = 2 ** stage
                nb = dim // (2 * s)
                yr = y.reshape(*lead, nb, 2, s)
                a = yr[..., 0, :]
                b = yr[..., 1, :]
                w = weights[stage].reshape(nb, s, 2, 2)
                na = w[..., 0, 0] * a + w[..., 0, 1] * b
                nb2 = w[..., 1, 0] * a + w[..., 1, 1] * b
                y = jnp.stack([na, nb2], axis=-2).reshape(*lead, dim)
            return y
        key = jax.random.key(seed)
        ks = jax.random.split(key, 6)
        B, S = (4, 256)
        x = jax.random.normal(ks[0], (B, S, D_MODEL), jnp.float32)
        W_exp = jax.random.normal(ks[1], (D_MODEL, D_HIDDEN), jnp.float32) * 0.02
        b_exp = jnp.zeros((D_HIDDEN,), jnp.float32)
        up_weights = jax.random.normal(ks[2], (NUM_STAGES, D_HIDDEN // 2, 2, 2), jnp.float32) * 0.02
        up_bias = jnp.zeros((D_HIDDEN,), jnp.float32)
        down_weights = jax.random.normal(ks[3], (NUM_STAGES, D_HIDDEN // 2, 2, 2), jnp.float32) * 0.02
        W_con = jax.random.normal(ks[4], (D_HIDDEN, D_MODEL), jnp.float32) * 0.02
        b_con = jnp.zeros((D_MODEL,), jnp.float32)
        down_bias = jnp.zeros((D_MODEL,), jnp.float32)
        return dict(x=x, W_exp=W_exp, b_exp=b_exp, up_weights=up_weights, up_bias=up_bias, down_weights=down_weights, W_con=W_con, b_con=b_con, down_bias=down_bias)
    _L1_ffn_all = _L1_ffn_setup()
    _L1_ffn_in = {k: v for k, v in _L1_ffn_all.items() if k in ('W_exp', 'b_exp', 'up_weights', 'up_bias', 'down_weights', 'W_con', 'b_con', 'down_bias')}
    del _L1_ffn_all
    return {'x': x, 'ctx_1024': ctx_1024, 'L0_xattn_W': _L0_xattn_in['W'], 'L0_xattn_b': _L0_xattn_in['b'], 'L0_attn_Wq': _L0_attn_in['Wq'], 'L0_attn_Wk': _L0_attn_in['Wk'], 'L0_attn_Wv': _L0_attn_in['Wv'], 'L0_attn_Wo': _L0_attn_in['Wo'], 'L0_attn_Wg1': _L0_attn_in['Wg1'], 'L0_attn_Wg2': _L0_attn_in['Wg2'], 'L0_attn_ln_w': _L0_attn_in['ln_w'], 'L0_attn_ln_b': _L0_attn_in['ln_b'], 'L0_ffn_attn_mask': _L0_ffn_in['attn_mask'], 'L0_ffn_Wg': _L0_ffn_in['Wg'], 'L0_ffn_Wq': _L0_ffn_in['Wq'], 'L0_ffn_bq': _L0_ffn_in['bq'], 'L0_ffn_Wkv': _L0_ffn_in['Wkv'], 'L0_ffn_bkv': _L0_ffn_in['bkv'], 'L0_ffn_Wo': _L0_ffn_in['Wo'], 'L0_ffn_bo': _L0_ffn_in['bo'], 'L0_ffn_ln_g': _L0_ffn_in['ln_g'], 'L0_ffn_ln_b': _L0_ffn_in['ln_b'], 'L1_xattn_qkv_w': _L1_xattn_in['qkv_w'], 'L1_xattn_qkv_b': _L1_xattn_in['qkv_b'], 'L1_xattn_sa_out_w': _L1_xattn_in['sa_out_w'], 'L1_xattn_sa_out_b': _L1_xattn_in['sa_out_b'], 'L1_xattn_in_proj_w': _L1_xattn_in['in_proj_w'], 'L1_xattn_in_proj_b': _L1_xattn_in['in_proj_b'], 'L1_xattn_mha_out_w': _L1_xattn_in['mha_out_w'], 'L1_xattn_mha_out_b': _L1_xattn_in['mha_out_b'], 'L1_xattn_lin1_w': _L1_xattn_in['lin1_w'], 'L1_xattn_lin1_b': _L1_xattn_in['lin1_b'], 'L1_xattn_lin2_w': _L1_xattn_in['lin2_w'], 'L1_xattn_lin2_b': _L1_xattn_in['lin2_b'], 'L1_xattn_ln1_g': _L1_xattn_in['ln1_g'], 'L1_xattn_ln1_b': _L1_xattn_in['ln1_b'], 'L1_xattn_ln2_g': _L1_xattn_in['ln2_g'], 'L1_xattn_ln2_b': _L1_xattn_in['ln2_b'], 'L1_xattn_ln3_g': _L1_xattn_in['ln3_g'], 'L1_xattn_ln3_b': _L1_xattn_in['ln3_b'], 'L1_attn_rms_w': _L1_attn_in['rms_w'], 'L1_attn_in_W': _L1_attn_in['in_W'], 'L1_attn_in_b': _L1_attn_in['in_b'], 'L1_attn_conv_w': _L1_attn_in['conv_w'], 'L1_attn_conv_b': _L1_attn_in['conv_b'], 'L1_attn_A_log': _L1_attn_in['A_log'], 'L1_attn_dbc_W': _L1_attn_in['dbc_W'], 'L1_attn_dbc_b': _L1_attn_in['dbc_b'], 'L1_attn_dup_W': _L1_attn_in['dup_W'], 'L1_attn_dup_b': _L1_attn_in['dup_b'], 'L1_attn_out_W': _L1_attn_in['out_W'], 'L1_attn_out_b': _L1_attn_in['out_b'], 'L1_ffn_W_exp': _L1_ffn_in['W_exp'], 'L1_ffn_b_exp': _L1_ffn_in['b_exp'], 'L1_ffn_up_weights': _L1_ffn_in['up_weights'], 'L1_ffn_up_bias': _L1_ffn_in['up_bias'], 'L1_ffn_down_weights': _L1_ffn_in['down_weights'], 'L1_ffn_W_con': _L1_ffn_in['W_con'], 'L1_ffn_b_con': _L1_ffn_in['b_con'], 'L1_ffn_down_bias': _L1_ffn_in['down_bias']}

def reference(x, ctx_1024, L0_xattn_W, L0_xattn_b, L0_attn_Wq, L0_attn_Wk, L0_attn_Wv, L0_attn_Wo, L0_attn_Wg1, L0_attn_Wg2, L0_attn_ln_w, L0_attn_ln_b, L0_ffn_attn_mask, L0_ffn_Wg, L0_ffn_Wq, L0_ffn_bq, L0_ffn_Wkv, L0_ffn_bkv, L0_ffn_Wo, L0_ffn_bo, L0_ffn_ln_g, L0_ffn_ln_b, L1_xattn_qkv_w, L1_xattn_qkv_b, L1_xattn_sa_out_w, L1_xattn_sa_out_b, L1_xattn_in_proj_w, L1_xattn_in_proj_b, L1_xattn_mha_out_w, L1_xattn_mha_out_b, L1_xattn_lin1_w, L1_xattn_lin1_b, L1_xattn_lin2_w, L1_xattn_lin2_b, L1_xattn_ln1_g, L1_xattn_ln1_b, L1_xattn_ln2_g, L1_xattn_ln2_b, L1_xattn_ln3_g, L1_xattn_ln3_b, L1_attn_rms_w, L1_attn_in_W, L1_attn_in_b, L1_attn_conv_w, L1_attn_conv_b, L1_attn_A_log, L1_attn_dbc_W, L1_attn_dbc_b, L1_attn_dup_W, L1_attn_dup_b, L1_attn_out_W, L1_attn_out_b, L1_ffn_W_exp, L1_ffn_b_exp, L1_ffn_up_weights, L1_ffn_up_bias, L1_ffn_down_weights, L1_ffn_W_con, L1_ffn_b_con, L1_ffn_down_bias):
    import jax
    import jax.numpy as jnp

    def _L0_xattn_ref(proj_p, proj_q, W, b):
        import jax, jax.numpy as jnp
        import numpy as np
        B, LP, LQ, H = (16, 256, 256, 128)
        trans_q = jnp.einsum('bqh,oh->bqo', proj_q, W) + b
        att_weights = jnp.einsum('bph,bqh->bpq', proj_p, trans_q)
        att_norm = jax.nn.softmax(att_weights, axis=-1)
        att_vec = jnp.einsum('bpq,bqh->bph', att_norm, proj_q)
        out = jax.nn.relu(jnp.einsum('bph,oh->bpo', att_vec, W) + b)
        return out

    def _L0_attn_ref(x, Wq, Wk, Wv, Wo, Wg1, Wg2, ln_w, ln_b):
        import jax, jax.numpy as jnp
        import numpy as np
        B, N, EMBED, HEADS = (1, 256, 128, 16)
        HD = EMBED // HEADS
        BASE = 10000.0
        EPS = 1e-05

        def _rope(t):
            d = t.shape[-1]
            n = t.shape[-2]
            inv_freq = 1.0 / BASE ** (jnp.arange(0, d, 2, dtype=jnp.float32) / d)
            pos = jnp.arange(n, dtype=jnp.float32)
            ang = pos[:, None] * inv_freq[None, :]
            cos = jnp.concatenate([jnp.cos(ang), jnp.cos(ang)], axis=-1)
            sin = jnp.concatenate([jnp.sin(ang), jnp.sin(ang)], axis=-1)
            t1, t2 = (t[..., :d // 2], t[..., d // 2:])
            rot = jnp.concatenate([-t2, t1], axis=-1)
            return t * cos + rot * sin
        b, n, _ = x.shape
        q = jax.nn.silu(x @ Wq)
        k = jax.nn.silu(x @ Wk)
        v = x @ Wv
        split = lambda t: t.reshape(b, n, HEADS, HD).transpose(0, 2, 1, 3)
        q, k, v = (split(q), split(k), split(v))
        q = _rope(q)
        k = _rope(k)
        energy = jnp.einsum('bhnd,bhmd->bhnm', q, k)
        mask = jnp.tril(jnp.ones((n, n), dtype=energy.dtype))
        energy = energy * mask
        out = jnp.einsum('bhnm,bhmd->bhnd', energy, v)
        out = out.transpose(0, 2, 1, 3).reshape(b, n, EMBED)
        gate = jax.nn.sigmoid(x @ Wg1 @ Wg2)
        out = out * gate
        mu = out.mean(axis=-1, keepdims=True)
        var = ((out - mu) ** 2).mean(axis=-1, keepdims=True)
        out = (out - mu) / jnp.sqrt(var + EPS) * ln_w + ln_b
        return out @ Wo

    def _L0_ffn_ref(x, attn_mask, Wg, Wq, bq, Wkv, bkv, Wo, bo, ln_g, ln_b):
        import jax, jax.numpy as jnp
        import numpy as np
        S, B, D, H, DH = (512, 8, 128, 16, 64)

        def _forward(x, Wg, Wq, bq, Wkv, bkv, Wo, bo, ln_g, ln_b):
            s_len, bsz, d_model = x.shape
            n_head, _, d_head = Wq.shape
            cap = s_len // n_head
            scale = 1.0 / d_head ** 0.5
            h = jnp.transpose(x, (1, 0, 2))
            t = h
            probs = jax.nn.softmax(h @ Wg, axis=-1)
            scores = jnp.transpose(probs, (0, 2, 1))
            _, idx = jax.lax.top_k(scores, cap)
            idx = jnp.sort(idx, axis=-1)
            hg = jnp.take_along_axis(h[:, None, :, :], idx[..., None], axis=2)
            hg = jnp.transpose(hg, (1, 0, 2, 3))
            q = jnp.einsum('hbcd,hde->hbce', hg, Wq) + bq[:, None, None, :]
            kv = jnp.einsum('hbcd,hde->hbce', hg, Wkv) + bkv[:, None, None, :]
            k, v = jnp.split(kv, 2, axis=-1)
            att = jnp.einsum('hbid,hbjd->hbij', q, k) * scale
            p = jax.nn.softmax(att, axis=1)
            av = jnp.einsum('hbij,hbjd->hbid', p, v)
            ao = jnp.einsum('hbid,hde->hbie', av, Wo) + bo
            tok = jnp.transpose(idx, (1, 0, 2))
            b_ids = jnp.arange(bsz)[None, :, None]
            outs = jnp.zeros_like(t).at[b_ids, tok].add(ao)
            y = t + outs
            mu = jnp.mean(y, axis=-1, keepdims=True)
            var = jnp.var(y, axis=-1, keepdims=True)
            yn = (y - mu) * jax.lax.rsqrt(var + 1e-05) * ln_g + ln_b
            return jnp.transpose(yn, (1, 0, 2))
        return _forward(x, Wg, Wq, bq, Wkv, bkv, Wo, bo, ln_g, ln_b)

    def _L1_xattn_ref(tgt, memory, qkv_w, qkv_b, sa_out_w, sa_out_b, in_proj_w, in_proj_b, mha_out_w, mha_out_b, lin1_w, lin1_b, lin2_w, lin2_b, ln1_g, ln1_b, ln2_g, ln2_b, ln3_g, ln3_b):
        import jax, jax.numpy as jnp
        import numpy as np
        B, NT, NM, C, H, FF = (8, 128, 256, 128, 8, 512)

        def _ln(x, g, b):
            m = x.mean(-1, keepdims=True)
            v = jnp.mean((x - m) ** 2, axis=-1, keepdims=True)
            return (x - m) / jnp.sqrt(v + 1e-05) * g + b
        Bx, N, Cx = tgt.shape
        qkv = tgt @ qkv_w.T + qkv_b
        q, k, v = jnp.split(qkv, 3, axis=-1)
        scores = jnp.einsum('bnc,bmc->bnm', q, k) * jnp.sqrt(jnp.float32(Cx))
        diag = jnp.eye(N, dtype=bool)
        scores = jnp.where(diag[None, :, :], scores, -jnp.inf)
        attn = jax.nn.softmax(scores, axis=-1)
        sa = jnp.einsum('bnm,bmc->bnc', attn, v) @ sa_out_w.T + sa_out_b
        x = _ln(tgt + sa, ln1_g, ln1_b)
        d = Cx // H
        wq, wk, wv = jnp.split(in_proj_w, 3, axis=0)
        bq, bk, bv = jnp.split(in_proj_b, 3, axis=0)
        qh = (x @ wq.T + bq).reshape(Bx, N, H, d).transpose(0, 2, 1, 3)
        kh = (memory @ wk.T + bk).reshape(Bx, -1, H, d).transpose(0, 2, 1, 3)
        vh = (memory @ wv.T + bv).reshape(Bx, -1, H, d).transpose(0, 2, 1, 3)
        a = jax.nn.softmax(jnp.einsum('bhnd,bhmd->bhnm', qh, kh) / jnp.sqrt(jnp.float32(d)), axis=-1)
        ca = jnp.einsum('bhnm,bhmd->bhnd', a, vh).transpose(0, 2, 1, 3).reshape(Bx, N, Cx)
        ca = ca @ mha_out_w.T + mha_out_b
        x = _ln(x + ca, ln2_g, ln2_b)
        ff = jax.nn.relu(x @ lin1_w.T + lin1_b) @ lin2_w.T + lin2_b
        return _ln(x + ff, ln3_g, ln3_b)

    def _L1_attn_ref(x, rms_w, in_W, in_b, conv_w, conv_b, A_log, dbc_W, dbc_b, dup_W, dup_b, out_W, out_b):
        import jax, jax.numpy as jnp
        import numpy as np
        DM, EXP, N, K, FRAC = (128, 2, 16, 4, 16)
        D = DM * EXP
        DTR = D // FRAC
        EPS = 1e-06

        def _mamba_block(x, rms_w, in_W, in_b, conv_w, conv_b, A_log, dbc_W, dbc_b, dup_W, dup_b, out_W, out_b):
            residual = x
            h = x * jax.lax.rsqrt(jnp.mean(x * x, axis=-1, keepdims=True) + EPS) * rms_w
            proj = h @ in_W + in_b
            x1, g = (proj[..., :D], proj[..., D:])
            xt = jnp.transpose(x1, (0, 2, 1))
            xc = jax.lax.conv_general_dilated(xt, conv_w[:, None, :], window_strides=(1,), padding=[(K - 1, 0)], feature_group_count=D, dimension_numbers=('NCH', 'OIH', 'NCH'))
            xc = xc + conv_b[:, None]
            x1 = jax.nn.silu(jnp.transpose(xc, (0, 2, 1)))
            A = -jnp.exp(A_log)
            dbc = x1 @ dbc_W + dbc_b
            delta, Bm, Cm = (dbc[..., :DTR], dbc[..., DTR:DTR + N], dbc[..., DTR + N:])
            delta = jax.nn.softplus(delta @ dup_W + dup_b)
            A_disc = jnp.exp(delta[..., None] * A)
            B_x = delta[..., None] * Bm[:, :, None, :] * x1[..., None]
            Ad_t = jnp.transpose(A_disc, (1, 0, 2, 3))
            Bx_t = jnp.transpose(B_x, (1, 0, 2, 3))

            def step(hc, inp):
                a, b = inp
                hc = a * hc + b
                return (hc, hc)
            h0 = jnp.zeros((x.shape[0], D, N), x1.dtype)
            _, hs = jax.lax.scan(step, h0, (Ad_t, Bx_t))
            y = jnp.einsum('tbdn,btn->btd', hs, Cm)
            y = jax.nn.silu(g) * y
            out = y @ out_W + out_b
            return out + residual
        return _mamba_block(x, rms_w, in_W, in_b, conv_w, conv_b, A_log, dbc_W, dbc_b, dup_W, dup_b, out_W, out_b)

    def _L1_ffn_ref(x, W_exp, b_exp, up_weights, up_bias, down_weights, W_con, b_con, down_bias):
        import jax, jax.numpy as jnp
        import numpy as np
        D_MODEL = 128
        EXPANSION = 4
        D_HIDDEN = D_MODEL * EXPANSION
        NUM_STAGES = int(np.log2(D_HIDDEN))

        def butterfly(y, weights, dim):
            lead = y.shape[:-1]
            for stage in range(weights.shape[0]):
                s = 2 ** stage
                nb = dim // (2 * s)
                yr = y.reshape(*lead, nb, 2, s)
                a = yr[..., 0, :]
                b = yr[..., 1, :]
                w = weights[stage].reshape(nb, s, 2, 2)
                na = w[..., 0, 0] * a + w[..., 0, 1] * b
                nb2 = w[..., 1, 0] * a + w[..., 1, 1] * b
                y = jnp.stack([na, nb2], axis=-2).reshape(*lead, dim)
            return y
        h = jnp.einsum('bsd,dh->bsh', x, W_exp) + b_exp
        h = butterfly(h, up_weights, D_HIDDEN)
        h = jax.nn.gelu(h + up_bias, approximate=False)
        h = butterfly(h, down_weights, D_HIDDEN)
        y = jnp.einsum('bsh,hd->bsd', h, W_con) + b_con
        return y + down_bias
    x = x + _L0_xattn_ref(_layernorm(x, axis=-1), ctx_1024, L0_xattn_W, L0_xattn_b)
    x = x + _L0_attn_ref(_layernorm(x, axis=-1), L0_attn_Wq, L0_attn_Wk, L0_attn_Wv, L0_attn_Wo, L0_attn_Wg1, L0_attn_Wg2, L0_attn_ln_w, L0_attn_ln_b)
    x = x + _L0_ffn_ref(_layernorm(x, axis=-1), L0_ffn_attn_mask, L0_ffn_Wg, L0_ffn_Wq, L0_ffn_bq, L0_ffn_Wkv, L0_ffn_bkv, L0_ffn_Wo, L0_ffn_bo, L0_ffn_ln_g, L0_ffn_ln_b)
    x = x + _L1_xattn_ref(_layernorm(x, axis=-1), ctx_1024, L1_xattn_qkv_w, L1_xattn_qkv_b, L1_xattn_sa_out_w, L1_xattn_sa_out_b, L1_xattn_in_proj_w, L1_xattn_in_proj_b, L1_xattn_mha_out_w, L1_xattn_mha_out_b, L1_xattn_lin1_w, L1_xattn_lin1_b, L1_xattn_lin2_w, L1_xattn_lin2_b, L1_xattn_ln1_g, L1_xattn_ln1_b, L1_xattn_ln2_g, L1_xattn_ln2_b, L1_xattn_ln3_g, L1_xattn_ln3_b)
    x = x + _L1_attn_ref(_layernorm(x, axis=-1), L1_attn_rms_w, L1_attn_in_W, L1_attn_in_b, L1_attn_conv_w, L1_attn_conv_b, L1_attn_A_log, L1_attn_dbc_W, L1_attn_dbc_b, L1_attn_dup_W, L1_attn_dup_b, L1_attn_out_W, L1_attn_out_b)
    x = x + _L1_ffn_ref(_layernorm(x, axis=-1), L1_ffn_W_exp, L1_ffn_b_exp, L1_ffn_up_weights, L1_ffn_up_bias, L1_ffn_down_weights, L1_ffn_W_con, L1_ffn_b_con, L1_ffn_down_bias)
    return x

_drawn_inputs = setup_inputs


def setup_inputs(seed=0):
    import zlib

    import numpy as np

    out = dict(_drawn_inputs(seed))
    spreads = {'L0_xattn_b': (0.0, 0.1),
     'L0_attn_ln_w': (1.0, 0.2),
     'L0_attn_ln_b': (0.0, 0.1),
     'L0_ffn_bq': (0.0, 0.1),
     'L0_ffn_bkv': (0.0, 0.1),
     'L0_ffn_bo': (0.0, 0.1),
     'L0_ffn_ln_g': (1.0, 0.2),
     'L0_ffn_ln_b': (0.0, 0.1),
     'L1_xattn_qkv_b': (0.0, 0.8),
     'L1_xattn_sa_out_b': (0.0, 0.317),
     'L1_xattn_in_proj_b': (0.0, 0.8),
     'L1_xattn_mha_out_b': (0.0, 0.913),
     'L1_xattn_lin1_b': (0.0, 0.8),
     'L1_xattn_lin2_b': (0.0, 0.305),
     'L1_xattn_ln1_g': (1.0, 0.2),
     'L1_xattn_ln1_b': (0.0, 0.3),
     'L1_xattn_ln2_g': (1.0, 0.2),
     'L1_xattn_ln2_b': (0.0, 0.319),
     'L1_xattn_ln3_g': (1.0, 0.2),
     'L1_xattn_ln3_b': (0.0, 0.307),
     'L1_attn_rms_w': (1.0, 0.2),
     'L1_ffn_b_exp': (0.0, 0.1),
     'L1_ffn_up_bias': (0.0, 0.1),
     'L1_ffn_b_con': (0.0, 0.408),
     'L1_ffn_down_bias': (0.0, 0.454)}
    factors = {'L1_xattn_qkv_w': 4.185,
     'L1_xattn_sa_out_w': 3.747,
     'L1_xattn_in_proj_w': 8.0,
     'L1_xattn_mha_out_w': 6.77,
     'L1_xattn_lin1_w': 3.475,
     'L1_xattn_lin2_w': 2.789,
     'L1_attn_in_b': 2.859,
     'L1_attn_A_log': 2.891,
     'L1_attn_dup_b': 2.98,
     'L1_attn_out_b': 3.869}
    for name, (base, spread) in spreads.items():
        noise = np.random.default_rng([zlib.crc32(name.encode()), seed]).standard_normal(out[name].shape)
        drawn = base * np.exp(spread * noise) if base else spread * noise
        out[name] = jnp.asarray(drawn.astype(out[name].dtype))
    for name, factor in factors.items():
        out[name] = (out[name] * factor).astype(out[name].dtype)
    return out
```

```python
from contextlib import ExitStack

import numpy as np
import concourse.bass as bass
from concourse import mybir

T = 64
D = 128
M = 6272
TILES = M // D
CHUNK = 4
CHUNKS = -(-TILES // CHUNK)
HALF0 = 25
HALF1 = TILES - HALF0
H0, HD0 = 16, 8
H1, HD1 = 8, 16
PAIRS = H1 // 2
N = 16
DI = 256
FF = 512
FB = FF // D
IN_BLOCK = 7
STAGES = 9
EPS = 1e-5
RMS_EPS = 1e-6

FIRST = [("W0", D), ("ident", D), ("b0", 1), ("swap", D), ("pair_sum", D), ("stack", T), ("W0T", D)]
KV = [("WkT", D), ("WvT", D), ("bk", 1)]
MATS = [("Wq", D), ("Wk", D), ("Wv", D), ("Wg1", HD0), ("Wo", D), ("rotT", D), ("cosT", T), ("sinT", T),
        ("head", H0), ("causal", T), ("ln_w", 1), ("ln_b", 1),
        ("saWvT", D), ("sa_bv", 1), ("sa_outT", D), ("ln1_g", 1), ("ln1_b", 1), ("WqT", D), ("bq", 1), ("head1", H1),
        ("bv", 1), ("sumsel", 32), ("mha_outT", D), ("ln2_g", 1), ("ln2_b", 1)]
LATE = [("lin1T", FF), ("lin1_b", FB), ("lin2T", FB * D), ("rms_w", 1), ("in_W", 2 * DI), ("in_b", 4),
        ("conv_w", 8), ("conv_b", 2), ("A_log", 2 * N), ("dbc_W", 2 * 48), ("dup_b", 2), ("out_W", 2 * D),
        ("up_bias", FB)]
BFLY = [("perm", IN_BLOCK * D), ("coef_up", STAGES * FB * 2), ("coef_dn", STAGES * FB * 2),
        ("expT", FB * (D + 1)), ("con", FB * D)]
PACKS = {"first": FIRST, "kv": KV, "mats": MATS, "late": LATE, "bfly": BFLY}
ROWS = ["b0", "sa_out_b", "mha_out_b", "lin2_b", "out_b", "b_con", "down_bias"]
WIDE = ["ffn_g", "ffn_b", "ln1_g", "ln1_b", "ln2_g", "ln2_b", "ln3_g", "ln3_b"]
SMALL = [("Wg2", D), ("dup_W", 2 * D), ("dt_b", 1), ("bc_b", 1), ("own", N), ("onesB", D), ("onesC", D)]


def offsets(entries):
    at, out = 0, {}
    for name, width in entries:
        out[name] = (at, at + width)
        at += width
    return out, at


def build(nc, x_in, ctxT_in, ctxN_in, first_in, kv_in, mats_in, late_in, bfly_in, rows_in, wide_in, small_in, out):
    f32 = mybir.dt.float32
    ACT = mybir.ActivationFunctionType
    ALU = mybir.AluOpType
    X = mybir.AxisListType.X
    ctx = ExitStack()
    with ctx:
        sems = {}

        def sem(name):
            if name not in sems:
                sems[name] = ctx.enter_context(nc.semaphore(name))
            return sems[name]

        def sb(name, *shape):
            return ctx.enter_context(nc.sbuf_tensor(name, list(shape), f32))

        pack, place = {}, {}
        for name, entries in PACKS.items():
            place[name], width = offsets(entries)
            pack[name] = sb("p_" + name, D, width)
        small_at, small_w = offsets(SMALL)
        small = sb("p_small", 32, small_w)

        def of(p, name, lo=0, hi=None):
            a, b = place[p][name]
            return pack[p][:, a + lo:(a + hi if hi is not None else b)]

        def sm(name, rows):
            a, b = small_at[name]
            return small[0:rows, a:b]

        rows = sb("rows", 1, len(ROWS) * D)

        def row(name):
            i = ROWS.index(name)
            return rows[0:1, i * D:(i + 1) * D]

        wide = sb("wide", T, len(WIDE) * D)

        def wd(name):
            i = WIDE.index(name)
            return wide[:, i * D:(i + 1) * D]

        ident = of("first", "ident")
        ctxT = sb("ctxT", D, M)
        KT = sb("KT", D, M)
        V = sb("V", D, TILES, D)
        scoresA = sb("scoresA", D, M)
        big = sb("big", D, M)
        ctxN = big[:, :].rearrange("p (t c) -> p t c", c=D)
        scores = [scoresA, big]
        pT = sb("pT", D, 4, CHUNK * D)
        EARLY = 4
        m_up = sb("m_up", D, EARLY, FB, D)
        late_mats = ctxT[:, 0:(2 * IN_BLOCK - EARLY) * FB * D].rearrange("p (k b c) -> p k b c", b=FB, c=D)
        mats = {"up": [m_up[:, k] for k in range(EARLY)] + [late_mats[:, k] for k in range(IN_BLOCK - EARLY)],
                "dn": [late_mats[:, IN_BLOCK - EARLY + k] for k in range(IN_BLOCK)]}

        x = sb("x", T, D)
        half_power = sb("half_power", T, 1)
        ones = sb("ones", 1, T)
        LN = 12
        stats, mv = sb("stats", T, 6 * LN), sb("mv", T, 2 * LN)
        var_eps, rstd = sb("var_eps", T, LN), sb("rstd", T, LN)
        norm = sb("norm", T, LN * D)

        def nm(i):
            return norm[:, i * D:(i + 1) * D]

        x1, x2, x3, x4, x5, x6 = (sb(f"x{i}", T, D) for i in range(1, 7))
        used = [0]

        def after(_name, parts, *shape):
            n = int(np.prod(shape))
            flat = V[0:parts].rearrange("p t c -> p (t c)")[:, used[0]:used[0] + n]
            used[0] += n
            assert used[0] <= M
            if len(shape) == 1:
                return flat
            names = "abc"[:len(shape)]
            return flat.rearrange(f"p ({' '.join(names)}) -> p {' '.join(names)}", **dict(zip(names, shape)))

        xnT = sb("xnT", D, 2, T)
        qWT, cp = sb("qWT", D, T), sb("cp", D, 1)
        cmax, lsum = sb("cmax", D, 8), sb("lsum", D, 8)
        nmax0, nmaxM, w0, l0, wl, rL, fac = (sb(n, D, 1) for n in ("nmax0", "nmaxM", "w0", "l0", "wl", "rL", "fac"))
        o_sc, attT = sb("o_sc", D, D), sb("attT", D, T)
        xn1T = sb("xn1T", D, 2, T)
        tanh_qk, s2, s2cos, s2sin, qk = (sb(n, D, 2, T) for n in ("tanh_qk", "s2", "s2cos", "s2sin", "qk"))
        q_heads = big[:, 0:H0 * T].rearrange("p (h n) -> p h n", h=H0)
        energy = big[:, 2048:2048 + H0 // 2 * T].rearrange("p (h n) -> p h n", h=H0 // 2)
        g1T, tanh_gate = sb("g1T", HD0, T), sb("tanh_gate", T, D)
        v_halves = sb("v_halves", D, 2, T)
        gated, yT = sb("gated", T, D), sb("yT", D, T)
        x2b, zg, tgtT, vT, t1, z6T = sb("x2b", T, D), sb("zg", T, D), sb("tgtT", D, T), sb("vT", D, T), sb("t1", T, D), sb("z6T", D, T)
        xg, x_q, q_all = sb("xg", T, D), sb("x_q", T, D), sb("q_all", D, T)
        q_wide = sb("q_wide", D, H1, T)
        max1, sum1 = sb("max1", D, PAIRS, 16), sb("sum1", D, PAIRS, 16)
        nmax1, l1, rl1 = sb("nmax1", D, PAIRS), sb("l1", D, PAIRS), sb("rl1", D, PAIRS)
        oS, ca, caT = sb("oS", D, 2, D), sb("ca", T, D), sb("caT", D, T)
        t2, z7T, x7g, x7, hT, t3, z8g, x3b = after("t2", T, D), after("z7T", D, T), after("x7g", T, D), after("x7", T, D), after("hT", D, FB, T), after("t3", T, D), after("z8g", T, D), sb("x3b", T, D)
        sq, msum, rms_h, hmT = after("sq", T, D), after("msum", T, 1), after("rms_h", T, D), after("hmT", D, T)
        pad = sb("pad", D, 2, T + 3)
        xc, tanh_xc, xs2 = after("xc", D, 2, T), after("tanh_xc", D, 2, T), after("xs2", D, 2, T)
        gT, tanh_g, gs2 = after("gT", D, 2, T), after("tanh_g", D, 2, T), after("gs2", D, 2, T)
        dtT, bcT = after("dtT", N, T), after("bcT", 2 * N, T)
        bc_own = big[0:2 * N, 0:N * T].rearrange("p (n t) -> p n t", n=N)
        z, zneg, ez, lz, zpos, delta, dx = (after(n, D, 2, T) for n in ("z", "zneg", "ez", "lz", "zpos", "delta", "dx"))
        expA = sb("expA", D, 2, N)
        dA, Bx, hs = (KT[:, i * 2 * N * T:(i + 1) * 2 * N * T].rearrange("p (b n t) -> p b n t", b=2, n=N) for i in range(3))
        decay = scoresA[:, 0:2 * N * T].rearrange("p (b n t) -> p b n t", b=2, n=N)
        hC = scoresA[:, 2 * N * T:4 * N * T].rearrange("p (b n t) -> p b n t", b=2, n=N)
        y, yg, xr = after("y", D, 2, T), after("yg", D, 2, T), after("xr", T, D)
        x6T, h6T, gl6 = after("x6T", D, T), after("h6T", D, FB, T), after("gl6", D, FB, T)
        up = [of("bfly", "expT").rearrange("p (b c) -> p b c", b=FB), after("upA", D, FB, D + 1), after("upB", D, FB, D + 1)]
        dn = [of("bfly", "con").rearrange("p (b c) -> p b c", b=FB), *(ctxT[:, 5120 + 512 * i:5632 + 512 * i].rearrange("p (b c) -> p b c", b=FB) for i in range(2))]
        bt = [sb("btA", D, FB, D + 1), sb("btB", D, FB, D + 1)]
        wup, beff = after("wup", D, FB, D), after("beff", D, FB)

        PS = ctx.enter_context(nc.psum_tensor("PS", [D, 8, 512], f32))
        S_BANKS, T_BANKS, O_BANKS, F_BANKS = (0, 1), (2, 3), (4, 7), (5, 6)

        up_c = of("bfly", "coef_up").rearrange("p (k b j) -> p k b j", k=STAGES, b=FB)
        dn_c = of("bfly", "coef_dn").rearrange("p (k b j) -> p k b j", k=STAGES, b=FB)
        perm = of("bfly", "perm").rearrange("p (k c) -> p k c", k=IN_BLOCK)

        def width(c):
            return min(CHUNK, TILES - CHUNK * c) * D

        FILL = [("k", c) for c in range(CHUNKS)] + [("v", c) for c in range(CHUNKS)]
        BSTEPS = [s for i in range(IN_BLOCK) for s in (("up", i), ("dn", i))]

        def ctxT_pieces(j):
            a = HALF0 * D
            return (1024 * j, min(1024 * j + 1024, a)), (a + 1024 * j, min(a + 1024 * j + 1024, M))

        block = ctx.enter_context(nc.Block())

        @block.sync
        def _(sp):
            sp.dma_start(x[:], x_in).then_inc(sem("x_in"), 16)
            sp.dma_start(pack["first"][:], first_in).then_inc(sem("first_in"), 16)
            for j in range(4):
                for lo, hi in ctxT_pieces(j):
                    if lo < hi:
                        sp.dma_start(ctxT[:, lo:hi], ctxT_in[:, lo:hi]).then_inc(sem(f"ctxT_in{j}"), 16)
                if j == 0:
                    sp.dma_start(pack["kv"][:], kv_in).then_inc(sem("kv_in"), 16)
            for j in range(5):
                for lo, hi in ((5 * j, 5 * j + 5), (HALF0 + 5 * j, min(HALF0 + 5 * j + 5, TILES))):
                    sp.dma_start(ctxN[:, lo:hi, :], ctxN_in[:, lo:hi, :]).then_inc(sem(f"ctxN_in{j}"), 16)
                if j == 0:
                    sp.dma_start(rows[:], rows_in).then_inc(sem("rows_in"), 16)
                    sp.dma_start(pack["bfly"][:], bfly_in).then_inc(sem("bfly_in"), 16)
            sp.dma_start(pack["mats"][:], mats_in).then_inc(sem("mats_in"), 16)
            sp.dma_start(wide[:], wide_in).then_inc(sem("wide_in"), 16)
            sp.dma_start(small[:], small_in).then_inc(sem("small_in"), 16)
            sp.dma_start(pack["late"][:], late_in).then_inc(sem("late_in"), 16)
            sp.wait_ge(sem("x6"), 1)
            sp.dma_start(out, x6[:]).then_inc(sem("stored"), 16)
            sp.wait_ge(sem("stored"), 16)

        @block.gpsimd
        def _(pool):
            def rsqrt(i):
                pool.wait_ge(sem("var_ready"), i + 1)
                pool.tensor_tensor(rstd[:, i:i + 1], var_eps[:, i:i + 1], half_power[:], ALU.pow).then_inc(sem("rstd_ready"), 1)

            steps = [0]

            def link(ins):
                steps[0] += 1
                ins.then_inc(sem("pool_step"), 1)
                pool.wait_ge(sem("pool_step"), steps[0])

            tmp = [0]

            def build_matrices(which, k):
                coef = up_c if which == "up" else dn_c
                m = mats[which][k]
                link(pool.tensor_tensor(m, ident.unsqueeze(1).to_broadcast([D, FB, D]),
                                        coef[:, k, :, 0:1].to_broadcast([D, FB, D]), ALU.mult))
                t = bt[tmp[0] % 2][:, :, 0:D]
                tmp[0] += 1
                link(pool.tensor_tensor(t, perm[:, k:k + 1, :].to_broadcast([D, FB, D]),
                                        coef[:, k, :, 1:2].to_broadcast([D, FB, D]), ALU.mult))
                steps[0] += 1
                pool.tensor_tensor(m, m, t, ALU.add).then_inc(sem("pool_step"), 1)
                pool.wait_ge(sem("pool_step"), steps[0])
                pool.sem_inc(sem(f"mats_{which}"), 1)

            def across_blocks(which, k, src, dst, width):
                coef = up_c if which == "up" else dn_c
                p = 1 if k == 7 else 2
                t = bt[tmp[0] % 2][:, :, 0:width]
                tmp[0] += 1
                halves = [slice(0, 4, 2), slice(1, 4, 2)] if p == 1 else [slice(0, 2), slice(2, 4)]
                for a, b in (halves, halves[::-1]):
                    link(pool.tensor_tensor(t[:, a, :], src[:, b, :], coef[:, k, a, 1:2].to_broadcast([D, 2, width]), ALU.mult))
                link(pool.tensor_tensor(dst, src, coef[:, k, :, 0:1].to_broadcast([D, FB, width]), ALU.mult))
                link(pool.tensor_tensor(dst, dst, t, ALU.add))

            pool.memset(half_power[:], -0.5).then_inc(sem("pool_const"), 1)
            pool.memset(ones[:], 1.0).then_inc(sem("ones_ready"), 1)
            pool.wait_ge(sem("pool_const"), 1)
            rsqrt(0)
            pool.wait_ge(sem("first_in"), 16)
            pool.wait_ge(sem("bfly_in"), 16)
            for k in range(EARLY):
                build_matrices("up", k)
            rsqrt(1)
            rsqrt(2)
            rsqrt(3)
            pool.wait_ge(sem("wide_in"), 16)
            pool.wait_ge(sem("x2"), 1)
            pool.tensor_tensor(x2b[:], x2[:], wd("ffn_b"), ALU.add).then_inc(sem("x2b"), 1)
            rsqrt(4)
            rsqrt(5)
            rsqrt(6)
            pool.wait_ge(sem("normed"), 7)
            link(pool.tensor_tensor(xg[:], nm(6), wd("ln1_g"), ALU.mult))
            pool.tensor_tensor(x_q[:], xg[:], wd("ln1_b"), ALU.add).then_inc(sem("x_q"), 1)
            pool.tensor_tensor(x3b[:], x3[:], wd("ln3_b"), ALU.add).then_inc(sem("x3b"), 1)
            pool.wait_ge(sem("fill_out"), len(FILL))
            for k in range(EARLY, IN_BLOCK):
                build_matrices("up", k)
            across_blocks("dn", 8, dn[0], dn[1][:, :, :], D)
            across_blocks("dn", 7, dn[1], dn[2][:, :, :], D)
            pool.sem_inc(sem("dn_start"), 1)
            for k in reversed(range(IN_BLOCK)):
                build_matrices("dn", k)
            rsqrt(7)
            pool.wait_ge(sem("normed"), 8)
            link(pool.tensor_tensor(x7g[:], nm(7), wd("ln2_g"), ALU.mult))
            pool.tensor_tensor(x7[:], x7g[:], wd("ln2_b"), ALU.add).then_inc(sem("x7"), 1)
            rsqrt(8)
            rsqrt(9)
            pool.wait_ge(sem("normed"), 10)
            pool.tensor_tensor(xr[:], nm(9), x4[:], ALU.add).then_inc(sem("xr"), 1)
            rsqrt(10)
            pool.wait_ge(sem("up_evac"), IN_BLOCK)
            last = up[1 + (IN_BLOCK - 1) % 2]
            other = up[1 + IN_BLOCK % 2]
            across_blocks("up", 7, last, other[:, :, :], D + 1)
            across_blocks("up", 8, other, last[:, :, :], D + 1)
            pool.wait_ge(sem("late_in"), 16)
            pool.tensor_tensor(beff[:].unsqueeze(2), last[:, :, D:D + 1], of("late", "up_bias").unsqueeze(2), ALU.add).then_inc(sem("up_done"), 1)
            rsqrt(11)

        @block.scalar
        def _(act):
            A = act.activation
            fills = iter(range(len(FILL)))

            def fill(n=1):
                for _ in range(n):
                    i = next(fills)
                    kind, c = FILL[i]
                    bank = PS[:, F_BANKS[i % 2], 0:width(c)]
                    act.wait_ge(sem("fill"), i + 1)
                    if kind == "k":
                        A(KT[:, c * 512:c * 512 + width(c)], bank, ACT.Identity, bias=of("kv", "bk")).then_inc(sem("fill_out"), 1)
                    else:
                        A(V[:, c * CHUNK:c * CHUNK + width(c) // D, :], bank.rearrange("p (t c) -> p t c", c=D), ACT.Copy).then_inc(sem("fill_out"), 1)

            bsteps = iter(range(len(BSTEPS)))

            def bfly(n=1):
                for _ in range(n):
                    i = next(bsteps)
                    which, k = BSTEPS[i]
                    act.wait_ge(sem(f"{which}_step"), k + 1)
                    if which == "up":
                        A(up[1 + k % 2][:, :, :].rearrange("p (a b) c -> p a (b c)", a=2), PS[:, 5:7, 0:2 * (D + 1)], ACT.Copy).then_inc(sem("up_evac"), 1)
                    else:
                        A(dn[1 + k % 2][:, :, :], PS[:, 7, :].rearrange("p (b c) -> p b c", b=FB), ACT.Copy).then_inc(sem("dn_evac"), 1)

            act.wait_ge(sem("kv_in"), 16)
            act.wait_ge(sem("nmax0"), 1)
            for j in range(7):
                P, w = (D, 512) if j < 6 else (T, D)
                s = scoresA[0:P, 512 * j:512 * j + w]
                A(s, s, ACT.Exp, bias=nmax0[0:P], accum_out=lsum[0:P, j:j + 1]).then_inc(sem("exp0"), 1)
                fill(1)
            act.wait_ge(sem("nmaxM"), 1)
            A(w0[:], nmax0[:], ACT.Exp, scale=-1.0, bias=nmaxM[:]).then_inc(sem("w0"), 1)
            fill(2)
            act.wait_ge(sem("qkT"), 1)
            A(tanh_qk[:], PS[:, 0, 0:2 * T].rearrange("p (a n) -> p a n", a=2), ACT.Tanh, scale=0.5).then_inc(sem("tanh_qk"), 1)
            act.wait_ge(sem("g1"), 1)
            A(g1T[:], PS[0:HD0, 1, 0:T], ACT.Copy).then_inc(sem("g1T"), 1)
            act.wait_ge(sem("v0"), 1)
            act.wait_ge(sem("v_zero"), 1)
            for h in range(2):
                P = slice(T * h, T * h + T)
                A(v_halves[P, h, :], PS[P, 2, T * h:T * h + T], ACT.Copy).then_inc(sem("v_halves"), 1)
            act.wait_ge(sem("gate"), 1)
            A(tanh_gate[:], PS[0:T, 7, 256:256 + D], ACT.Tanh, scale=0.5).then_inc(sem("tanh_gate"), 1)
            fill(11)
            act.wait_ge(sem("v1"), 1)
            A(vT[:], PS[:, 1, 0:T], ACT.Identity, bias=of("mats", "sa_bv")).then_inc(sem("vT"), 1)
            fill(6)
            act.wait_ge(sem("late_in"), 16)
            A(expA[:].rearrange("p b n -> p (b n)"), of("late", "A_log"), ACT.Exp).then_inc(sem("expA"), 1)

            def turned(g, c):
                n = g * CHUNKS + c
                act.wait_ge(sem("turned"), n + 1)
                if n >= 4:
                    act.wait_ge(sem("pv"), n - 3)
                A(pT[:, n % 4, 0:width(c)], PS[:, T_BANKS[n % 2], 0:width(c)], ACT.Copy).then_inc(sem("pT_act"), 1)

            for g in range(PAIRS):
                act.wait_ge(sem("nmax1"), g + 1)
                for c in range(CHUNKS + 2):
                    if c < CHUNKS:
                        s = scores[g % 2][:, 512 * c:512 * c + width(c)]
                        A(s, s, ACT.Exp, bias=nmax1[:, g:g + 1], accum_out=sum1[:, g, c:c + 1]).then_inc(sem("exp1"), 1)
                    if c >= 2 and (c - 2) % 2 == 1:
                        turned(g, c - 2)

            act.wait_ge(sem("lin1_b"), 1)
            for b in (2, 3):
                A(hT[:, b, :], PS[:, 1, T * (b - 2):T * (b - 1)], ACT.Relu, bias=of("late", "lin1_b", b, b + 1)).then_inc(sem("h_act"), 1)
            bfly(4)
            act.wait_ge(sem("gate1"), 1)
            for b in range(2):
                A(gT[:, b, :], PS[:, 1, T * b:T * b + T], ACT.Identity, bias=of("late", "in_b", 2 + b, 3 + b)).then_inc(sem("gT"), 1)
            act.wait_ge(sem("gT"), 2)
            A(tanh_g[:], gT[:], ACT.Tanh, scale=0.5).then_inc(sem("tanh_g"), 1)
            act.wait_ge(sem("xc"), 1)
            A(tanh_xc[:], xc[:], ACT.Tanh, scale=0.5).then_inc(sem("tanh_xc"), 1)
            bfly(1)
            act.wait_ge(sem("dt_low"), 1)
            A(dtT[:], PS[0:N, 2, 0:T], ACT.Identity, scale=0.5, bias=sm("dt_b", N)).then_inc(sem("dtT"), 1)
            bfly(1)
            act.wait_ge(sem("zneg"), 1)
            A(ez[:], zneg[:], ACT.Exp).then_inc(sem("ez"), 1)
            act.wait_ge(sem("ez"), 1)
            A(lz[:], ez[:], ACT.Ln, bias=1.0).then_inc(sem("lz"), 1)
            bfly(2)
            for b in range(2):
                act.wait_ge(sem("dA"), b + 1)
                A(decay[:, b, :, 1:T], dA[:, b, :, 1:T], ACT.Exp, scale=-1.0).then_inc(sem("decay"), 1)
                bfly(3)
            act.wait_ge(sem("wup_turned"), 1)
            A(wup[:], PS[:, 5, :].rearrange("p (b c) -> p b c", b=FB), ACT.Copy).then_inc(sem("wup"), 1)
            act.wait_ge(sem("h6"), 1)
            for b in range(FB):
                A(gl6[:, b, :], PS[:, 0, T * b:T * b + T], ACT.Gelu, bias=beff[:, b:b + 1]).then_inc(sem("gelu"), 1)

        @block.vector
        def _(dve):
            steps = [0]

            def link(ins):
                steps[0] += 1
                ins.then_inc(sem("dve_step"), 1)
                dve.wait_ge(sem("dve_step"), steps[0])

            norms = [0]

            def layer_norm(src, eps=EPS):
                i = norms[0]
                norms[0] += 1
                link(dve.bn_stats(stats[:, 6 * i:6 * i + 6], src))
                link(dve.bn_aggr(mv[:, 2 * i:2 * i + 2], stats[:, 6 * i:6 * i + 6]))
                dve.tensor_scalar(var_eps[:, i:i + 1], mv[:, 2 * i + 1:2 * i + 2], eps, None, ALU.add).then_inc(sem("var_ready"), 1)
                dve.wait_ge(sem("rstd_ready"), i + 1)
                dve.tensor_scalar(nm(i), src, mv[:, 2 * i:2 * i + 1], rstd[:, i:i + 1], ALU.subtract, ALU.mult).then_inc(sem("normed"), 1)

            dve.memset(scoresA[T:D, 3072:3200], 0.0).then_inc(sem("scores_tail"), 1)
            dve.memset(cmax[T:D, 6:7], -3.0e38).then_inc(sem("cmax_tail"), 1)
            dve.memset(lsum[T:D, 6:7], 0.0).then_inc(sem("lsum_tail"), 1)
            dve.memset(v_halves[:], 0.0).then_inc(sem("v_zero"), 1)
            dve.memset(pad[:, :, 0:3], 0.0).then_inc(sem("pad_zero"), 1)

            dve.wait_ge(sem("x_in"), 16)
            layer_norm(x[:])
            dve.wait_ge(sem("norm_turned"), 1)
            dve.tensor_copy(xnT[:], PS[:, 7, 0:T].unsqueeze(1).to_broadcast([D, 2, T])).then_inc(sem("norm_columns"), 1)
            dve.wait_ge(sem("qW"), 1)
            dve.tensor_copy(qWT[:], PS[:, 7, 64:64 + T]).then_inc(sem("qWT"), 1)
            link(dve.tensor_copy(cp[:], PS[:, 7, 128:129]))
            for j in range(7):
                P, w = (D, 512) if j < 6 else (T, D)
                dve.wait_ge(sem("s0"), j + 1)
                dve.tensor_scalar(scoresA[0:P, 512 * j:512 * j + w], PS[0:P, S_BANKS[j % 2], 0:w], cp[0:P], None,
                                  ALU.add, ALU.max, accum_out=cmax[0:P, j:j + 1]).then_inc(sem("s0_out"), 1)
            dve.wait_ge(sem("s0_out"), 7)
            dve.wait_ge(sem("cmax_tail"), 1)
            dve.tensor_reduce(nmax0[:], cmax[:, 0:7], X, ALU.max, negate=True).then_inc(sem("nmax0"), 1)
            dve.wait_ge(sem("nmax_other"), 1)
            dve.tensor_tensor(nmaxM[:], PS[:, 7, 130:131], nmax0[:], ALU.min).then_inc(sem("nmaxM"), 1)
            for c in range(7):
                w = 512 if c < 6 else D
                dve.wait_ge(sem("turned0"), c + 1)
                if c >= 3:
                    dve.wait_ge(sem("pv0"), c - 2)
                dve.tensor_copy(pT[:, c % 3, 0:w], PS[:, T_BANKS[c % 2], 0:w]).then_inc(sem("pT0"), 1)
            dve.wait_ge(sem("exp0"), 7)
            dve.wait_ge(sem("lsum_tail"), 1)
            link(dve.reduce_sum(l0[:], lsum[:, 0:7], X))
            dve.wait_ge(sem("w0"), 1)
            dve.tensor_tensor(wl[:], w0[:], l0[:], ALU.mult).then_inc(sem("wl"), 1)
            dve.wait_ge(sem("l_both"), 1)
            link(dve.reciprocal(rL[:], PS[:, 7, 132:133]))
            link(dve.tensor_tensor(fac[:], w0[:], rL[:], ALU.mult))
            dve.wait_ge(sem("pv0"), 7)
            dve.tensor_scalar(o_sc[:], PS[:, 4, 0:D], fac[:], None, ALU.mult).then_inc(sem("o_sc"), 1)
            dve.wait_ge(sem("att"), 1)
            dve.tensor_copy(attT[:], PS[:, 7, 192:192 + T]).then_inc(sem("attT"), 1)
            dve.wait_ge(sem("xattn"), 1)
            link(dve.scalar_tensor_tensor(x1[:], PS[0:T, 3, 256:256 + D], 0.0, x[:], ALU.max, ALU.add))

            layer_norm(x1[:])
            dve.wait_ge(sem("norm_turned"), 2)
            dve.tensor_copy(xn1T[:], PS[:, 4, 0:T].unsqueeze(1).to_broadcast([D, 2, T])).then_inc(sem("norm_columns"), 1)
            dve.wait_ge(sem("tanh_qk"), 1)
            dve.scalar_tensor_tensor(s2[:], tanh_qk[:], 1.0, PS[:, 0, 0:2 * T].rearrange("p (a n) -> p a n", a=2), ALU.add, ALU.mult).then_inc(sem("s2"), 1)
            dve.wait_ge(sem("s2"), 1)
            link(dve.tensor_tensor(s2cos[:], s2[:], of("mats", "cosT").unsqueeze(1).to_broadcast([D, 2, T]), ALU.mult))
            dve.wait_ge(sem("rotated"), 1)
            link(dve.tensor_tensor(s2sin[:], PS[:, 3, 0:2 * T].rearrange("p (a n) -> p a n", a=2), of("mats", "sinT").unsqueeze(1).to_broadcast([D, 2, T]), ALU.mult))
            link(dve.tensor_tensor(qk[:], s2cos[:], s2sin[:], ALU.add))
            for h in range(2):
                dve.tensor_tensor(q_heads[:, 8 * h:8 * h + 8, :], qk[:, 0:1, :].to_broadcast([D, 8, T]),
                                  of("mats", "head", 8 * h, 8 * h + 8).unsqueeze(2).to_broadcast([D, 8, T]), ALU.mult).then_inc(sem("q_heads"), 1)
            dve.wait_ge(sem("energy"), 1)
            dve.tensor_tensor(energy[:, :, :], PS[:, 0, :].rearrange("p (h n) -> p h n", h=8),
                              of("mats", "causal").unsqueeze(1).to_broadcast([D, 8, T]), ALU.mult).then_inc(sem("masked"), 1)
            dve.wait_ge(sem("tanh_gate"), 1)
            dve.wait_ge(sem("lin_att"), 1)
            link(dve.scalar_tensor_tensor(gated[:], tanh_gate[:], 1.0, PS[0:T, 1, 128:128 + D], ALU.add, ALU.mult))
            layer_norm(gated[:])
            dve.wait_ge(sem("norm_turned"), 3)
            dve.tensor_scalar(yT[:], PS[:, 4, 64:64 + T], of("mats", "ln_w"), of("mats", "ln_b"), ALU.mult, ALU.add).then_inc(sem("norm_columns"), 1)
            dve.wait_ge(sem("attn_out"), 1)
            dve.tensor_tensor(x2[:], PS[0:T, 4, 128:128 + D], x1[:], ALU.add).then_inc(sem("x2"), 1)
            dve.wait_ge(sem("x2"), 1)

            layer_norm(x2[:])
            dve.wait_ge(sem("normed"), 4)
            layer_norm(nm(3))
            dve.wait_ge(sem("normed"), 5)
            link(dve.tensor_tensor(zg[:], nm(4), wd("ffn_g"), ALU.mult))
            dve.wait_ge(sem("x2b"), 1)
            link(dve.tensor_tensor(x3[:], zg[:], x2b[:], ALU.add))

            layer_norm(x3[:])
            dve.wait_ge(sem("norm_turned"), 4)
            dve.tensor_copy(tgtT[:], PS[:, 0, 0:T]).then_inc(sem("norm_columns"), 1)
            dve.wait_ge(sem("sa"), 1)
            link(dve.tensor_tensor(t1[:], PS[0:T, 2, 128:128 + D], nm(5), ALU.add))
            layer_norm(t1[:])
            dve.wait_ge(sem("norm_turned"), 5)
            dve.tensor_scalar(z6T[:], PS[:, 0, 64:64 + T], of("mats", "ln1_g"), of("mats", "ln1_b"), ALU.mult, ALU.add).then_inc(sem("norm_columns"), 1)
            dve.wait_ge(sem("q1"), 1)
            for p in range(2):
                dve.tensor_scalar(q_wide[:, p, :], PS[:, 4, 256:256 + T], of("mats", "bq"), of("mats", "head1", p, p + 1), ALU.add, ALU.mult).then_inc(sem("q_wide"), 1)
            link(dve.tensor_scalar(q_all[:], PS[:, 4, 256:256 + T], of("mats", "bq"), None, ALU.add))
            dve.tensor_tensor(q_wide[:, 2:H1, :], q_all[:].unsqueeze(1).to_broadcast([D, H1 - 2, T]),
                              of("mats", "head1", 2, H1).unsqueeze(2).to_broadcast([D, H1 - 2, T]), ALU.mult).then_inc(sem("q_wide"), 1)

            def turned(g, c):
                n = g * CHUNKS + c
                dve.wait_ge(sem("turned"), n + 1)
                if n >= 4:
                    dve.wait_ge(sem("pv"), n - 3)
                dve.tensor_copy(pT[:, n % 4, 0:width(c)], PS[:, T_BANKS[n % 2], 0:width(c)]).then_inc(sem("pT_dve"), 1)

            def finish(g):
                dve.wait_ge(sem("exp1"), (g + 1) * CHUNKS)
                link(dve.reduce_sum(l1[:, g:g + 1], sum1[:, g, 0:CHUNKS], X))
                link(dve.reciprocal(rl1[:, g:g + 1], l1[:, g:g + 1]))
                dve.wait_ge(sem("pv"), (g + 1) * CHUNKS)
                if g >= 2:
                    dve.wait_ge(sem("heads"), g - 1)
                dve.tensor_copy(oS[:, g % 2, :], PS[:, O_BANKS[g % 2], 0:D]).then_inc(sem("oS"), 1)
                dve.wait_ge(sem("heads"), g + 1)
                for p in range(2):
                    P = slice(T * p, T * p + T)
                    dve.tensor_scalar(ca[:, 32 * g + HD1 * p:32 * g + HD1 * p + HD1], PS[P, 5, HD1 * p:HD1 * p + HD1],
                                      rl1[P, g:g + 1], None, ALU.mult).then_inc(sem("ca"), 1)

            for g in range(PAIRS + 1):
                for c in range(CHUNKS + 1):
                    if g < PAIRS and c < CHUNKS:
                        n = g * CHUNKS + c
                        dve.wait_ge(sem("s1"), n + 1)
                        if g >= 2 and c == 0:
                            dve.wait_ge(sem("turned"), (g - 1) * CHUNKS)
                        dve.tensor_scalar(scores[g % 2][:, 512 * c:512 * c + width(c)], PS[:, S_BANKS[n % 2], 0:width(c)], 0.0, None,
                                          ALU.add, ALU.max, accum_out=max1[:, g, c:c + 1]).then_inc(sem("s1_out"), 1)
                    if g >= 1 and c % 2 == 1:
                        turned(g - 1, c - 1)
                if g < PAIRS:
                    dve.wait_ge(sem("s1_out"), (g + 1) * CHUNKS)
                    dve.tensor_reduce(nmax1[:, g:g + 1], max1[:, g, 0:CHUNKS], X, ALU.max, negate=True).then_inc(sem("nmax1"), 1)
                if g >= 1:
                    finish(g - 1)
            dve.wait_ge(sem("caT"), 1)
            dve.tensor_scalar(caT[:], PS[:, 0, 0:T], of("mats", "bv"), None, ALU.add).then_inc(sem("caT_out"), 1)
            dve.wait_ge(sem("mha"), 1)
            dve.wait_ge(sem("x_q"), 1)
            link(dve.tensor_tensor(t2[:], PS[0:T, 1, 256:256 + D], x_q[:], ALU.add))
            layer_norm(t2[:])
            dve.wait_ge(sem("norm_turned"), 6)
            dve.tensor_scalar(z7T[:], PS[:, 2, 0:T], of("mats", "ln2_g"), of("mats", "ln2_b"), ALU.mult, ALU.add).then_inc(sem("norm_columns"), 1)
            dve.wait_ge(sem("lin1_a"), 1)
            for b in (0, 1):
                dve.tensor_scalar(hT[:, b, :], PS[:, 0, T * b:T * b + T], of("late", "lin1_b", b, b + 1), 0.0, ALU.add, ALU.max).then_inc(sem("h_dve"), 1)
            dve.wait_ge(sem("ff"), 1)
            dve.wait_ge(sem("x7"), 1)
            link(dve.tensor_tensor(t3[:], PS[0:T, 2, 128:128 + D], x7[:], ALU.add))
            layer_norm(t3[:])
            dve.wait_ge(sem("normed"), 9)
            link(dve.tensor_tensor(z8g[:], nm(8), wd("ln3_g"), ALU.mult))
            dve.wait_ge(sem("x3b"), 1)
            link(dve.tensor_tensor(x4[:], z8g[:], x3b[:], ALU.add))

            layer_norm(x4[:])
            dve.wait_ge(sem("normed"), 10)
            link(dve.scalar_tensor_tensor(sq[:], nm(9), 1.0, nm(9), ALU.mult, ALU.mult, accum_out=msum[:]))
            dve.tensor_scalar(var_eps[:, 10:11], msum[:], 1.0 / D, RMS_EPS, ALU.mult, ALU.add).then_inc(sem("var_ready"), 1)
            norms[0] += 1
            dve.wait_ge(sem("rstd_ready"), 11)
            dve.tensor_scalar(rms_h[:], nm(9), rstd[:, 10:11], None, ALU.mult).then_inc(sem("rms_h"), 1)
            dve.wait_ge(sem("rmsT"), 1)
            dve.tensor_scalar(hmT[:], PS[:, 2, 256:256 + T], of("late", "rms_w"), None, ALU.mult).then_inc(sem("hmT"), 1)
            dve.wait_ge(sem("x_in1"), 1)
            dve.wait_ge(sem("pad_zero"), 1)
            for b in range(2):
                dve.tensor_scalar(pad[:, b, 3:3 + T], PS[:, 0, T * b:T * b + T], of("late", "in_b", b, b + 1), None, ALU.add).then_inc(sem("pad"), 1)
            dve.wait_ge(sem("pad"), 2)
            for k in range(4):
                for b in range(2):
                    w = of("late", "conv_w", 4 * b + k, 4 * b + k + 1)
                    if k == 0:
                        ins = dve.tensor_scalar(xc[:, b, :], pad[:, b, 0:T], w, of("late", "conv_b", b, b + 1), ALU.mult, ALU.add)
                    else:
                        ins = dve.scalar_tensor_tensor(xc[:, b, :], pad[:, b, k:k + T], w, xc[:, b, :], ALU.mult, ALU.add)
                    ins.then_inc(sem("taps"), 1)
                dve.wait_ge(sem("taps"), 2 * k + 2)
            dve.sem_inc(sem("xc"), 1)
            dve.wait_ge(sem("tanh_g"), 1)
            dve.scalar_tensor_tensor(gs2[:], tanh_g[:], 1.0, gT[:], ALU.add, ALU.mult).then_inc(sem("gs2"), 1)
            dve.wait_ge(sem("tanh_xc"), 1)
            dve.scalar_tensor_tensor(xs2[:], tanh_xc[:], 1.0, xc[:], ALU.add, ALU.mult).then_inc(sem("xs2"), 1)
            dve.memset(decay[:, :, :, 0:1], 0.0).then_inc(sem("decay_zero"), 1)
            dve.wait_ge(sem("bc"), 1)
            link(dve.tensor_scalar(bcT[:], PS[0:2 * N, 3, 0:T], 0.5, sm("bc_b", 2 * N), ALU.mult, ALU.add))
            dve.tensor_tensor(bc_own[:, :, :], bcT[:].unsqueeze(1).to_broadcast([2 * N, N, T]),
                              sm("own", 2 * N).unsqueeze(2).to_broadcast([2 * N, N, T]), ALU.mult).then_inc(sem("bc_own"), 1)
            dve.wait_ge(sem("dt"), 1)
            for b in range(2):
                dve.tensor_scalar(z[:, b, :], PS[:, 4, T * b:T * b + T], of("late", "dup_b", b, b + 1), None, ALU.add).then_inc(sem("z"), 1)
            dve.wait_ge(sem("z"), 2)
            dve.scalar_tensor_tensor(zneg[:], z[:], -1.0, z[:], ALU.mult, ALU.min).then_inc(sem("zneg"), 1)
            link(dve.tensor_scalar(zpos[:], z[:], 0.0, None, ALU.max))
            dve.wait_ge(sem("xs2"), 1)
            dve.wait_ge(sem("lz"), 1)
            link(dve.tensor_tensor(delta[:], zpos[:], lz[:], ALU.add))
            dve.wait_ge(sem("expA"), 1)
            for b in range(2):
                dve.tensor_tensor(dA[:, b], delta[:, b:b + 1, :].to_broadcast([D, N, T]), expA[:, b, :].unsqueeze(2).to_broadcast([D, N, T]), ALU.mult).then_inc(sem("dA"), 1)
            link(dve.scalar_tensor_tensor(dx[:], delta[:], 0.5, xs2[:], ALU.mult, ALU.mult))
            for b in range(2):
                dve.wait_ge(sem("b_wide"), 1)
                link(dve.tensor_tensor(Bx[:, b], PS[:, 0:2, :].rearrange("p k (n t) -> p (k n) t", t=T), dx[:, b:b + 1, :].to_broadcast([D, N, T]), ALU.mult))
                dve.wait_ge(sem("decay"), b + 1)
                dve.wait_ge(sem("decay_zero"), 1)
                flat = [a[:, b].rearrange("p n t -> p (n t)") for a in (hs, decay, Bx)]
                link(dve.tensor_tensor_scan(flat[0], flat[1], flat[2], 0.0, ALU.mult, ALU.add))
                dve.wait_ge(sem("c_wide"), 1)
                link(dve.tensor_tensor(hC[:, b], PS[:, 2:4, :].rearrange("p k (n t) -> p (k n) t", t=T), hs[:, b], ALU.mult))
                link(dve.reduce_sum(y[:, b, :], hC[:, b].rearrange("p n t -> p t n"), X))
                dve.wait_ge(sem("gs2"), 1)
                dve.scalar_tensor_tensor(yg[:, b, :], y[:, b, :], 0.5, gs2[:, b, :], ALU.mult, ALU.mult).then_inc(sem("yg"), 1)
            dve.wait_ge(sem("ssm"), 1)
            dve.wait_ge(sem("xr"), 1)
            link(dve.tensor_tensor(x5[:], PS[0:T, 4, 256:256 + D], xr[:], ALU.add))

            layer_norm(x5[:])
            dve.wait_ge(sem("norm_turned"), 7)
            dve.tensor_copy(x6T[:], PS[:, 1, 0:T]).then_inc(sem("norm_columns"), 1)
            dve.wait_ge(sem("ff6"), 1)
            dve.tensor_tensor(x6[:], PS[0:T, 2, 128:128 + D], x5[:], ALU.add).then_inc(sem("x6"), 1)

        @block.tensor
        def _(pe):
            mm = pe.matmul

            def turn(out_, in_):
                return pe.transpose(out_, in_, ident[0:T, 0:T])

            fills = iter(range(len(FILL)))

            def fill(n=1):
                for _ in range(n):
                    i = next(fills)
                    kind, c = FILL[i]
                    if i >= 2:
                        pe.wait_ge(sem("fill_out"), i - 1)
                    if i == 0:
                        pe.wait_ge(sem("kv_in"), 16)
                        for j in range(4):
                            pe.wait_ge(sem(f"ctxT_in{j}"), 32 if j < 3 else 16)
                    bank = PS[:, F_BANKS[i % 2], :]
                    if kind == "k":
                        mm(bank[:, 0:width(c)], of("kv", "WkT"), ctxT[:, 512 * c:512 * c + width(c)], start=True, stop=True).then_inc(sem("fill"), 1)
                    else:
                        for t in range(width(c) // D):
                            tile = CHUNK * c + t
                            ins = mm(bank[:, D * t:D * t + D], ctxT[:, D * tile:D * tile + D], of("kv", "WvT"), start=True, stop=True)
                        ins.then_inc(sem("fill"), 1)

            bsteps = iter(range(len(BSTEPS)))

            def bfly(n=1):
                for _ in range(n):
                    which, i = BSTEPS[next(bsteps)]
                    k = i if which == "up" else IN_BLOCK - 1 - i
                    pe.wait_ge(sem(f"mats_{which}"), i + 1)
                    if i:
                        pe.wait_ge(sem(f"{which}_evac"), i)
                    elif which == "dn":
                        pe.wait_ge(sem("dn_start"), 1)
                    for b in range(FB):
                        if which == "up":
                            src = up[1 + (i - 1) % 2] if i else up[0]
                            o = PS[:, 5 + b // 2, (b % 2) * (D + 1):(b % 2 + 1) * (D + 1)]
                        else:
                            src = dn[1 + (i - 1) % 2] if i else dn[2]
                            o = PS[:, 7, D * b:D * b + D]
                        ins = mm(o, mats[which][k][:, b, :], src[:, b, :], start=True, stop=True)
                    ins.then_inc(sem(f"{which}_step"), 1)

            pe.wait_ge(sem("first_in"), 16)
            pe.wait_ge(sem("normed"), 1)
            turn(PS[:, 7, 0:T], nm(0)).then_inc(sem("norm_turned"), 1)
            pe.wait_ge(sem("norm_columns"), 1)
            mm(PS[:, 7, 64:64 + T], of("first", "W0"), xnT[:, 0, :], start=True, stop=True)
            mm(PS[:, 7, 128:129], xnT[:].rearrange("p a n -> p (a n)"), of("first", "b0"), start=True, stop=True).then_inc(sem("qW"), 1)
            pe.wait_ge(sem("qWT"), 1)
            for j in range(7):
                pe.wait_ge(sem(f"ctxT_in{j // 2}"), 32 if j < 6 else 16)
                if j >= 2:
                    pe.wait_ge(sem("s0_out"), j - 1)
                bank = PS[:, S_BANKS[j % 2], :]
                if j < 6:
                    a = HALF0 * D + 512 * j
                    mm(bank[0:T, :], qWT[:], ctxT[:, 512 * j:512 * j + 512], start=True, stop=True)
                    mm(bank[T:D, :], qWT[:], ctxT[:, a:a + 512], start=True, stop=True).then_inc(sem("s0"), 1)
                else:
                    mm(bank[0:T, 0:D], qWT[:], ctxT[:, 512 * j:512 * j + D], start=True, stop=True).then_inc(sem("s0"), 1)
            fill(2)
            pe.wait_ge(sem("nmax0"), 1)
            mm(PS[:, 7, 130:131], of("first", "swap"), nmax0[:], start=True, stop=True).then_inc(sem("nmax_other"), 1)
            pe.wait_ge(sem("scores_tail"), 1)
            for c in range(8):
                if c < 7:
                    pe.wait_ge(sem("exp0"), c + 1)
                    if c >= 2:
                        pe.wait_ge(sem("pT0"), c - 1)
                    for t in range(CHUNK * c, min(CHUNK * c + CHUNK, HALF0)):
                        ins = pe.transpose(PS[:, T_BANKS[c % 2], (t % CHUNK) * D:(t % CHUNK + 1) * D], scoresA[:, D * t:D * t + D], ident)
                    ins.then_inc(sem("turned0"), 1)
                if c >= 1:
                    pe.wait_ge(sem("pT0"), c)
                    for j in range(5):
                        pe.wait_ge(sem(f"ctxN_in{j}"), 32)
                    for t in range(CHUNK * (c - 1), min(CHUNK * c, HALF0)):
                        w = pT[:, (c - 1) % 3, (t % CHUNK) * D:(t % CHUNK + 1) * D]
                        ins = mm(PS[0:T, 4, 0:D], w[:, 0:T], ctxN[:, t, :], start=(t == 0), stop=(t == HALF0 - 1))
                        if t < HALF1:
                            ins = mm(PS[T:D, 4, 0:D], w[:, T:D], ctxN[:, HALF0 + t, :], start=(t == 0), stop=(t == HALF1 - 1))
                    ins.then_inc(sem("pv0"), 1)
                if c < 5:
                    fill(1)
            pe.wait_ge(sem("wl"), 1)
            mm(PS[:, 7, 132:133], of("first", "pair_sum"), wl[:], start=True, stop=True).then_inc(sem("l_both"), 1)
            pe.wait_ge(sem("o_sc"), 1)
            mm(PS[:, 7, 192:192 + T], o_sc[:], of("first", "stack"), start=True, stop=True).then_inc(sem("att"), 1)
            pe.wait_ge(sem("rows_in"), 16)
            pe.wait_ge(sem("ones_ready"), 1)
            mm(PS[0:T, 3, 256:256 + D], ones[:], row("b0"), start=True, stop=False)
            pe.wait_ge(sem("attT"), 1)
            mm(PS[0:T, 3, 256:256 + D], attT[:], of("first", "W0T"), start=False, stop=True).then_inc(sem("xattn"), 1)
            fill(2)

            pe.wait_ge(sem("mats_in"), 16)
            pe.wait_ge(sem("normed"), 2)
            turn(PS[:, 4, 0:T], nm(1)).then_inc(sem("norm_turned"), 1)
            pe.wait_ge(sem("norm_columns"), 2)
            mm(PS[:, 0, 0:T], of("mats", "Wq"), xn1T[:, 0, :], start=True, stop=True)
            mm(PS[:, 0, T:2 * T], of("mats", "Wk"), xn1T[:, 0, :], start=True, stop=True).then_inc(sem("qkT"), 1)
            mm(PS[0:HD0, 1, 0:T], of("mats", "Wg1"), xn1T[:, 0, :], start=True, stop=True).then_inc(sem("g1"), 1)
            mm(PS[:, 2, 0:D], xn1T[:].rearrange("p a n -> p (a n)"), of("mats", "Wv"), start=True, stop=True).then_inc(sem("v0"), 1)
            pe.wait_ge(sem("s2"), 1)
            mm(PS[:, 3, 0:2 * T], of("mats", "rotT"), s2[:].rearrange("p a n -> p (a n)"), start=True, stop=True).then_inc(sem("rotated"), 1)
            pe.wait_ge(sem("small_in"), 16)
            pe.wait_ge(sem("g1T"), 1)
            mm(PS[0:T, 7, 256:256 + D], g1T[:], sm("Wg2", HD0), start=True, stop=True).then_inc(sem("gate"), 1)
            fill(1)
            pe.wait_ge(sem("q_heads"), 1)
            mm(PS[0:T, 0, :], qk[:, 1, :], q_heads[:, 0:8, :].rearrange("p h n -> p (h n)"), start=True, stop=True)
            pe.wait_ge(sem("q_heads"), 2)
            mm(PS[T:D, 0, :], qk[:, 1, :], q_heads[:, 8:16, :].rearrange("p h n -> p (h n)"), start=True, stop=True).then_inc(sem("energy"), 1)
            fill(1)
            pe.wait_ge(sem("v_halves"), 2)
            pe.wait_ge(sem("masked"), 1)
            v4 = v_halves[:].rearrange("p a (h d) -> p a h d", d=HD0)
            o4 = PS[0:T, 1, 128:128 + D].rearrange("p (a h d) -> p a h d", a=2, d=HD0)
            for h in range(8):
                ins = mm(o4[:, :, h, :], energy[:, h, :], v4[:, :, h, :], start=True, stop=True)
            ins.then_inc(sem("lin_att"), 1)
            fill(2)
            pe.wait_ge(sem("normed"), 3)
            turn(PS[:, 4, 64:64 + T], nm(2)).then_inc(sem("norm_turned"), 1)
            pe.wait_ge(sem("norm_columns"), 3)
            mm(PS[0:T, 4, 128:128 + D], yT[:], of("mats", "Wo"), start=True, stop=True).then_inc(sem("attn_out"), 1)
            fill(7)

            pe.wait_ge(sem("normed"), 6)
            turn(PS[:, 0, 0:T], nm(5)).then_inc(sem("norm_turned"), 1)
            pe.wait_ge(sem("norm_columns"), 4)
            mm(PS[:, 1, 0:T], of("mats", "saWvT"), tgtT[:], start=True, stop=True).then_inc(sem("v1"), 1)
            mm(PS[0:T, 2, 128:128 + D], ones[:], row("sa_out_b"), start=True, stop=False)
            pe.wait_ge(sem("vT"), 1)
            mm(PS[0:T, 2, 128:128 + D], vT[:], of("mats", "sa_outT"), start=False, stop=True).then_inc(sem("sa"), 1)
            fill(6)
            pe.wait_ge(sem("normed"), 7)
            turn(PS[:, 0, 64:64 + T], nm(6)).then_inc(sem("norm_turned"), 1)
            pe.wait_ge(sem("norm_columns"), 5)
            mm(PS[:, 4, 256:256 + T], of("mats", "WqT"), z6T[:], start=True, stop=True).then_inc(sem("q1"), 1)

            pe.wait_ge(sem("q_wide"), 2)
            pe.wait_ge(sem("fill_out"), len(FILL))

            def score(g, c):
                n = g * CHUNKS + c
                if n == CHUNKS:
                    pe.wait_ge(sem("q_wide"), 3)
                if n >= 2:
                    pe.wait_ge(sem("s1_out"), n - 1)
                mm(PS[:, S_BANKS[n % 2], 0:width(c)], q_wide[:, 2 * g:2 * g + 2, :].rearrange("p a n -> p (a n)"), KT[:, 512 * c:512 * c + width(c)],
                   start=True, stop=True).then_inc(sem("s1"), 1)

            def turn_weights(g, c):
                n = g * CHUNKS + c
                pe.wait_ge(sem("exp1"), n + 1)
                if n >= 2:
                    m = n - 2
                    even, odd = taken(m)
                    if m % CHUNKS % 2 == 0:
                        pe.wait_ge(sem("pT_dve"), even)
                    else:
                        pe.wait_ge(sem("pT_act"), odd)
                for t in range(width(c) // D):
                    a = 512 * c + D * t
                    ins = pe.transpose(PS[:, T_BANKS[n % 2], D * t:D * t + D], scores[g % 2][:, a:a + D], ident)
                ins.then_inc(sem("turned"), 1)

            def taken(n):
                g, c = divmod(n, CHUNKS)
                return g * 7 + c // 2 + 1, g * 6 + (c + 1) // 2

            def apply_weights(g, c):
                n = g * CHUNKS + c
                even, odd = taken(n)
                if c % 2 == 0:
                    pe.wait_ge(sem("pT_dve"), even)
                else:
                    pe.wait_ge(sem("pT_act"), odd)
                if g >= 2 and c == 0:
                    pe.wait_ge(sem("oS"), g - 1)
                for t in range(width(c) // D):
                    tile = CHUNK * c + t
                    ins = mm(PS[32 * t:32 * t + 32, O_BANKS[g % 2], 0:D], V[:, tile, 32 * g:32 * g + 32], pT[:, n % 4, D * t:D * t + D],
                             start=(c == 0), stop=(tile + CHUNK >= TILES))
                ins.then_inc(sem("pv"), 1)

            def heads(g):
                pe.wait_ge(sem("oS"), g + 1)
                if g:
                    pe.wait_ge(sem("ca"), 2 * g)
                mm(PS[:, 5, 0:32], oS[:, g % 2, :], of("mats", "sumsel"), start=True, stop=True).then_inc(sem("heads"), 1)

            for g in range(PAIRS + 1):
                for c in range(CHUNKS + 2):
                    if g < PAIRS and c < CHUNKS:
                        score(g, c)
                    if g >= 1 and c < CHUNKS:
                        turn_weights(g - 1, c)
                    if g >= 1 and c >= 2:
                        apply_weights(g - 1, c - 2)
                if g >= 1:
                    heads(g - 1)
            pe.wait_ge(sem("ca"), 2 * PAIRS)
            turn(PS[:, 0, 0:T], ca[:]).then_inc(sem("caT"), 1)
            mm(PS[0:T, 1, 256:256 + D], ones[:], row("mha_out_b"), start=True, stop=False)
            pe.wait_ge(sem("caT_out"), 1)
            mm(PS[0:T, 1, 256:256 + D], caT[:], of("mats", "mha_outT"), start=False, stop=True).then_inc(sem("mha"), 1)
            bfly(1)
            pe.wait_ge(sem("normed"), 8)
            turn(PS[:, 2, 0:T], nm(7)).then_inc(sem("norm_turned"), 1)
            pe.wait_ge(sem("late_in"), 16)
            pe.wait_ge(sem("norm_columns"), 6)
            for b in (2, 3, 0, 1):
                ins = mm(PS[:, b // 2, T * (b % 2):T * (b % 2) + T], of("late", "lin1T", D * b, D * b + D), z7T[:], start=True, stop=True)
                if b % 2:
                    ins.then_inc(sem("lin1_b" if b == 3 else "lin1_a"), 1)
            mm(PS[0:T, 2, 128:128 + D], ones[:], row("lin2_b"), start=True, stop=False)
            pe.wait_ge(sem("h_act"), 2)
            pe.wait_ge(sem("h_dve"), 2)
            for b in range(FB):
                ins = mm(PS[0:T, 2, 128:128 + D], hT[:, b, :], of("late", "lin2T", D * b, D * b + D), start=False, stop=(b == FB - 1))
            ins.then_inc(sem("ff"), 1)
            bfly(3)
            pe.wait_ge(sem("rms_h"), 1)
            turn(PS[:, 2, 256:256 + T], rms_h[:]).then_inc(sem("rmsT"), 1)
            pe.wait_ge(sem("hmT"), 1)
            for b in range(4):
                ins = mm(PS[:, b // 2, T * (b % 2):T * (b % 2) + T], of("late", "in_W", D * b, D * b + D), hmT[:], start=True, stop=True)
                if b % 2:
                    ins.then_inc(sem("x_in1" if b == 1 else "gate1"), 1)
            bfly(1)
            pe.wait_ge(sem("xs2"), 1)
            dbc = of("late", "dbc_W").rearrange("p (b j) -> p b j", b=2)
            for b in range(2):
                ins = mm(PS[0:N, 2, 0:T], dbc[:, b, 0:N], xs2[:, b, :], start=(b == 0), stop=(b == 1))
            ins.then_inc(sem("dt_low"), 1)
            for b in range(2):
                ins = mm(PS[0:2 * N, 3, 0:T], dbc[:, b, N:3 * N], xs2[:, b, :], start=(b == 0), stop=(b == 1))
            ins.then_inc(sem("bc"), 1)
            pe.wait_ge(sem("dtT"), 1)
            for b in range(2):
                ins = mm(PS[:, 4, T * b:T * b + T], sm("dup_W", N)[:, D * b:D * b + D], dtT[:], start=True, stop=True)
            ins.then_inc(sem("dt"), 1)
            bfly(1)
            pe.wait_ge(sem("bc_own"), 1)
            own = bc_own.rearrange("p n t -> p (n t)")
            for name, bank, done in (("onesB", 0, "b_wide"), ("onesC", 2, "c_wide")):
                for h in range(2):
                    ins = mm(PS[:, bank + h, :], sm(name, 2 * N), own[:, 512 * h:512 * h + 512], start=True, stop=True)
                ins.then_inc(sem(done), 1)
            bfly(8)
            pe.wait_ge(sem("up_done"), 1)
            last = up[1 + (IN_BLOCK - 1) % 2]
            for b in range(FB):
                ins = pe.transpose(PS[:, 5, D * b:D * b + D], last[:, b, 0:D], ident)
            ins.then_inc(sem("wup_turned"), 1)
            pe.wait_ge(sem("z"), 2)
            mm(PS[0:T, 4, 256:256 + D], ones[:], row("out_b"), start=True, stop=False)
            for b in range(2):
                pe.wait_ge(sem("yg"), b + 1)
                ins = mm(PS[0:T, 4, 256:256 + D], yg[:, b, :], of("late", "out_W", D * b, D * b + D), start=False, stop=(b == 1))
            ins.then_inc(sem("ssm"), 1)

            pe.wait_ge(sem("normed"), 11)
            turn(PS[:, 1, 0:T], nm(11)).then_inc(sem("norm_turned"), 1)
            mm(PS[0:T, 2, 128:128 + D], ones[:], row("b_con"), start=True, stop=False)
            mm(PS[0:T, 2, 128:128 + D], ones[:], row("down_bias"), start=False, stop=False)
            pe.wait_ge(sem("wup"), 1)
            pe.wait_ge(sem("norm_columns"), 7)
            for b in range(FB):
                ins = mm(PS[:, 0, T * b:T * b + T], wup[:, b, :], x6T[:], start=True, stop=True)
            ins.then_inc(sem("h6"), 1)
            pe.wait_ge(sem("dn_evac"), IN_BLOCK)
            wdn = dn[1 + (IN_BLOCK - 1) % 2]
            for b in range(FB):
                pe.wait_ge(sem("gelu"), b + 1)
                ins = mm(PS[0:T, 2, 128:128 + D], gl6[:, b, :], wdn[:, b, :], start=False, stop=(b == FB - 1))
            ins.then_inc(sem("ff6"), 1)


def shape_constants():
    eye = np.eye(D, dtype=np.float32)
    c = {"ident": eye, "swap": np.roll(eye, T, axis=0)}
    c["pair_sum"] = np.tile(np.eye(T, dtype=np.float32), (2, 2))
    c["stack"] = np.tile(np.eye(T, dtype=np.float32), (2, 1))
    inv = 1.0 / np.float32(10000.0) ** (np.arange(0, HD0, 2, dtype=np.float32) / np.float32(HD0))
    ang = np.arange(T, dtype=np.float32)[:, None] * inv[None, :].astype(np.float32)
    c["cosT"] = np.tile(np.cos(ang).T, (2 * H0, 1))
    c["sinT"] = np.tile(np.sin(ang).T, (2 * H0, 1))
    rot = np.zeros((D, D), np.float32)
    for i in range(D):
        rot[i, i + 4 if i % 8 < 4 else i - 4] = -1.0 if i % 8 < 4 else 1.0
    c["rotT"] = rot.T
    r = np.arange(D)
    c["head"] = (r[:, None] // HD0 == np.arange(H0)[None, :]).astype(np.float32)
    c["causal"] = (r[:, None] % T <= np.arange(T)[None, :]).astype(np.float32) * np.float32(0.125)
    c["head1"] = (r[:, None] // HD1 == np.arange(H1)[None, :]).astype(np.float32) * np.float32(HD1 ** -0.5)
    c["sumsel"] = np.tile(np.eye(32, dtype=np.float32), (4, 1))
    c["perm"] = np.concatenate([(r[:, None] == (r ^ (1 << k))[None, :]).astype(np.float32) for k in range(IN_BLOCK)], axis=1)
    n = np.arange(2 * N)
    c["own"] = (n[:, None] % N == np.arange(N)[None, :]).astype(np.float32)
    c["onesB"] = np.repeat((n[:, None] < N).astype(np.float32), D, axis=1)
    c["onesC"] = np.repeat((n[:, None] >= N).astype(np.float32), D, axis=1)
    return c


def stage_weights(w, turned):
    f = np.arange(FF)
    out = np.empty((STAGES, FF, 2), w.dtype)
    for k in range(STAGES):
        s = 1 << k
        pair, second = (f // (2 * s)) * s + f % s, (f // s) % 2
        out[k, :, 0] = w[k, pair, second, second]
        swap = turned != (k < IN_BLOCK)
        i, j = (1 - second, second) if swap else (second, 1 - second)
        out[k, :, 1] = w[k, pair, i, j]
    return out.reshape(STAGES, FB, D, 2).transpose(2, 0, 1, 3).reshape(D, -1)


def kernel(**inputs):
    import concourse.bacc as bacc
    from concourse.bass_utils import run_bass_kernel_spmd as run

    a = {k: np.asarray(v) for k, v in inputs.items()}
    c = shape_constants()

    def col(v):
        return v.reshape(-1, D).T

    def blocks(w):
        return w.reshape(-1, D, w.shape[1]).transpose(1, 0, 2).reshape(D, -1)

    in_proj, in_proj_b = a["L1_xattn_in_proj_w"], a["L1_xattn_in_proj_b"]
    expT = np.concatenate([a["L1_ffn_W_exp"].T, a["L1_ffn_b_exp"][:, None]], axis=1)
    conv = a["L1_attn_conv_w"]
    values = dict(c)
    values.update({
        "W0": a["L0_xattn_W"], "W0T": a["L0_xattn_W"].T, "b0": col(a["L0_xattn_b"]),
        "WkT": in_proj[D:2 * D].T, "WvT": in_proj[2 * D:].T, "bk": col(in_proj_b[D:2 * D]),
        "Wq": a["L0_attn_Wq"], "Wk": a["L0_attn_Wk"], "Wv": a["L0_attn_Wv"], "Wg1": a["L0_attn_Wg1"], "Wo": a["L0_attn_Wo"],
        "ln_w": col(a["L0_attn_ln_w"]), "ln_b": col(a["L0_attn_ln_b"]),
        "saWvT": a["L1_xattn_qkv_w"][2 * D:].T, "sa_bv": col(a["L1_xattn_qkv_b"][2 * D:]), "sa_outT": a["L1_xattn_sa_out_w"].T,
        "ln1_g": col(a["L1_xattn_ln1_g"]), "ln1_b": col(a["L1_xattn_ln1_b"]),
        "WqT": in_proj[:D].T, "bq": col(in_proj_b[:D]), "bv": col(in_proj_b[2 * D:]), "mha_outT": a["L1_xattn_mha_out_w"].T,
        "ln2_g": col(a["L1_xattn_ln2_g"]), "ln2_b": col(a["L1_xattn_ln2_b"]),
        "lin1T": a["L1_xattn_lin1_w"].T, "lin1_b": col(a["L1_xattn_lin1_b"]), "lin2T": blocks(a["L1_xattn_lin2_w"].T),
        "rms_w": col(a["L1_attn_rms_w"]), "in_W": a["L1_attn_in_W"], "in_b": col(a["L1_attn_in_b"]),
        "conv_w": blocks(conv), "conv_b": col(a["L1_attn_conv_b"]), "A_log": blocks(a["L1_attn_A_log"]),
        "dbc_W": blocks(a["L1_attn_dbc_W"]), "dup_b": col(a["L1_attn_dup_b"]), "out_W": blocks(a["L1_attn_out_W"]),
        "up_bias": col(a["L1_ffn_up_bias"]),
        "coef_up": stage_weights(a["L1_ffn_up_weights"], False), "coef_dn": stage_weights(a["L1_ffn_down_weights"], True),
        "expT": blocks(expT), "con": blocks(a["L1_ffn_W_con"]),
    })
    small_at, small_w = offsets(SMALL)
    small = np.zeros((32, small_w), np.float32)
    dbc_b = a["L1_attn_dbc_b"][:, None]
    for name, v in (("Wg2", a["L0_attn_Wg2"]), ("dup_W", a["L1_attn_dup_W"]), ("dt_b", dbc_b[:N]), ("bc_b", dbc_b[N:]),
                    ("own", c["own"]), ("onesB", c["onesB"]), ("onesC", c["onesC"])):
        small[0:v.shape[0], small_at[name][0]:small_at[name][1]] = v
    ctx = a["ctx_1024"][0]
    row_values = {"b0": "L0_xattn_b", "sa_out_b": "L1_xattn_sa_out_b", "mha_out_b": "L1_xattn_mha_out_b", "lin2_b": "L1_xattn_lin2_b",
                  "out_b": "L1_attn_out_b", "b_con": "L1_ffn_b_con", "down_bias": "L1_ffn_down_bias"}
    wide_values = {n: "L1_xattn_" + n for n in WIDE}
    wide_values.update({"ffn_g": "L0_ffn_ln_g", "ffn_b": "L0_ffn_ln_b"})
    arrays = {
        "x_in": a["x"][0], "ctxT_in": ctx.T, "ctxN_in": ctx.reshape(TILES, D, D).transpose(1, 0, 2),
        **{f"{p}_in": np.concatenate([values[n] for n, _ in entries], axis=1) for p, entries in PACKS.items()},
        "rows_in": np.concatenate([a[row_values[n]] for n in ROWS])[None, :],
        "wide_in": np.broadcast_to(np.concatenate([a[wide_values[n]] for n in WIDE]), (T, len(WIDE) * D)),
        "small_in": small,
    }
    nc = bacc.Bacc("TRN2", target_bir_lowering=False, num_devices=1)
    arrays = {k: np.ascontiguousarray(v) for k, v in arrays.items()}
    aps = {k: nc.dram_tensor(k, v.shape, mybir.dt.from_np(v.dtype), kind="ExternalInput").ap() for k, v in arrays.items()}
    out = nc.dram_tensor("out", (T, D), mybir.dt.float32, kind="ExternalOutput").ap()
    build(nc, out=out, **aps)
    r = run(nc, [arrays], core_ids=[0])
    return r.results[0]["out"].reshape(1, T, D)
```

```python
from contextlib import ExitStack

import numpy as np
import concourse.bass as bass
from concourse import mybir

T = 64
D = 128
M = 6272
TILES = M // D
CHUNK = 4
CHUNKS = -(-TILES // CHUNK)
HALF0 = 25
HALF1 = TILES - HALF0
H0, HD0 = 16, 8
H1, HD1 = 8, 16
PAIRS = H1 // 2
N = 16
DI = 256
FF = 512
FB = FF // D
STAGES = 9
LO = 5
RING = 4
EPS = 1e-5
RMS_EPS = 1e-6

FIRST = [("W0", D), ("ident", D), ("b0", 1), ("swap", D), ("pair_sum", D), ("stack", T), ("W0T", D)]
KV = [("WvT", D)]
MATS = [("Wq", D), ("Wk", D), ("Wv", D), ("Wg1", HD0), ("Wo", D), ("rotT", D), ("cosT", T), ("sinT", T),
        ("head", H0), ("causal", T), ("ln_w", 1), ("ln_b", 1),
        ("saWvT", D), ("sa_bv", 1), ("sa_outT", D), ("ln1_g", 1), ("ln1_b", 1), ("WqT", D), ("bq", 1), ("Wk1", D), ("bk", 1), ("head1", H1),
        ("bv", 1), ("sumsel", 32), ("mha_outT", D), ("ln2_g", 1), ("ln2_b", 1)]
LATE = [("lin1T", FF), ("lin1_b", FB), ("lin2T", FB * D), ("rms_w", 1), ("in_W", 2 * DI), ("in_b", 4),
        ("conv_w", 8), ("conv_b", 2), ("A_log", 2 * N), ("dbc_W", 2 * 48), ("dup_b", 2), ("out_W", 2 * D),
        ("up_bias", FB)]
BFLY = [("exp", FF), ("conT", FF)]
PACKS = {"first": FIRST, "kv": KV, "mats": MATS, "late": LATE, "bfly": BFLY}
ROWS = ["b0", "sa_out_b", "mha_out_b", "lin2_b", "out_b", "b_con", "down_bias"]
WIDE = ["ffn_g", "ffn_b", "ln1_g", "ln1_b", "ln2_g", "ln2_b", "ln3_g", "ln3_b"]
SMALL = [("Wg2", D), ("dup_W", 2 * D), ("dt_b", 1), ("bc_b", 1), ("own", N), ("onesB", D), ("onesC", D),
         ("b_exp", 32), ("coef_lo", LO * 2 * 32), ("coef_hi", (STAGES - LO) * 2 * 16)]


def offsets(entries):
    at, out = 0, {}
    for name, width in entries:
        out[name] = (at, at + width)
        at += width
    return out, at


def build(nc, x_in, ctxT_in, ctxN_in, first_in, kv_in, mats_in, late_in, bfly_in, rows_in, wide_in, small_in, coef_in, out):
    f32 = mybir.dt.float32
    ACT = mybir.ActivationFunctionType
    ALU = mybir.AluOpType
    X = mybir.AxisListType.X
    ctx = ExitStack()
    with ctx:
        sems = {}

        def sem(name):
            if name not in sems:
                sems[name] = ctx.enter_context(nc.semaphore(name))
            return sems[name]

        def sb(name, *shape):
            return ctx.enter_context(nc.sbuf_tensor(name, list(shape), f32))

        pack, place = {}, {}
        for name, entries in PACKS.items():
            place[name], width = offsets(entries)
            pack[name] = sb("p_" + name, D, width)
        small_at, small_w = offsets(SMALL)
        small = sb("p_small", 32, small_w)

        def of(p, name, lo=0, hi=None):
            a, b = place[p][name]
            return pack[p][:, a + lo:(a + hi if hi is not None else b)]

        def sm(name, rows):
            a, b = small_at[name]
            return small[0:rows, a:b]

        rows = sb("rows", 1, len(ROWS) * D)

        def row(name):
            i = ROWS.index(name)
            return rows[0:1, i * D:(i + 1) * D]

        wide = sb("wide", T, len(WIDE) * D)

        def wd(name):
            i = WIDE.index(name)
            return wide[:, i * D:(i + 1) * D]

        ident = of("first", "ident")
        ctxT = sb("ctxT", D, M)
        V = sb("V", D, TILES, D)
        scoresA = sb("scoresA", D, M)
        big = sb("big", D, M)
        ctxN = big[:, :].rearrange("p (t c) -> p t c", c=D)
        scores = [scoresA, big]
        pT = sb("pT", D, 4, CHUNK * D)
        coefs = sb("coefs", D, RING, 2, FF)

        x = sb("x", T, D)
        half_power = sb("half_power", T, 1)
        ones = sb("ones", 1, T)
        LN = 12
        stats, mv = sb("stats", T, 6 * LN), sb("mv", T, 2 * LN)
        var_eps, rstd = sb("var_eps", T, LN), sb("rstd", T, LN)
        norm = sb("norm", T, LN * D)

        def nm(i):
            return norm[:, i * D:(i + 1) * D]

        x1, x2, x3, x4, x5, x6 = (sb(f"x{i}", T, D) for i in range(1, 7))
        used = [0]

        def after(_name, parts, *shape):
            n = int(np.prod(shape))
            flat = V[0:parts].rearrange("p t c -> p (t c)")[:, used[0]:used[0] + n]
            used[0] += n
            assert used[0] <= M
            if len(shape) == 1:
                return flat
            names = "abc"[:len(shape)]
            return flat.rearrange(f"p ({' '.join(names)}) -> p {' '.join(names)}", **dict(zip(names, shape)))

        xnT = sb("xnT", D, 2, T)
        qWT, cp = sb("qWT", D, T), sb("cp", D, 1)
        cmax, lsum = sb("cmax", D, 8), sb("lsum", D, 8)
        nmax0, nmaxM, w0, l0, wl, rL, fac = (sb(n, D, 1) for n in ("nmax0", "nmaxM", "w0", "l0", "wl", "rL", "fac"))
        o_sc, attT = sb("o_sc", D, D), sb("attT", D, T)
        xn1T = sb("xn1T", D, 2, T)
        tanh_qk, s2, s2cos, s2sin, qk = (sb(n, D, 2, T) for n in ("tanh_qk", "s2", "s2cos", "s2sin", "qk"))
        q_heads = big[:, 0:H0 * T].rearrange("p (h n) -> p h n", h=H0)
        energy = big[:, 2048:2048 + H0 // 2 * T].rearrange("p (h n) -> p h n", h=H0 // 2)
        g1T, tanh_gate = sb("g1T", HD0, T), sb("tanh_gate", T, D)
        v_halves = sb("v_halves", D, 2, T)
        gated, yT = sb("gated", T, D), sb("yT", D, T)
        x2b, zg, tgtT, vT, t1, z6T = sb("x2b", T, D), sb("zg", T, D), sb("tgtT", D, T), sb("vT", D, T), sb("t1", T, D), sb("z6T", D, T)
        xg, x_q, q_all = sb("xg", T, D), sb("x_q", T, D), sb("q_all", D, T)
        q_wide = sb("q_wide", D, H1, T)
        qk1 = sb("qk1", D, H1, T)
        cp1 = sb("cp1", D, PAIRS)
        max1, sum1 = sb("max1", D, PAIRS, 16), sb("sum1", D, PAIRS, 16)
        nmax1, l1, rl1 = sb("nmax1", D, PAIRS), sb("l1", D, PAIRS), sb("rl1", D, PAIRS)
        oS, ca, caT = sb("oS", D, 2, D), sb("ca", T, D), sb("caT", D, T)
        t2, z7T, x7g, x7, hT, t3, z8g, x3b = after("t2", T, D), after("z7T", D, T), after("x7g", T, D), after("x7", T, D), after("hT", D, FB, T), after("t3", T, D), after("z8g", T, D), sb("x3b", T, D)
        sq, msum, rms_h, hmT = after("sq", T, D), after("msum", T, 1), after("rms_h", T, D), after("hmT", D, T)
        pad = sb("pad", D, 2, T + 3)
        xc, tanh_xc, xs2 = after("xc", D, 2, T), after("tanh_xc", D, 2, T), after("xs2", D, 2, T)
        gT, tanh_g, gs2 = after("gT", D, 2, T), after("tanh_g", D, 2, T), after("gs2", D, 2, T)
        dtT, bcT = after("dtT", N, T), after("bcT", 2 * N, T)
        bc_own = big[0:2 * N, 0:N * T].rearrange("p (n t) -> p n t", n=N)
        z, zneg, ez, lz, zpos, delta, dx = (after(n, D, 2, T) for n in ("z", "zneg", "ez", "lz", "zpos", "delta", "dx"))
        expA = sb("expA", D, 2, N)
        dA, Bx, hs = (ctxT[:, i * 2 * N * T:(i + 1) * 2 * N * T].rearrange("p (b n t) -> p b n t", b=2, n=N) for i in range(3))
        decay = scoresA[:, 0:2 * N * T].rearrange("p (b n t) -> p b n t", b=2, n=N)
        hC = scoresA[:, 2 * N * T:4 * N * T].rearrange("p (b n t) -> p b n t", b=2, n=N)
        y, yg, xr = after("y", D, 2, T), after("yg", D, 2, T), after("xr", T, D)
        x6T, h6T, gl6 = after("x6T", D, T), after("h6T", D, FB, T), after("gl6", D, FB, T)
        hidden = {"up": [of("bfly", "exp"), sb("upB", D, FF)[:]], "dn": [of("bfly", "conT"), sb("dnB", D, FF)[:]]}
        partner = sb("partner", D, FF)
        wup, wdn = hidden["up"][STAGES % 2], after("wdn", D, FB, D)
        b_lo, b_hi = [sm("b_exp", 16), sb("b_lo", 16, 32)[:]], [sb("b_hiA", 32, 16)[:], sb("b_hiB", 32, 16)[:]]
        b_partner = sb("b_partner", 32, 32)
        beff = after("beff", D, FB)

        PS = ctx.enter_context(nc.psum_tensor("PS", [D, 8, 512], f32))
        S_BANKS, T_BANKS, O_BANKS, F_BANKS = (0, 1), (2, 3), (4, 7), (5, 6)

        def width(c):
            return min(CHUNK, TILES - CHUNK * c) * D

        STEPS = [("up", k) for k in range(STAGES)] + [("dn", k) for k in reversed(range(STAGES))]

        def ctxT_pieces(j):
            a = HALF0 * D
            return (1024 * j, min(1024 * j + 1024, a)), (a + 1024 * j, min(a + 1024 * j + 1024, M))

        def ctxN_pieces(j):
            return (8 * j, min(8 * j + 8, HALF0)), (HALF0 + 8 * j, min(HALF0 + 8 * j + 8, TILES))

        block = ctx.enter_context(nc.Block())

        @block.sync
        def _(sp):
            sp.dma_start(x[:], x_in).then_inc(sem("x_in"), 16)
            sp.dma_start(pack["first"][:], first_in).then_inc(sem("first_in"), 16)
            for j in range(4):
                for lo, hi in ctxT_pieces(j):
                    if lo < hi:
                        sp.dma_start(ctxT[:, lo:hi], ctxT_in[:, lo:hi]).then_inc(sem(f"ctxT_in{j}"), 16)
            for j in range(4):
                for lo, hi in ctxN_pieces(j):
                    if lo < hi:
                        sp.dma_start(ctxN[:, lo:hi, :], ctxN_in[:, lo:hi, :]).then_inc(sem(f"ctxN_in{j}"), 16)
                if j == 2:
                    sp.dma_start(rows[:], rows_in).then_inc(sem("rows_in"), 16)
                    sp.dma_start(pack["kv"][:], kv_in).then_inc(sem("kv_in"), 16)
            sp.dma_start(pack["mats"][:], mats_in).then_inc(sem("mats_in"), 16)
            sp.dma_start(small[:], small_in).then_inc(sem("small_in"), 16)
            sp.dma_start(pack["bfly"][:], bfly_in).then_inc(sem("bfly_in"), 16)
            sp.dma_start(wide[:], wide_in).then_inc(sem("wide_in"), 16)
            sp.dma_start(pack["late"][:], late_in).then_inc(sem("late_in"), 16)
            for i in range(2 * STAGES):
                if i >= RING:
                    sp.wait_ge(sem("coefs_used"), i - RING + 1)
                sp.dma_start(coefs[:, i % RING, :, :].rearrange("p j f -> p (j f)"), coef_in[i:i + 1, :].to_broadcast([D, 2 * FF])).then_inc(sem(f"coefs_in{i % RING}"), 16)
            sp.wait_ge(sem("x6"), 1)
            sp.dma_start(out, x6[:]).then_inc(sem("stored"), 16)
            sp.wait_ge(sem("stored"), 16)

        @block.gpsimd
        def _(pool):
            def rsqrt(i):
                pool.wait_ge(sem("var_ready"), i + 1)
                pool.tensor_tensor(rstd[:, i:i + 1], var_eps[:, i:i + 1], half_power[:], ALU.pow).then_inc(sem("rstd_ready"), 1)

            steps = [0]

            def link(ins):
                steps[0] += 1
                ins.then_inc(sem("pool_step"), 1)
                pool.wait_ge(sem("pool_step"), steps[0])

            def butterfly(dst, src, t, coef, stride):
                def half(ap, h):
                    return ap.rearrange("p (n h s) -> p n h s", h=2, s=stride)[:, :, h, :]
                for h in range(2):
                    link(pool.tensor_tensor(half(t, h), half(src, 1 - h), half(coef[:, 1, :], h), ALU.mult))
                link(pool.tensor_tensor(dst, src, coef[:, 0, :], ALU.mult))
                link(pool.tensor_tensor(dst, dst, t, ALU.add))

            stages = iter(enumerate(STEPS))

            def stage(n=1):
                for _ in range(n):
                    i, (which, k) = next(stages)
                    bufs, m = hidden[which], i % STAGES
                    pool.wait_ge(sem(f"coefs_in{i % RING}"), 16 * (i // RING + 1))
                    butterfly(bufs[(m + 1) % 2], bufs[m % 2], partner[:], coefs[:, i % RING], 1 << k)
                    pool.sem_inc(sem("coefs_used"), 1)

            pool.memset(half_power[:], -0.5).then_inc(sem("pool_const"), 1)
            pool.memset(ones[:], 1.0).then_inc(sem("ones_ready"), 1)
            pool.wait_ge(sem("pool_const"), 1)
            rsqrt(0)
            rsqrt(1)
            pool.wait_ge(sem("small_in"), 16)
            lo = sm("coef_lo", 16).rearrange("p (k j f) -> p k j f", k=LO, j=2)
            for k in range(LO):
                butterfly(b_lo[(k + 1) % 2], b_lo[k % 2], b_partner[0:16, 0:32], lo[:, k], 1 << k)
            pool.sem_inc(sem("b_lo"), 1)
            pool.wait_ge(sem("bfly_in"), 16)
            stage(1)
            rsqrt(2)
            rsqrt(3)
            pool.wait_ge(sem("wide_in"), 16)
            pool.wait_ge(sem("x2"), 1)
            pool.tensor_tensor(x2b[:], x2[:], wd("ffn_b"), ALU.add).then_inc(sem("x2b"), 1)
            rsqrt(4)
            rsqrt(5)
            rsqrt(6)
            pool.wait_ge(sem("normed"), 7)
            link(pool.tensor_tensor(xg[:], nm(6), wd("ln1_g"), ALU.mult))
            pool.tensor_tensor(x_q[:], xg[:], wd("ln1_b"), ALU.add).then_inc(sem("x_q"), 1)
            pool.tensor_tensor(x3b[:], x3[:], wd("ln3_b"), ALU.add).then_inc(sem("x3b"), 1)
            stage(2)
            pool.wait_ge(sem("b_hi"), 1)
            hi = sm("coef_hi", 32).rearrange("p (k j f) -> p k j f", k=STAGES - LO, j=2)
            for k in range(STAGES - LO):
                butterfly(b_hi[(k + 1) % 2], b_hi[k % 2], b_partner[:, 0:16], hi[:, k], 1 << k)
            pool.sem_inc(sem("b_up"), 1)
            stage(STAGES - 3)
            pool.sem_inc(sem("up_done"), 1)
            stage(STAGES)
            pool.sem_inc(sem("dn_done"), 1)
            rsqrt(7)
            pool.wait_ge(sem("normed"), 8)
            link(pool.tensor_tensor(x7g[:], nm(7), wd("ln2_g"), ALU.mult))
            pool.tensor_tensor(x7[:], x7g[:], wd("ln2_b"), ALU.add).then_inc(sem("x7"), 1)
            rsqrt(8)
            rsqrt(9)
            pool.wait_ge(sem("normed"), 10)
            pool.tensor_tensor(xr[:], nm(9), x4[:], ALU.add).then_inc(sem("xr"), 1)
            rsqrt(10)
            rsqrt(11)

        @block.scalar
        def _(act):
            A = act.activation
            fills = iter(range(CHUNKS))

            def fill(n=1):
                for _ in range(n):
                    c = next(fills)
                    act.wait_ge(sem("fill"), c + 1)
                    A(V[:, c * CHUNK:c * CHUNK + width(c) // D, :], PS[:, F_BANKS[c % 2], 0:width(c)].rearrange("p (t c) -> p t c", c=D),
                      ACT.Copy).then_inc(sem("fill_out"), 1)

            act.wait_ge(sem("nmax0"), 1)
            for j in range(7):
                P, w = (D, 512) if j < 6 else (T, D)
                s = scoresA[0:P, 512 * j:512 * j + w]
                A(s, s, ACT.Exp, bias=nmax0[0:P], accum_out=lsum[0:P, j:j + 1]).then_inc(sem("exp0"), 1)
            act.wait_ge(sem("nmaxM"), 1)
            A(w0[:], nmax0[:], ACT.Exp, scale=-1.0, bias=nmaxM[:]).then_inc(sem("w0"), 1)
            fill(1)
            act.wait_ge(sem("qkT"), 1)
            A(tanh_qk[:], PS[:, 0, 0:2 * T].rearrange("p (a n) -> p a n", a=2), ACT.Tanh, scale=0.5).then_inc(sem("tanh_qk"), 1)
            act.wait_ge(sem("g1"), 1)
            A(g1T[:], PS[0:HD0, 1, 0:T], ACT.Copy).then_inc(sem("g1T"), 1)
            act.wait_ge(sem("v0"), 1)
            act.wait_ge(sem("v_zero"), 1)
            for h in range(2):
                P = slice(T * h, T * h + T)
                A(v_halves[P, h, :], PS[P, 2, T * h:T * h + T], ACT.Copy).then_inc(sem("v_halves"), 1)
            act.wait_ge(sem("gate"), 1)
            A(tanh_gate[:], PS[0:T, 7, 256:256 + D], ACT.Tanh, scale=0.5).then_inc(sem("tanh_gate"), 1)
            fill(8)
            act.wait_ge(sem("v1"), 1)
            A(vT[:], PS[:, 1, 0:T], ACT.Identity, bias=of("mats", "sa_bv")).then_inc(sem("vT"), 1)
            fill(4)
            act.wait_ge(sem("late_in"), 16)
            A(expA[:].rearrange("p b n -> p (b n)"), of("late", "A_log"), ACT.Exp).then_inc(sem("expA"), 1)

            act.wait_ge(sem("b_turned"), 1)
            A(b_hi[0], PS[0:32, 7, 384:400], ACT.Copy).then_inc(sem("b_hi"), 1)

            def turned(g, c):
                n = g * CHUNKS + c
                act.wait_ge(sem("turned"), n + 1)
                if n >= 4:
                    act.wait_ge(sem("pv"), n - 3)
                A(pT[:, n % 4, 0:width(c)], PS[:, T_BANKS[n % 2], 0:width(c)], ACT.Copy).then_inc(sem("pT_act"), 1)

            for g in range(PAIRS):
                act.wait_ge(sem("nmax1"), g + 1)
                for c in range(CHUNKS + 2):
                    if c < CHUNKS:
                        s = scores[g % 2][:, 512 * c:512 * c + width(c)]
                        A(s, s, ACT.Exp, bias=nmax1[:, g:g + 1], accum_out=sum1[:, g, c:c + 1]).then_inc(sem("exp1"), 1)
                    if c >= 2 and (c - 2) % 2 == 1:
                        turned(g, c - 2)

            act.wait_ge(sem("dn_turned"), 1)
            A(wdn[:, :, :], PS[:, 7, :].rearrange("p (b c) -> p b c", b=FB), ACT.Copy).then_inc(sem("wdn"), 1)
            act.wait_ge(sem("lin1_b"), 1)
            for b in (2, 3):
                A(hT[:, b, :], PS[:, 1, T * (b - 2):T * (b - 1)], ACT.Relu, bias=of("late", "lin1_b", b, b + 1)).then_inc(sem("h_act"), 1)
            act.wait_ge(sem("gate1"), 1)
            for b in range(2):
                A(gT[:, b, :], PS[:, 1, T * b:T * b + T], ACT.Identity, bias=of("late", "in_b", 2 + b, 3 + b)).then_inc(sem("gT"), 1)
            act.wait_ge(sem("gT"), 2)
            A(tanh_g[:], gT[:], ACT.Tanh, scale=0.5).then_inc(sem("tanh_g"), 1)
            act.wait_ge(sem("xc"), 1)
            A(tanh_xc[:], xc[:], ACT.Tanh, scale=0.5).then_inc(sem("tanh_xc"), 1)
            act.wait_ge(sem("dt_low"), 1)
            A(dtT[:], PS[0:N, 2, 0:T], ACT.Identity, scale=0.5, bias=sm("dt_b", N)).then_inc(sem("dtT"), 1)
            act.wait_ge(sem("zneg"), 1)
            A(ez[:], zneg[:], ACT.Exp).then_inc(sem("ez"), 1)
            act.wait_ge(sem("ez"), 1)
            A(lz[:], ez[:], ACT.Ln, bias=1.0).then_inc(sem("lz"), 1)
            for b in range(2):
                act.wait_ge(sem("dA"), b + 1)
                A(decay[:, b, :, 1:T], dA[:, b, :, 1:T], ACT.Exp, scale=-1.0).then_inc(sem("decay"), 1)
            act.wait_ge(sem("beff"), 1)
            act.wait_ge(sem("h6"), 1)
            for b in range(FB):
                A(gl6[:, b, :], PS[:, 0, T * b:T * b + T], ACT.Gelu, bias=beff[:, b:b + 1]).then_inc(sem("gelu"), 1)

        @block.vector
        def _(dve):
            steps = [0]

            def link(ins):
                steps[0] += 1
                ins.then_inc(sem("dve_step"), 1)
                dve.wait_ge(sem("dve_step"), steps[0])

            norms = [0]

            def layer_norm(src, eps=EPS):
                i = norms[0]
                norms[0] += 1
                link(dve.bn_stats(stats[:, 6 * i:6 * i + 6], src))
                link(dve.bn_aggr(mv[:, 2 * i:2 * i + 2], stats[:, 6 * i:6 * i + 6]))
                dve.tensor_scalar(var_eps[:, i:i + 1], mv[:, 2 * i + 1:2 * i + 2], eps, None, ALU.add).then_inc(sem("var_ready"), 1)
                dve.wait_ge(sem("rstd_ready"), i + 1)
                dve.tensor_scalar(nm(i), src, mv[:, 2 * i:2 * i + 1], rstd[:, i:i + 1], ALU.subtract, ALU.mult).then_inc(sem("normed"), 1)

            dve.memset(scoresA[T:D, 3072:3200], 0.0).then_inc(sem("scores_tail"), 1)
            dve.memset(cmax[T:D, 6:7], -3.0e38).then_inc(sem("cmax_tail"), 1)
            dve.memset(lsum[T:D, 6:7], 0.0).then_inc(sem("lsum_tail"), 1)
            dve.memset(v_halves[:], 0.0).then_inc(sem("v_zero"), 1)
            dve.memset(pad[:, :, 0:3], 0.0).then_inc(sem("pad_zero"), 1)

            dve.wait_ge(sem("x_in"), 16)
            layer_norm(x[:])
            dve.wait_ge(sem("norm_turned"), 1)
            dve.tensor_copy(xnT[:], PS[:, 7, 0:T].unsqueeze(1).to_broadcast([D, 2, T])).then_inc(sem("norm_columns"), 1)
            dve.wait_ge(sem("qW"), 1)
            dve.tensor_copy(qWT[:], PS[:, 7, 64:64 + T]).then_inc(sem("qWT"), 1)
            link(dve.tensor_copy(cp[:], PS[:, 7, 128:129]))
            for j in range(7):
                P, w = (D, 512) if j < 6 else (T, D)
                dve.wait_ge(sem("s0"), j + 1)
                dve.tensor_scalar(scoresA[0:P, 512 * j:512 * j + w], PS[0:P, S_BANKS[j % 2], 0:w], cp[0:P], None,
                                  ALU.add, ALU.max, accum_out=cmax[0:P, j:j + 1]).then_inc(sem("s0_out"), 1)
            dve.wait_ge(sem("s0_out"), 7)
            dve.wait_ge(sem("cmax_tail"), 1)
            dve.tensor_reduce(nmax0[:], cmax[:, 0:7], X, ALU.max, negate=True).then_inc(sem("nmax0"), 1)
            dve.wait_ge(sem("nmax_other"), 1)
            dve.tensor_tensor(nmaxM[:], PS[:, 7, 130:131], nmax0[:], ALU.min).then_inc(sem("nmaxM"), 1)
            for c in range(7):
                w = 512 if c < 6 else D
                dve.wait_ge(sem("turned0"), c + 1)
                if c >= 3:
                    dve.wait_ge(sem("pv0"), c - 2)
                dve.tensor_copy(pT[:, c % 3, 0:w], PS[:, T_BANKS[c % 2], 0:w]).then_inc(sem("pT0"), 1)
            dve.wait_ge(sem("exp0"), 7)
            dve.wait_ge(sem("lsum_tail"), 1)
            link(dve.reduce_sum(l0[:], lsum[:, 0:7], X))
            dve.wait_ge(sem("w0"), 1)
            dve.tensor_tensor(wl[:], w0[:], l0[:], ALU.mult).then_inc(sem("wl"), 1)
            dve.wait_ge(sem("l_both"), 1)
            link(dve.reciprocal(rL[:], PS[:, 7, 132:133]))
            link(dve.tensor_tensor(fac[:], w0[:], rL[:], ALU.mult))
            dve.wait_ge(sem("pv0"), 7)
            dve.tensor_scalar(o_sc[:], PS[:, 4, 0:D], fac[:], None, ALU.mult).then_inc(sem("o_sc"), 1)
            dve.wait_ge(sem("att"), 1)
            dve.tensor_copy(attT[:], PS[:, 7, 192:192 + T]).then_inc(sem("attT"), 1)
            dve.wait_ge(sem("xattn"), 1)
            link(dve.scalar_tensor_tensor(x1[:], PS[0:T, 3, 256:256 + D], 0.0, x[:], ALU.max, ALU.add))

            layer_norm(x1[:])
            dve.wait_ge(sem("norm_turned"), 2)
            dve.tensor_copy(xn1T[:], PS[:, 4, 0:T].unsqueeze(1).to_broadcast([D, 2, T])).then_inc(sem("norm_columns"), 1)
            dve.wait_ge(sem("tanh_qk"), 1)
            dve.scalar_tensor_tensor(s2[:], tanh_qk[:], 1.0, PS[:, 0, 0:2 * T].rearrange("p (a n) -> p a n", a=2), ALU.add, ALU.mult).then_inc(sem("s2"), 1)
            dve.wait_ge(sem("s2"), 1)
            link(dve.tensor_tensor(s2cos[:], s2[:], of("mats", "cosT").unsqueeze(1).to_broadcast([D, 2, T]), ALU.mult))
            dve.wait_ge(sem("rotated"), 1)
            link(dve.tensor_tensor(s2sin[:], PS[:, 3, 0:2 * T].rearrange("p (a n) -> p a n", a=2), of("mats", "sinT").unsqueeze(1).to_broadcast([D, 2, T]), ALU.mult))
            link(dve.tensor_tensor(qk[:], s2cos[:], s2sin[:], ALU.add))
            for h in range(2):
                dve.tensor_tensor(q_heads[:, 8 * h:8 * h + 8, :], qk[:, 0:1, :].to_broadcast([D, 8, T]),
                                  of("mats", "head", 8 * h, 8 * h + 8).unsqueeze(2).to_broadcast([D, 8, T]), ALU.mult).then_inc(sem("q_heads"), 1)
            dve.wait_ge(sem("energy"), 1)
            dve.tensor_tensor(energy[:, :, :], PS[:, 0, :].rearrange("p (h n) -> p h n", h=8),
                              of("mats", "causal").unsqueeze(1).to_broadcast([D, 8, T]), ALU.mult).then_inc(sem("masked"), 1)
            dve.wait_ge(sem("tanh_gate"), 1)
            dve.wait_ge(sem("lin_att"), 1)
            link(dve.scalar_tensor_tensor(gated[:], tanh_gate[:], 1.0, PS[0:T, 1, 128:128 + D], ALU.add, ALU.mult))
            layer_norm(gated[:])
            dve.wait_ge(sem("norm_turned"), 3)
            dve.tensor_scalar(yT[:], PS[:, 4, 64:64 + T], of("mats", "ln_w"), of("mats", "ln_b"), ALU.mult, ALU.add).then_inc(sem("norm_columns"), 1)
            dve.wait_ge(sem("attn_out"), 1)
            dve.tensor_tensor(x2[:], PS[0:T, 4, 128:128 + D], x1[:], ALU.add).then_inc(sem("x2"), 1)
            dve.wait_ge(sem("x2"), 1)

            layer_norm(x2[:])
            dve.wait_ge(sem("normed"), 4)
            layer_norm(nm(3))
            dve.wait_ge(sem("normed"), 5)
            link(dve.tensor_tensor(zg[:], nm(4), wd("ffn_g"), ALU.mult))
            dve.wait_ge(sem("x2b"), 1)
            link(dve.tensor_tensor(x3[:], zg[:], x2b[:], ALU.add))

            layer_norm(x3[:])
            dve.wait_ge(sem("norm_turned"), 4)
            dve.tensor_copy(tgtT[:], PS[:, 0, 0:T]).then_inc(sem("norm_columns"), 1)
            dve.wait_ge(sem("sa"), 1)
            link(dve.tensor_tensor(t1[:], PS[0:T, 2, 128:128 + D], nm(5), ALU.add))
            layer_norm(t1[:])
            dve.wait_ge(sem("norm_turned"), 5)
            dve.tensor_scalar(z6T[:], PS[:, 0, 64:64 + T], of("mats", "ln1_g"), of("mats", "ln1_b"), ALU.mult, ALU.add).then_inc(sem("norm_columns"), 1)
            dve.wait_ge(sem("q1"), 1)
            for p in range(2):
                dve.tensor_scalar(q_wide[:, p, :], PS[:, 4, 256:256 + T], of("mats", "bq"), of("mats", "head1", p, p + 1), ALU.add, ALU.mult).then_inc(sem("q_wide"), 1)
            link(dve.tensor_scalar(q_all[:], PS[:, 4, 256:256 + T], of("mats", "bq"), None, ALU.add))
            dve.tensor_tensor(q_wide[:, 2:H1, :], q_all[:].unsqueeze(1).to_broadcast([D, H1 - 2, T]),
                              of("mats", "head1", 2, H1).unsqueeze(2).to_broadcast([D, H1 - 2, T]), ALU.mult).then_inc(sem("q_wide"), 1)
            for h in range(2):
                dve.wait_ge(sem("qk1"), h + 1)
                cols = slice(0, 2) if h == 0 else slice(2, H1)
                dve.tensor_copy(qk1[:, cols, :], PS[:, 2 + h, 0:(2 if h == 0 else 6) * T].rearrange("p (h n) -> p h n", n=T)).then_inc(sem("qk1_out"), 1)
                dve.tensor_copy(cp1[:, 0:1] if h == 0 else cp1[:, 1:PAIRS], PS[:, 2 + h, 480:481] if h == 0 else PS[:, 2 + h, 481:484]).then_inc(sem("cp1"), 1)
            dve.wait_ge(sem("cp1"), 2)

            def turned(g, c):
                n = g * CHUNKS + c
                dve.wait_ge(sem("turned"), n + 1)
                if n >= 4:
                    dve.wait_ge(sem("pv"), n - 3)
                dve.tensor_copy(pT[:, n % 4, 0:width(c)], PS[:, T_BANKS[n % 2], 0:width(c)]).then_inc(sem("pT_dve"), 1)

            def finish(g):
                dve.wait_ge(sem("exp1"), (g + 1) * CHUNKS)
                link(dve.reduce_sum(l1[:, g:g + 1], sum1[:, g, 0:CHUNKS], X))
                link(dve.reciprocal(rl1[:, g:g + 1], l1[:, g:g + 1]))
                dve.wait_ge(sem("pv"), (g + 1) * CHUNKS)
                if g >= 2:
                    dve.wait_ge(sem("heads"), g - 1)
                dve.tensor_copy(oS[:, g % 2, :], PS[:, O_BANKS[g % 2], 0:D]).then_inc(sem("oS"), 1)
                dve.wait_ge(sem("heads"), g + 1)
                for p in range(2):
                    P = slice(T * p, T * p + T)
                    dve.tensor_scalar(ca[:, 32 * g + HD1 * p:32 * g + HD1 * p + HD1], PS[P, 5, HD1 * p:HD1 * p + HD1],
                                      rl1[P, g:g + 1], None, ALU.mult).then_inc(sem("ca"), 1)

            for g in range(PAIRS + 1):
                for c in range(CHUNKS + 1):
                    if g < PAIRS and c < CHUNKS:
                        n = g * CHUNKS + c
                        dve.wait_ge(sem("s1"), n + 1)
                        if g >= 2 and c == 0:
                            dve.wait_ge(sem("turned"), (g - 1) * CHUNKS)
                        dve.tensor_scalar(scores[g % 2][:, 512 * c:512 * c + width(c)], PS[:, S_BANKS[n % 2], 0:width(c)], cp1[:, g:g + 1], None,
                                          ALU.add, ALU.max, accum_out=max1[:, g, c:c + 1]).then_inc(sem("s1_out"), 1)
                    if g >= 1 and c % 2 == 1:
                        turned(g - 1, c - 1)
                if g < PAIRS:
                    dve.wait_ge(sem("s1_out"), (g + 1) * CHUNKS)
                    dve.tensor_reduce(nmax1[:, g:g + 1], max1[:, g, 0:CHUNKS], X, ALU.max, negate=True).then_inc(sem("nmax1"), 1)
                if g >= 1:
                    finish(g - 1)
            dve.wait_ge(sem("caT"), 1)
            dve.tensor_scalar(caT[:], PS[:, 0, 0:T], of("mats", "bv"), None, ALU.add).then_inc(sem("caT_out"), 1)
            dve.wait_ge(sem("mha"), 1)
            dve.wait_ge(sem("x_q"), 1)
            link(dve.tensor_tensor(t2[:], PS[0:T, 1, 256:256 + D], x_q[:], ALU.add))
            layer_norm(t2[:])
            dve.wait_ge(sem("late_in"), 16)
            dve.wait_ge(sem("b_columns"), 1)
            dve.tensor_tensor(beff[:], PS[:, 6, 0:FB], of("late", "up_bias"), ALU.add).then_inc(sem("beff"), 1)
            dve.wait_ge(sem("norm_turned"), 6)
            dve.tensor_scalar(z7T[:], PS[:, 2, 0:T], of("mats", "ln2_g"), of("mats", "ln2_b"), ALU.mult, ALU.add).then_inc(sem("norm_columns"), 1)
            dve.wait_ge(sem("lin1_a"), 1)
            for b in (0, 1):
                dve.tensor_scalar(hT[:, b, :], PS[:, 0, T * b:T * b + T], of("late", "lin1_b", b, b + 1), 0.0, ALU.add, ALU.max).then_inc(sem("h_dve"), 1)
            dve.wait_ge(sem("ff"), 1)
            dve.wait_ge(sem("x7"), 1)
            link(dve.tensor_tensor(t3[:], PS[0:T, 2, 128:128 + D], x7[:], ALU.add))
            layer_norm(t3[:])
            dve.wait_ge(sem("normed"), 9)
            link(dve.tensor_tensor(z8g[:], nm(8), wd("ln3_g"), ALU.mult))
            dve.wait_ge(sem("x3b"), 1)
            link(dve.tensor_tensor(x4[:], z8g[:], x3b[:], ALU.add))

            layer_norm(x4[:])
            dve.wait_ge(sem("normed"), 10)
            link(dve.scalar_tensor_tensor(sq[:], nm(9), 1.0, nm(9), ALU.mult, ALU.mult, accum_out=msum[:]))
            dve.tensor_scalar(var_eps[:, 10:11], msum[:], 1.0 / D, RMS_EPS, ALU.mult, ALU.add).then_inc(sem("var_ready"), 1)
            norms[0] += 1
            dve.wait_ge(sem("rstd_ready"), 11)
            dve.tensor_scalar(rms_h[:], nm(9), rstd[:, 10:11], None, ALU.mult).then_inc(sem("rms_h"), 1)
            dve.wait_ge(sem("rmsT"), 1)
            dve.tensor_scalar(hmT[:], PS[:, 2, 256:256 + T], of("late", "rms_w"), None, ALU.mult).then_inc(sem("hmT"), 1)
            dve.wait_ge(sem("x_in1"), 1)
            dve.wait_ge(sem("pad_zero"), 1)
            for b in range(2):
                dve.tensor_scalar(pad[:, b, 3:3 + T], PS[:, 0, T * b:T * b + T], of("late", "in_b", b, b + 1), None, ALU.add).then_inc(sem("pad"), 1)
            dve.wait_ge(sem("pad"), 2)
            for k in range(4):
                for b in range(2):
                    w = of("late", "conv_w", 4 * b + k, 4 * b + k + 1)
                    if k == 0:
                        ins = dve.tensor_scalar(xc[:, b, :], pad[:, b, 0:T], w, of("late", "conv_b", b, b + 1), ALU.mult, ALU.add)
                    else:
                        ins = dve.scalar_tensor_tensor(xc[:, b, :], pad[:, b, k:k + T], w, xc[:, b, :], ALU.mult, ALU.add)
                    ins.then_inc(sem("taps"), 1)
                dve.wait_ge(sem("taps"), 2 * k + 2)
            dve.sem_inc(sem("xc"), 1)
            dve.wait_ge(sem("tanh_g"), 1)
            dve.scalar_tensor_tensor(gs2[:], tanh_g[:], 1.0, gT[:], ALU.add, ALU.mult).then_inc(sem("gs2"), 1)
            dve.wait_ge(sem("tanh_xc"), 1)
            dve.scalar_tensor_tensor(xs2[:], tanh_xc[:], 1.0, xc[:], ALU.add, ALU.mult).then_inc(sem("xs2"), 1)
            dve.memset(decay[:, :, :, 0:1], 0.0).then_inc(sem("decay_zero"), 1)
            dve.wait_ge(sem("bc"), 1)
            link(dve.tensor_scalar(bcT[:], PS[0:2 * N, 3, 0:T], 0.5, sm("bc_b", 2 * N), ALU.mult, ALU.add))
            dve.tensor_tensor(bc_own[:, :, :], bcT[:].unsqueeze(1).to_broadcast([2 * N, N, T]),
                              sm("own", 2 * N).unsqueeze(2).to_broadcast([2 * N, N, T]), ALU.mult).then_inc(sem("bc_own"), 1)
            dve.wait_ge(sem("dt"), 1)
            for b in range(2):
                dve.tensor_scalar(z[:, b, :], PS[:, 4, T * b:T * b + T], of("late", "dup_b", b, b + 1), None, ALU.add).then_inc(sem("z"), 1)
            dve.wait_ge(sem("z"), 2)
            dve.scalar_tensor_tensor(zneg[:], z[:], -1.0, z[:], ALU.mult, ALU.min).then_inc(sem("zneg"), 1)
            link(dve.tensor_scalar(zpos[:], z[:], 0.0, None, ALU.max))
            dve.wait_ge(sem("xs2"), 1)
            dve.wait_ge(sem("lz"), 1)
            link(dve.tensor_tensor(delta[:], zpos[:], lz[:], ALU.add))
            dve.wait_ge(sem("expA"), 1)
            for b in range(2):
                dve.tensor_tensor(dA[:, b], delta[:, b:b + 1, :].to_broadcast([D, N, T]), expA[:, b, :].unsqueeze(2).to_broadcast([D, N, T]), ALU.mult).then_inc(sem("dA"), 1)
            link(dve.scalar_tensor_tensor(dx[:], delta[:], 0.5, xs2[:], ALU.mult, ALU.mult))
            for b in range(2):
                dve.wait_ge(sem("b_wide"), 1)
                link(dve.tensor_tensor(Bx[:, b], PS[:, 0:2, :].rearrange("p k (n t) -> p (k n) t", t=T), dx[:, b:b + 1, :].to_broadcast([D, N, T]), ALU.mult))
                dve.wait_ge(sem("decay"), b + 1)
                dve.wait_ge(sem("decay_zero"), 1)
                flat = [a[:, b].rearrange("p n t -> p (n t)") for a in (hs, decay, Bx)]
                link(dve.tensor_tensor_scan(flat[0], flat[1], flat[2], 0.0, ALU.mult, ALU.add))
                dve.wait_ge(sem("c_wide"), 1)
                link(dve.tensor_tensor(hC[:, b], PS[:, 2:4, :].rearrange("p k (n t) -> p (k n) t", t=T), hs[:, b], ALU.mult))
                link(dve.reduce_sum(y[:, b, :], hC[:, b].rearrange("p n t -> p t n"), X))
                dve.wait_ge(sem("gs2"), 1)
                dve.scalar_tensor_tensor(yg[:, b, :], y[:, b, :], 0.5, gs2[:, b, :], ALU.mult, ALU.mult).then_inc(sem("yg"), 1)
            dve.wait_ge(sem("ssm"), 1)
            dve.wait_ge(sem("xr"), 1)
            link(dve.tensor_tensor(x5[:], PS[0:T, 4, 256:256 + D], xr[:], ALU.add))

            layer_norm(x5[:])
            dve.wait_ge(sem("norm_turned"), 7)
            dve.tensor_copy(x6T[:], PS[:, 1, 0:T]).then_inc(sem("norm_columns"), 1)
            dve.wait_ge(sem("ff6"), 1)
            dve.tensor_tensor(x6[:], PS[0:T, 2, 128:128 + D], x5[:], ALU.add).then_inc(sem("x6"), 1)

        @block.tensor
        def _(pe):
            mm = pe.matmul

            def turn(out_, in_):
                return pe.transpose(out_, in_, ident[0:T, 0:T])

            fills = iter(range(CHUNKS))

            def fill(n=1):
                for _ in range(n):
                    c = next(fills)
                    if c >= 2:
                        pe.wait_ge(sem("fill_out"), c - 1)
                    if c == 0:
                        pe.wait_ge(sem("kv_in"), 16)
                        for j in range(4):
                            pe.wait_ge(sem(f"ctxT_in{j}"), 32 if j < 3 else 16)
                    for t in range(width(c) // D):
                        tile = CHUNK * c + t
                        ins = mm(PS[:, F_BANKS[c % 2], D * t:D * t + D], ctxT[:, D * tile:D * tile + D], of("kv", "WvT"), start=True, stop=True)
                    ins.then_inc(sem("fill"), 1)

            pe.wait_ge(sem("first_in"), 16)
            pe.wait_ge(sem("normed"), 1)
            turn(PS[:, 7, 0:T], nm(0)).then_inc(sem("norm_turned"), 1)
            pe.wait_ge(sem("norm_columns"), 1)
            mm(PS[:, 7, 64:64 + T], of("first", "W0"), xnT[:, 0, :], start=True, stop=True)
            mm(PS[:, 7, 128:129], xnT[:].rearrange("p a n -> p (a n)"), of("first", "b0"), start=True, stop=True).then_inc(sem("qW"), 1)
            pe.wait_ge(sem("qWT"), 1)
            for j in range(7):
                pe.wait_ge(sem(f"ctxT_in{j // 2}"), 32 if j < 6 else 16)
                if j >= 2:
                    pe.wait_ge(sem("s0_out"), j - 1)
                bank = PS[:, S_BANKS[j % 2], :]
                if j < 6:
                    a = HALF0 * D + 512 * j
                    mm(bank[0:T, :], qWT[:], ctxT[:, 512 * j:512 * j + 512], start=True, stop=True)
                    mm(bank[T:D, :], qWT[:], ctxT[:, a:a + 512], start=True, stop=True).then_inc(sem("s0"), 1)
                else:
                    mm(bank[0:T, 0:D], qWT[:], ctxT[:, 512 * j:512 * j + D], start=True, stop=True).then_inc(sem("s0"), 1)
            pe.wait_ge(sem("nmax0"), 1)
            mm(PS[:, 7, 130:131], of("first", "swap"), nmax0[:], start=True, stop=True).then_inc(sem("nmax_other"), 1)
            pe.wait_ge(sem("scores_tail"), 1)
            for c in range(8):
                if c < 7:
                    pe.wait_ge(sem("exp0"), c + 1)
                    if c >= 2:
                        pe.wait_ge(sem("pT0"), c - 1)
                    for t in range(CHUNK * c, min(CHUNK * c + CHUNK, HALF0)):
                        ins = pe.transpose(PS[:, T_BANKS[c % 2], (t % CHUNK) * D:(t % CHUNK + 1) * D], scoresA[:, D * t:D * t + D], ident)
                    ins.then_inc(sem("turned0"), 1)
                if c >= 1:
                    pe.wait_ge(sem("pT0"), c)
                    j = (c - 1) // 2
                    pe.wait_ge(sem(f"ctxN_in{j}"), 32 if j < 3 else 16)
                    for t in range(CHUNK * (c - 1), min(CHUNK * c, HALF0)):
                        w = pT[:, (c - 1) % 3, (t % CHUNK) * D:(t % CHUNK + 1) * D]
                        ins = mm(PS[0:T, 4, 0:D], w[:, 0:T], ctxN[:, t, :], start=(t == 0), stop=(t == HALF0 - 1))
                        if t < HALF1:
                            ins = mm(PS[T:D, 4, 0:D], w[:, T:D], ctxN[:, HALF0 + t, :], start=(t == 0), stop=(t == HALF1 - 1))
                    ins.then_inc(sem("pv0"), 1)
            pe.wait_ge(sem("wl"), 1)
            mm(PS[:, 7, 132:133], of("first", "pair_sum"), wl[:], start=True, stop=True).then_inc(sem("l_both"), 1)
            pe.wait_ge(sem("o_sc"), 1)
            mm(PS[:, 7, 192:192 + T], o_sc[:], of("first", "stack"), start=True, stop=True).then_inc(sem("att"), 1)
            pe.wait_ge(sem("rows_in"), 16)
            pe.wait_ge(sem("ones_ready"), 1)
            mm(PS[0:T, 3, 256:256 + D], ones[:], row("b0"), start=True, stop=False)
            pe.wait_ge(sem("attT"), 1)
            mm(PS[0:T, 3, 256:256 + D], attT[:], of("first", "W0T"), start=False, stop=True).then_inc(sem("xattn"), 1)
            fill(1)

            pe.wait_ge(sem("mats_in"), 16)
            pe.wait_ge(sem("normed"), 2)
            turn(PS[:, 4, 0:T], nm(1)).then_inc(sem("norm_turned"), 1)
            pe.wait_ge(sem("norm_columns"), 2)
            mm(PS[:, 0, 0:T], of("mats", "Wq"), xn1T[:, 0, :], start=True, stop=True)
            mm(PS[:, 0, T:2 * T], of("mats", "Wk"), xn1T[:, 0, :], start=True, stop=True).then_inc(sem("qkT"), 1)
            mm(PS[0:HD0, 1, 0:T], of("mats", "Wg1"), xn1T[:, 0, :], start=True, stop=True).then_inc(sem("g1"), 1)
            mm(PS[:, 2, 0:D], xn1T[:].rearrange("p a n -> p (a n)"), of("mats", "Wv"), start=True, stop=True).then_inc(sem("v0"), 1)
            pe.wait_ge(sem("s2"), 1)
            mm(PS[:, 3, 0:2 * T], of("mats", "rotT"), s2[:].rearrange("p a n -> p (a n)"), start=True, stop=True).then_inc(sem("rotated"), 1)
            pe.wait_ge(sem("small_in"), 16)
            pe.wait_ge(sem("g1T"), 1)
            mm(PS[0:T, 7, 256:256 + D], g1T[:], sm("Wg2", HD0), start=True, stop=True).then_inc(sem("gate"), 1)
            fill(1)
            pe.wait_ge(sem("q_heads"), 1)
            mm(PS[0:T, 0, :], qk[:, 1, :], q_heads[:, 0:8, :].rearrange("p h n -> p (h n)"), start=True, stop=True)
            pe.wait_ge(sem("q_heads"), 2)
            mm(PS[T:D, 0, :], qk[:, 1, :], q_heads[:, 8:16, :].rearrange("p h n -> p (h n)"), start=True, stop=True).then_inc(sem("energy"), 1)
            fill(1)
            pe.wait_ge(sem("v_halves"), 2)
            pe.wait_ge(sem("masked"), 1)
            v4 = v_halves[:].rearrange("p a (h d) -> p a h d", d=HD0)
            o4 = PS[0:T, 1, 128:128 + D].rearrange("p (a h d) -> p a h d", a=2, d=HD0)
            for h in range(8):
                ins = mm(o4[:, :, h, :], energy[:, h, :], v4[:, :, h, :], start=True, stop=True)
            ins.then_inc(sem("lin_att"), 1)
            fill(2)
            pe.wait_ge(sem("normed"), 3)
            turn(PS[:, 4, 64:64 + T], nm(2)).then_inc(sem("norm_turned"), 1)
            pe.wait_ge(sem("norm_columns"), 3)
            mm(PS[0:T, 4, 128:128 + D], yT[:], of("mats", "Wo"), start=True, stop=True).then_inc(sem("attn_out"), 1)
            fill(4)

            pe.wait_ge(sem("normed"), 6)
            turn(PS[:, 0, 0:T], nm(5)).then_inc(sem("norm_turned"), 1)
            pe.wait_ge(sem("norm_columns"), 4)
            mm(PS[:, 1, 0:T], of("mats", "saWvT"), tgtT[:], start=True, stop=True).then_inc(sem("v1"), 1)
            mm(PS[0:T, 2, 128:128 + D], ones[:], row("sa_out_b"), start=True, stop=False)
            pe.wait_ge(sem("vT"), 1)
            mm(PS[0:T, 2, 128:128 + D], vT[:], of("mats", "sa_outT"), start=False, stop=True).then_inc(sem("sa"), 1)
            fill(4)
            pe.wait_ge(sem("normed"), 7)
            turn(PS[:, 0, 64:64 + T], nm(6)).then_inc(sem("norm_turned"), 1)
            pe.wait_ge(sem("norm_columns"), 5)
            mm(PS[:, 4, 256:256 + T], of("mats", "WqT"), z6T[:], start=True, stop=True).then_inc(sem("q1"), 1)

            qw = q_wide[:].rearrange("p h n -> p (h n)")
            pe.wait_ge(sem("q_wide"), 2)
            mm(PS[:, 2, 0:2 * T], of("mats", "Wk1"), qw[:, 0:2 * T], start=True, stop=True)
            mm(PS[:, 2, 480:481], qw[:, 0:2 * T], of("mats", "bk"), start=True, stop=True).then_inc(sem("qk1"), 1)
            pe.wait_ge(sem("q_wide"), 3)
            mm(PS[:, 3, 0:6 * T], of("mats", "Wk1"), qw[:, 2 * T:], start=True, stop=True)
            for g in range(1, PAIRS):
                ins = mm(PS[:, 3, 480 + g:481 + g], qw[:, 2 * T * g:2 * T * g + 2 * T], of("mats", "bk"), start=True, stop=True)
            ins.then_inc(sem("qk1"), 1)
            pe.wait_ge(sem("qk1_out"), 1)

            def score(g, c):
                n = g * CHUNKS + c
                if n == CHUNKS:
                    pe.wait_ge(sem("qk1_out"), 2)
                if n >= 2:
                    pe.wait_ge(sem("s1_out"), n - 1)
                mm(PS[:, S_BANKS[n % 2], 0:width(c)], qk1[:, 2 * g:2 * g + 2, :].rearrange("p a n -> p (a n)"), ctxT[:, 512 * c:512 * c + width(c)],
                   start=True, stop=True).then_inc(sem("s1"), 1)

            def turn_weights(g, c):
                n = g * CHUNKS + c
                pe.wait_ge(sem("exp1"), n + 1)
                if n >= 2:
                    m = n - 2
                    even, odd = taken(m)
                    if m % CHUNKS % 2 == 0:
                        pe.wait_ge(sem("pT_dve"), even)
                    else:
                        pe.wait_ge(sem("pT_act"), odd)
                for t in range(width(c) // D):
                    a = 512 * c + D * t
                    ins = pe.transpose(PS[:, T_BANKS[n % 2], D * t:D * t + D], scores[g % 2][:, a:a + D], ident)
                ins.then_inc(sem("turned"), 1)

            def taken(n):
                g, c = divmod(n, CHUNKS)
                return g * 7 + c // 2 + 1, g * 6 + (c + 1) // 2

            def apply_weights(g, c):
                n = g * CHUNKS + c
                even, odd = taken(n)
                if c % 2 == 0:
                    pe.wait_ge(sem("pT_dve"), even)
                else:
                    pe.wait_ge(sem("pT_act"), odd)
                if g >= 2 and c == 0:
                    pe.wait_ge(sem("oS"), g - 1)
                for t in range(width(c) // D):
                    tile = CHUNK * c + t
                    ins = mm(PS[32 * t:32 * t + 32, O_BANKS[g % 2], 0:D], V[:, tile, 32 * g:32 * g + 32], pT[:, n % 4, D * t:D * t + D],
                             start=(c == 0), stop=(tile + CHUNK >= TILES))
                ins.then_inc(sem("pv"), 1)

            def heads(g):
                pe.wait_ge(sem("oS"), g + 1)
                if g:
                    pe.wait_ge(sem("ca"), 2 * g)
                mm(PS[:, 5, 0:32], oS[:, g % 2, :], of("mats", "sumsel"), start=True, stop=True).then_inc(sem("heads"), 1)

            pe.wait_ge(sem("b_lo"), 1)
            pe.transpose(PS[0:32, 7, 384:400], b_lo[LO % 2], ident[0:16, 0:16]).then_inc(sem("b_turned"), 1)
            pe.wait_ge(sem("fill_out"), CHUNKS)
            for g in range(PAIRS + 1):
                for c in range(CHUNKS + 2):
                    if g < PAIRS and c < CHUNKS:
                        score(g, c)
                    if g >= 1 and c < CHUNKS:
                        turn_weights(g - 1, c)
                    if g >= 1 and c >= 2:
                        apply_weights(g - 1, c - 2)
                if g >= 1:
                    heads(g - 1)
            pe.wait_ge(sem("ca"), 2 * PAIRS)
            turn(PS[:, 0, 0:T], ca[:]).then_inc(sem("caT"), 1)
            mm(PS[0:T, 1, 256:256 + D], ones[:], row("mha_out_b"), start=True, stop=False)
            pe.wait_ge(sem("caT_out"), 1)
            mm(PS[0:T, 1, 256:256 + D], caT[:], of("mats", "mha_outT"), start=False, stop=True).then_inc(sem("mha"), 1)
            pe.wait_ge(sem("b_up"), 1)
            b_up = b_hi[(STAGES - LO) % 2]
            for q in range(4):
                ins = mm(PS[32 * q:32 * q + 32, 6, 0:FB], ident[0:32, 0:32], b_up.rearrange("p (b q) -> p b q", q=4)[:, :, q], start=True, stop=True)
            ins.then_inc(sem("b_columns"), 1)
            pe.wait_ge(sem("dn_done"), 1)
            for b in range(FB):
                ins = pe.transpose(PS[:, 7, D * b:D * b + D], hidden["dn"][STAGES % 2][:, D * b:D * b + D], ident)
            ins.then_inc(sem("dn_turned"), 1)
            pe.wait_ge(sem("normed"), 8)
            turn(PS[:, 2, 0:T], nm(7)).then_inc(sem("norm_turned"), 1)
            pe.wait_ge(sem("late_in"), 16)
            pe.wait_ge(sem("norm_columns"), 6)
            for b in (2, 3, 0, 1):
                ins = mm(PS[:, b // 2, T * (b % 2):T * (b % 2) + T], of("late", "lin1T", D * b, D * b + D), z7T[:], start=True, stop=True)
                if b % 2:
                    ins.then_inc(sem("lin1_b" if b == 3 else "lin1_a"), 1)
            mm(PS[0:T, 2, 128:128 + D], ones[:], row("lin2_b"), start=True, stop=False)
            pe.wait_ge(sem("h_act"), 2)
            pe.wait_ge(sem("h_dve"), 2)
            for b in range(FB):
                ins = mm(PS[0:T, 2, 128:128 + D], hT[:, b, :], of("late", "lin2T", D * b, D * b + D), start=False, stop=(b == FB - 1))
            ins.then_inc(sem("ff"), 1)
            pe.wait_ge(sem("rms_h"), 1)
            turn(PS[:, 2, 256:256 + T], rms_h[:]).then_inc(sem("rmsT"), 1)
            pe.wait_ge(sem("hmT"), 1)
            for b in range(4):
                ins = mm(PS[:, b // 2, T * (b % 2):T * (b % 2) + T], of("late", "in_W", D * b, D * b + D), hmT[:], start=True, stop=True)
                if b % 2:
                    ins.then_inc(sem("x_in1" if b == 1 else "gate1"), 1)
            pe.wait_ge(sem("xs2"), 1)
            dbc = of("late", "dbc_W").rearrange("p (b j) -> p b j", b=2)
            for b in range(2):
                ins = mm(PS[0:N, 2, 0:T], dbc[:, b, 0:N], xs2[:, b, :], start=(b == 0), stop=(b == 1))
            ins.then_inc(sem("dt_low"), 1)
            for b in range(2):
                ins = mm(PS[0:2 * N, 3, 0:T], dbc[:, b, N:3 * N], xs2[:, b, :], start=(b == 0), stop=(b == 1))
            ins.then_inc(sem("bc"), 1)
            pe.wait_ge(sem("dtT"), 1)
            for b in range(2):
                ins = mm(PS[:, 4, T * b:T * b + T], sm("dup_W", N)[:, D * b:D * b + D], dtT[:], start=True, stop=True)
            ins.then_inc(sem("dt"), 1)
            pe.wait_ge(sem("bc_own"), 1)
            own = bc_own.rearrange("p n t -> p (n t)")
            for name, bank, done in (("onesB", 0, "b_wide"), ("onesC", 2, "c_wide")):
                for h in range(2):
                    ins = mm(PS[:, bank + h, :], sm(name, 2 * N), own[:, 512 * h:512 * h + 512], start=True, stop=True)
                ins.then_inc(sem(done), 1)
            pe.wait_ge(sem("z"), 2)
            mm(PS[0:T, 4, 256:256 + D], ones[:], row("out_b"), start=True, stop=False)
            for b in range(2):
                pe.wait_ge(sem("yg"), b + 1)
                ins = mm(PS[0:T, 4, 256:256 + D], yg[:, b, :], of("late", "out_W", D * b, D * b + D), start=False, stop=(b == 1))
            ins.then_inc(sem("ssm"), 1)

            pe.wait_ge(sem("normed"), 11)
            turn(PS[:, 1, 0:T], nm(11)).then_inc(sem("norm_turned"), 1)
            mm(PS[0:T, 2, 128:128 + D], ones[:], row("b_con"), start=True, stop=False)
            mm(PS[0:T, 2, 128:128 + D], ones[:], row("down_bias"), start=False, stop=False)
            pe.wait_ge(sem("up_done"), 1)
            pe.wait_ge(sem("norm_columns"), 7)
            for b in range(FB):
                ins = mm(PS[:, 0, T * b:T * b + T], wup[:, D * b:D * b + D], x6T[:], start=True, stop=True)
            ins.then_inc(sem("h6"), 1)
            pe.wait_ge(sem("wdn"), 1)
            for b in range(FB):
                pe.wait_ge(sem("gelu"), b + 1)
                ins = mm(PS[0:T, 2, 128:128 + D], gl6[:, b, :], wdn[:, b, :], start=False, stop=(b == FB - 1))
            ins.then_inc(sem("ff6"), 1)


def shape_constants():
    eye = np.eye(D, dtype=np.float32)
    c = {"ident": eye, "swap": np.roll(eye, T, axis=0)}
    c["pair_sum"] = np.tile(np.eye(T, dtype=np.float32), (2, 2))
    c["stack"] = np.tile(np.eye(T, dtype=np.float32), (2, 1))
    inv = 1.0 / np.float32(10000.0) ** (np.arange(0, HD0, 2, dtype=np.float32) / np.float32(HD0))
    ang = np.arange(T, dtype=np.float32)[:, None] * inv[None, :].astype(np.float32)
    c["cosT"] = np.tile(np.cos(ang).T, (2 * H0, 1))
    c["sinT"] = np.tile(np.sin(ang).T, (2 * H0, 1))
    rot = np.zeros((D, D), np.float32)
    for i in range(D):
        rot[i, i + 4 if i % 8 < 4 else i - 4] = -1.0 if i % 8 < 4 else 1.0
    c["rotT"] = rot.T
    r = np.arange(D)
    c["head"] = (r[:, None] // HD0 == np.arange(H0)[None, :]).astype(np.float32)
    c["causal"] = (r[:, None] % T <= np.arange(T)[None, :]).astype(np.float32) * np.float32(0.125)
    c["head1"] = (r[:, None] // HD1 == np.arange(H1)[None, :]).astype(np.float32) * np.float32(HD1 ** -0.5)
    c["sumsel"] = np.tile(np.eye(32, dtype=np.float32), (4, 1))
    n = np.arange(2 * N)
    c["own"] = (n[:, None] % N == np.arange(N)[None, :]).astype(np.float32)
    c["onesB"] = np.repeat((n[:, None] < N).astype(np.float32), D, axis=1)
    c["onesC"] = np.repeat((n[:, None] >= N).astype(np.float32), D, axis=1)
    return c


def stage_weights(w, turned):
    f = np.arange(FF)
    out = np.empty((STAGES, 2, FF), w.dtype)
    for k in range(STAGES):
        s = 1 << k
        pair, second = (f // (2 * s)) * s + f % s, (f // s) % 2
        out[k, 0] = w[k, pair, second, second]
        i, j = (1 - second, second) if turned else (second, 1 - second)
        out[k, 1] = w[k, pair, i, j]
    return out


def kernel(**inputs):
    import concourse.bacc as bacc
    from concourse.bass_utils import run_bass_kernel_spmd as run

    a = {k: np.asarray(v) for k, v in inputs.items()}
    c = shape_constants()

    def col(v):
        return v.reshape(-1, D).T

    def blocks(w):
        return w.reshape(-1, D, w.shape[1]).transpose(1, 0, 2).reshape(D, -1)

    in_proj, in_proj_b = a["L1_xattn_in_proj_w"], a["L1_xattn_in_proj_b"]
    up_w, dn_w = stage_weights(a["L1_ffn_up_weights"], False), stage_weights(a["L1_ffn_down_weights"], True)
    coef_lo = up_w[:LO].reshape(LO, 2, 16, 32).transpose(2, 0, 1, 3).reshape(16, -1)
    coef_hi = up_w[LO:].reshape(STAGES - LO, 2, 16, 32).transpose(3, 0, 1, 2).reshape(32, -1)
    conv = a["L1_attn_conv_w"]
    values = dict(c)
    values.update({
        "W0": a["L0_xattn_W"], "W0T": a["L0_xattn_W"].T, "b0": col(a["L0_xattn_b"]),
        "Wk1": in_proj[D:2 * D], "WvT": in_proj[2 * D:].T, "bk": col(in_proj_b[D:2 * D]),
        "Wq": a["L0_attn_Wq"], "Wk": a["L0_attn_Wk"], "Wv": a["L0_attn_Wv"], "Wg1": a["L0_attn_Wg1"], "Wo": a["L0_attn_Wo"],
        "ln_w": col(a["L0_attn_ln_w"]), "ln_b": col(a["L0_attn_ln_b"]),
        "saWvT": a["L1_xattn_qkv_w"][2 * D:].T, "sa_bv": col(a["L1_xattn_qkv_b"][2 * D:]), "sa_outT": a["L1_xattn_sa_out_w"].T,
        "ln1_g": col(a["L1_xattn_ln1_g"]), "ln1_b": col(a["L1_xattn_ln1_b"]),
        "WqT": in_proj[:D].T, "bq": col(in_proj_b[:D]), "bv": col(in_proj_b[2 * D:]), "mha_outT": a["L1_xattn_mha_out_w"].T,
        "ln2_g": col(a["L1_xattn_ln2_g"]), "ln2_b": col(a["L1_xattn_ln2_b"]),
        "lin1T": a["L1_xattn_lin1_w"].T, "lin1_b": col(a["L1_xattn_lin1_b"]), "lin2T": blocks(a["L1_xattn_lin2_w"].T),
        "rms_w": col(a["L1_attn_rms_w"]), "in_W": a["L1_attn_in_W"], "in_b": col(a["L1_attn_in_b"]),
        "conv_w": blocks(conv), "conv_b": col(a["L1_attn_conv_b"]), "A_log": blocks(a["L1_attn_A_log"]),
        "dbc_W": blocks(a["L1_attn_dbc_W"]), "dup_b": col(a["L1_attn_dup_b"]), "out_W": blocks(a["L1_attn_out_W"]),
        "up_bias": col(a["L1_ffn_up_bias"]),
        "exp": a["L1_ffn_W_exp"], "conT": a["L1_ffn_W_con"].T,
    })
    small_at, small_w = offsets(SMALL)
    small = np.zeros((32, small_w), np.float32)
    dbc_b = a["L1_attn_dbc_b"][:, None]
    for name, v in (("Wg2", a["L0_attn_Wg2"]), ("dup_W", a["L1_attn_dup_W"]), ("dt_b", dbc_b[:N]), ("bc_b", dbc_b[N:]),
                    ("own", c["own"]), ("onesB", c["onesB"]), ("onesC", c["onesC"]),
                    ("b_exp", a["L1_ffn_b_exp"].reshape(16, 32)), ("coef_lo", coef_lo), ("coef_hi", coef_hi)):
        small[0:v.shape[0], small_at[name][0]:small_at[name][1]] = v
    ctx = a["ctx_1024"][0]
    row_values = {"b0": "L0_xattn_b", "sa_out_b": "L1_xattn_sa_out_b", "mha_out_b": "L1_xattn_mha_out_b", "lin2_b": "L1_xattn_lin2_b",
                  "out_b": "L1_attn_out_b", "b_con": "L1_ffn_b_con", "down_bias": "L1_ffn_down_bias"}
    wide_values = {n: "L1_xattn_" + n for n in WIDE}
    wide_values.update({"ffn_g": "L0_ffn_ln_g", "ffn_b": "L0_ffn_ln_b"})
    arrays = {
        "x_in": a["x"][0], "ctxT_in": ctx.T, "ctxN_in": ctx.reshape(TILES, D, D).transpose(1, 0, 2),
        **{f"{p}_in": np.concatenate([values[n] for n, _ in entries], axis=1) for p, entries in PACKS.items()},
        "rows_in": np.concatenate([a[row_values[n]] for n in ROWS])[None, :],
        "wide_in": np.broadcast_to(np.concatenate([a[wide_values[n]] for n in WIDE]), (T, len(WIDE) * D)),
        "small_in": small, "coef_in": np.concatenate([up_w, dn_w[::-1]]).reshape(2 * STAGES, -1),
    }
    nc = bacc.Bacc("TRN2", target_bir_lowering=False, num_devices=1)
    arrays = {k: np.ascontiguousarray(v) for k, v in arrays.items()}
    aps = {k: nc.dram_tensor(k, v.shape, mybir.dt.from_np(v.dtype), kind="ExternalInput").ap() for k, v in arrays.items()}
    out = nc.dram_tensor("out", (T, D), mybir.dt.float32, kind="ExternalOutput").ap()
    build(nc, out=out, **aps)
    r = run(nc, [arrays], core_ids=[0])
    return r.results[0]["out"].reshape(1, T, D)
```

```python
from contextlib import ExitStack

import numpy as np
import concourse.bass as bass
from concourse import mybir

T = 64
D = 128
M = 6272
TILES = M // D
CHUNK = 4
CHUNKS = -(-TILES // CHUNK)
HALF0 = 25
HALF1 = TILES - HALF0
H0, HD0 = 16, 8
H1, HD1 = 8, 16
PAIRS = H1 // 2
HV = HD1 + 1
CONSTANTS = 7
STEPS1 = PAIRS * CHUNKS
POOL_FROM = 44
LAG = CHUNKS + 3
N = 16
DI = 256
FF = 512
FB = FF // D
STAGES = 9
LO = 5
RING = 4
EPS = 1e-5
RMS_EPS = 1e-6
NORMS = ["x", "x1", "gated", "ffn", "tgt", "t1", "t2", "t3", "rms", "x4", "x5"]

FIRST = [("W0", D), ("ident", D), ("b0", 1)]
SECOND = [("swap", D), ("pair_sum", D), ("stack", T), ("W0T", D), ("WvT", D)]
MATS = [("Wq", D), ("Wk", D), ("Wv", D), ("Wg1", HD0), ("Wo", D), ("rotT", D), ("cosT", T), ("sinT", T),
        ("head", H0), ("causal", T), ("ln_w", 1), ("ln_b", 1),
        ("saWvT", D), ("sa_bv", 1), ("sa_outT", D), ("ln1_g", 1), ("ln1_b", 1), ("WqT", D), ("bq", 1), ("Wk1", D), ("bk", 1), ("head1", H1),
        ("bv", 1), ("sumsel", 32), ("mha_outT", D), ("ln2_g", 1), ("ln2_b", 1)]
LATE = [("lin1T", FF), ("lin1_b", FB), ("lin2T", FB * D), ("rms_w", 1), ("in_W", 2 * DI), ("in_b", 4),
        ("conv_w", 8), ("conv_b", 2), ("A_log", 2 * N), ("dbc_W", 2 * 48), ("dup_b", 2), ("out_W", 2 * D),
        ("up_bias", FB)]
BFLY = [("exp", FF), ("conT", FF)]
PACKS = {"first": FIRST, "second": SECOND, "mats": MATS, "late": LATE, "bfly": BFLY}
ROWS = ["b0", "sa_out_b", "mha_out_b", "lin2_b", "out_b", "b_con", "down_bias"]
WIDE = ["ffn_g", "ffn_b", "ln1_g", "ln1_b", "ln2_g", "ln2_b", "ln3_g", "ln3_b"]
SMALL = [("Wg2", D), ("dup_W", 2 * D), ("dt_b", 1), ("bc_b", 1), ("own", N), ("onesB", D), ("onesC", D),
         ("b_exp", 32), ("coef_lo", LO * 2 * 32), ("coef_hi", (STAGES - LO) * 2 * 16)]


def offsets(entries):
    at, out = 0, {}
    for name, width in entries:
        out[name] = (at, at + width)
        at += width
    return out, at


def build(nc, x_in, ctxT_in, ctxN_in, first_in, second_in, mats_in, late_in, bfly_in, rows_in, wide_in, small_in, coef_in, out):
    f32 = mybir.dt.float32
    ACT = mybir.ActivationFunctionType
    ALU = mybir.AluOpType
    X = mybir.AxisListType.X
    ctx = ExitStack()
    with ctx:
        sems = {}

        def sem(name):
            if name not in sems:
                sems[name] = ctx.enter_context(nc.semaphore(name))
            return sems[name]

        def sb(name, *shape):
            return ctx.enter_context(nc.sbuf_tensor(name, list(shape), f32))

        pack, place = {}, {}
        for name, entries in PACKS.items():
            place[name], width = offsets(entries)
            pack[name] = sb("p_" + name, D, width)
        small_at, small_w = offsets(SMALL)
        small = sb("p_small", 32, small_w)

        def of(p, name, lo=0, hi=None):
            a, b = place[p][name]
            return pack[p][:, a + lo:(a + hi if hi is not None else b)]

        def sm(name, rows):
            a, b = small_at[name]
            return small[0:rows, a:b]

        rows = sb("rows", 1, len(ROWS) * D)

        def row(name):
            i = ROWS.index(name)
            return rows[0:1, i * D:(i + 1) * D]

        wide = sb("wide", T, len(WIDE) * D)

        def wd(name):
            i = WIDE.index(name)
            return wide[:, i * D:(i + 1) * D]

        ident = of("first", "ident")
        ctxT = sb("ctxT", D, M)
        V = sb("V", D, TILES * H1 * HV + 16)
        v_parts = V[:, 0:TILES * H1 * HV].rearrange("p (t h d) -> p t h d", h=H1, d=HV)
        scoresA = sb("scoresA", D, M)
        big = sb("big", D, M)
        ctxN = big[:, :].rearrange("p (t c) -> p t c", c=D)
        scores = [scoresA, big]
        pT = sb("pT", D, 3, CHUNK * D)
        coefs = sb("coefs", D, RING, 2, FF)

        x = sb("x", T, D)
        half_power = sb("half_power", T, 1)
        ones = sb("ones", 1, T)
        LN = len(NORMS)
        stats, mv = sb("stats", T, 6 * LN), sb("mv", T, 2 * LN)
        var_eps, rstd = sb("var_eps", T, LN), sb("rstd", T, LN)
        norm = sb("norm", T, LN * D)

        def nm(name):
            i = NORMS.index(name)
            return norm[:, i * D:(i + 1) * D]

        def nth(name):
            return sum(n not in ("ffn", "t3") for n in NORMS[:NORMS.index(name) + 1])

        x1, x2, x3, x4, x5 = (sb(f"x{i}", T, D) for i in range(1, 6))
        x6 = sb("x6", D, D // 2)
        used = [0]

        def after(parts, *shape):
            n = int(np.prod(shape))
            flat = V[0:parts, used[0]:used[0] + n]
            used[0] += n
            assert used[0] <= M
            if len(shape) == 1:
                return flat
            names = "abc"[:len(shape)]
            return flat.rearrange(f"p ({' '.join(names)}) -> p {' '.join(names)}", **dict(zip(names, shape)))

        xnT = sb("xnT", D, 2, T)
        qWT, cp = sb("qWT", D, T), sb("cp", D, 1)
        cmax, lsum = sb("cmax", D, 8), sb("lsum", D, 8)
        nmax0, nmaxM, w0, l0, wl, rL, fac = (sb(n, D, 1) for n in ("nmax0", "nmaxM", "w0", "l0", "wl", "rL", "fac"))
        o_sc, attT = sb("o_sc", D, D), sb("attT", D, T)
        xn1T = sb("xn1T", D, 2, T)
        tanh_qk, s2, s2cos, s2sin, qk = (sb(n, D, 2, T) for n in ("tanh_qk", "s2", "s2cos", "s2sin", "qk"))
        q_heads = big[:, 0:H0 * T].rearrange("p (h n) -> p h n", h=H0)
        energy = big[:, 2048:2048 + H0 // 2 * T].rearrange("p (h n) -> p h n", h=H0 // 2)
        g1T, tanh_gate = sb("g1T", HD0, T), sb("tanh_gate", T, D)
        v_halves = sb("v_halves", D, 2, T)
        gated, yT = sb("gated", T, D), sb("yT", D, T)
        x2b, tgtT, vT, t1, z6T = sb("x2b", T, D), sb("tgtT", D, T), sb("vT", D, T), sb("t1", T, D), sb("z6T", D, T)
        xg, x_q, q_all = sb("xg", T, D), sb("x_q", T, D), sb("q_all", D, T)
        q_wide = sb("q_wide", D, H1, T)
        qk1 = sb("qk1", D, H1, T)
        cp1 = sb("cp1", D, PAIRS)
        run_max = sb("run_max", D, 2, CHUNK, D)
        tile_max = sb("tile_max", D, D)
        max1, minus1, rl1 = (sb(n, D, PAIRS) for n in ("max1", "minus1", "rl1"))
        shift_cols, shift = sb("shift_cols", D, D), sb("shift", D, 2, D)
        oS, ca, caT = sb("oS", D, 2, D), sb("ca", T, D), sb("caT", D, T)
        x3b = sb("x3b", T, D)
        t2, x7g, x7, t3 = (after(T, D) for _ in range(4))
        z7T, hT = after(D, T), after(D, FB, T)
        hmT = after(D, T)
        pad = sb("pad", D, 2, T + 3)
        xc, tanh_xc, xs2 = after(D, 2, T), after(D, 2, T), after(D, 2, T)
        gT, tanh_g, gs2 = after(D, 2, T), after(D, 2, T), after(D, 2, T)
        dtT, bcT = after(N, T), after(2 * N, T)
        bc_own = big[0:2 * N, 0:N * T].rearrange("p (n t) -> p n t", n=N)
        z, zneg, ez, lz, zpos, delta, dx = (after(D, 2, T) for _ in range(7))
        expA = sb("expA", D, 2, N)
        dA, Bx, hs = (ctxT[:, i * 2 * N * T:(i + 1) * 2 * N * T].rearrange("p (b n t) -> p b n t", b=2, n=N) for i in range(3))
        decay = scoresA[:, 0:2 * N * T].rearrange("p (b n t) -> p b n t", b=2, n=N)
        hC = scoresA[:, 2 * N * T:4 * N * T].rearrange("p (b n t) -> p b n t", b=2, n=N)
        b_rows = big[:, 2 * N * T:3 * N * T].rearrange("p (n t) -> p n t", n=N)
        c_rows = big[:, N * T:2 * N * T].rearrange("p (n t) -> p n t", n=N)
        y, yg, xr = after(D, 2, T), after(D, 2, T), after(T, D)
        x6T, gl6 = after(D, T), after(D, FB, T)
        hidden = {"up": [of("bfly", "exp"), sb("upB", D, FF)[:]], "dn": [of("bfly", "conT"), sb("dnB", D, FF)[:]]}
        partner = sb("partner", D, FF)
        wup, wdn = hidden["up"][STAGES % 2], after(D, FB, D)
        b_lo, b_hi = [sm("b_exp", 16), sb("b_lo", 16, 32)[:]], [sb("b_hiA", 32, 16)[:], sb("b_hiB", 32, 16)[:]]
        b_partner = sb("b_partner", 32, 32)
        beff = after(D, FB)

        PS = ctx.enter_context(nc.psum_tensor("PS", [D, 8, 512], f32))
        S_BANKS, T_BANKS, O_BANKS, F_BANKS = (0, 1, 6, 2), (2, 3), (4, 7), (5, 6)

        def width(c):
            return min(CHUNK, TILES - CHUNK * c) * D

        STEPS = [("up", k) for k in range(STAGES)] + [("dn", k) for k in reversed(range(STAGES))]

        def by_pool(n):
            return n >= POOL_FROM and n % 4 == 3

        def shifts(n):
            pool_ = sum(by_pool(i) for i in range(n + 1))
            return n + 1 - pool_, pool_

        def by_tile(ap):
            return ap.rearrange("p (t q) -> p t q", q=D)

        def shift_of(n):
            g, c = divmod(n, CHUNKS)
            return shift[:, g % 2:g % 2 + 1, :].to_broadcast([D, width(c) // D, D])

        def chunk1(n):
            g, c = divmod(n, CHUNKS)
            return scores[g % 2][:, 512 * c:512 * c + width(c)]

        PIECES = [(0, 2), (2, 4), (4, 5), (5, 7)]

        def ctxT_pieces(j):
            a, (lo, hi) = HALF0 * D, PIECES[j]
            return (512 * lo, min(512 * hi, a)), (a + 512 * lo, min(a + 512 * hi, M))

        def ctxN_pieces(j):
            return (8 * j, min(8 * j + 8, HALF0)), (HALF0 + 8 * j, min(HALF0 + 8 * j + 8, TILES))

        block = ctx.enter_context(nc.Block())

        @block.sync
        def _(sp):
            sp.dma_start(x[:], x_in).then_inc(sem("x_in"), 16)
            sp.dma_start(pack["first"][:], first_in).then_inc(sem("first_in"), 16)
            for j in range(4):
                for lo, hi in ctxT_pieces(j):
                    sp.dma_start(ctxT[:, lo:hi], ctxT_in[:, lo:hi]).then_inc(sem(f"ctxT_in{j}"), 16)
            sp.dma_start(pack["second"][:], second_in).then_inc(sem("second_in"), 16)
            for j in range(4):
                for lo, hi in ctxN_pieces(j):
                    if lo < hi:
                        sp.dma_start(ctxN[:, lo:hi, :], ctxN_in[:, lo:hi, :]).then_inc(sem(f"ctxN_in{j}"), 16)
                if j == 2:
                    sp.dma_start(rows[:], rows_in).then_inc(sem("rows_in"), 16)
            sp.dma_start(pack["mats"][:], mats_in).then_inc(sem("mats_in"), 16)
            sp.dma_start(small[:], small_in).then_inc(sem("small_in"), 16)
            sp.dma_start(pack["bfly"][:], bfly_in).then_inc(sem("bfly_in"), 16)
            sp.dma_start(wide[:], wide_in).then_inc(sem("wide_in"), 16)
            sp.dma_start(pack["late"][:], late_in).then_inc(sem("late_in"), 16)
            for i in range(2 * STAGES):
                if i >= RING:
                    sp.wait_ge(sem("coefs_used"), i - RING + 1)
                sp.dma_start(coefs[:, i % RING, :, :].rearrange("p j f -> p (j f)"), coef_in[i:i + 1, :].to_broadcast([D, 2 * FF])).then_inc(sem(f"coefs_in{i % RING}"), 16)
            sp.wait_ge(sem("x6"), 1)
            sp.dma_start(out.rearrange("t (h c) -> h t c", h=2), x6[:]).then_inc(sem("stored"), 16)
            sp.wait_ge(sem("stored"), 16)

        @block.gpsimd
        def _(pool):
            def rsqrt(name):
                i = NORMS.index(name)
                pool.wait_ge(sem("var_ready"), i + 1)
                pool.tensor_tensor(rstd[:, i:i + 1], var_eps[:, i:i + 1], half_power[:], ALU.pow).then_inc(sem("rstd_ready"), 1)

            steps = [0]

            def link(ins):
                steps[0] += 1
                ins.then_inc(sem("pool_step"), 1)
                pool.wait_ge(sem("pool_step"), steps[0])

            def butterfly(dst, src, t, coef, stride):
                def half(ap, h):
                    return ap.rearrange("p (n h s) -> p n h s", h=2, s=stride)[:, :, h, :]
                for h in range(2):
                    link(pool.tensor_tensor(half(t, h), half(src, 1 - h), half(coef[:, 1, :], h), ALU.mult))
                link(pool.tensor_tensor(dst, src, coef[:, 0, :], ALU.mult))
                link(pool.tensor_tensor(dst, dst, t, ALU.add))

            stages = iter(enumerate(STEPS))

            def stage(n=1):
                for _ in range(n):
                    i, (which, k) = next(stages)
                    bufs, m = hidden[which], i % STAGES
                    pool.wait_ge(sem(f"coefs_in{i % RING}"), 16 * (i // RING + 1))
                    butterfly(bufs[(m + 1) % 2], bufs[m % 2], partner[:], coefs[:, i % RING], 1 << k)
                    pool.sem_inc(sem("coefs_used"), 1)

            pool.memset(half_power[:], -0.5).then_inc(sem("pool_const"), 1)
            pool.memset(ones[:], 1.0).then_inc(sem("ones_ready"), 1)
            pool.wait_ge(sem("pool_const"), 1)
            rsqrt("x")
            rsqrt("x1")
            pool.wait_ge(sem("small_in"), 16)
            lo = sm("coef_lo", 16).rearrange("p (k j f) -> p k j f", k=LO, j=2)
            for k in range(LO):
                butterfly(b_lo[(k + 1) % 2], b_lo[k % 2], b_partner[0:16, 0:32], lo[:, k], 1 << k)
            pool.sem_inc(sem("b_lo"), 1)
            rsqrt("gated")
            pool.wait_ge(sem("wide_in"), 16)
            pool.wait_ge(sem("x2"), 1)
            pool.tensor_tensor(x2b[:], x2[:], wd("ffn_b"), ALU.add).then_inc(sem("x2b"), 1)
            rsqrt("ffn")
            rsqrt("tgt")
            rsqrt("t1")
            pool.wait_ge(sem("normed"), nth("t1"))
            link(pool.tensor_tensor(xg[:], nm("t1"), wd("ln1_g"), ALU.mult))
            pool.tensor_tensor(x_q[:], xg[:], wd("ln1_b"), ALU.add).then_inc(sem("x_q"), 1)
            pool.tensor_tensor(x3b[:], x3[:], wd("ln3_b"), ALU.add).then_inc(sem("x3b"), 1)
            pool.wait_ge(sem("bfly_in"), 16)
            stage(3)
            pool.wait_ge(sem("b_hi"), 1)
            hi = sm("coef_hi", 32).rearrange("p (k j f) -> p k j f", k=STAGES - LO, j=2)
            for k in range(STAGES - LO):
                butterfly(b_hi[(k + 1) % 2], b_hi[k % 2], b_partner[:, 0:16], hi[:, k], 1 << k)
            pool.sem_inc(sem("b_up"), 1)
            stage(STAGES - 3)
            pool.sem_inc(sem("up_done"), 1)
            stage(STAGES - 3)
            for m in range(STEPS1):
                if by_pool(m):
                    pool.wait_ge(sem("shift"), m // CHUNKS + 1)
                    pool.wait_ge(sem("s1_out"), m + 1)
                    pool.wait_ge(sem("run_max"), m + 1)
                    t = by_tile(chunk1(m))
                    pool.tensor_tensor(t, t, shift_of(m), ALU.add).then_inc(sem("shifted_pool"), 1)
            stage(1)
            rsqrt("t2")
            pool.wait_ge(sem("normed"), nth("t2"))
            link(pool.tensor_tensor(x7g[:], nm("t2"), wd("ln2_g"), ALU.mult))
            pool.tensor_tensor(x7[:], x7g[:], wd("ln2_b"), ALU.add).then_inc(sem("x7"), 1)
            rsqrt("t3")
            rsqrt("rms")
            rsqrt("x4")
            pool.wait_ge(sem("normed"), nth("x4"))
            pool.tensor_tensor(xr[:], nm("x4"), x4[:], ALU.add).then_inc(sem("xr"), 1)
            stage(2)
            pool.sem_inc(sem("dn_done"), 1)
            pool.wait_ge(sem("delta"), 1)
            pool.wait_ge(sem("expA"), 1)
            pool.tensor_tensor(dA[:, 1], delta[:, 1:2, :].to_broadcast([D, N, T]), expA[:, 1, :].unsqueeze(2).to_broadcast([D, N, T]), ALU.mult).then_inc(sem("dA1"), 1)
            pool.wait_ge(sem("dx"), 1)
            for h in range(2):
                n = slice(h * N // 2, (h + 1) * N // 2)
                pool.wait_ge(sem("b_rows"), h + 1)
                pool.tensor_tensor(Bx[:, 1, n], b_rows[:, n], dx[:, 1:2, :].to_broadcast([D, N // 2, T]), ALU.mult).then_inc(sem("Bx1"), 1)
            pool.wait_ge(sem("scanned"), 1)
            for h in range(2):
                n = slice(h * N // 2, (h + 1) * N // 2)
                pool.wait_ge(sem("c_rows"), h + 1)
                pool.tensor_tensor(hC[:, 0, n], c_rows[:, n], hs[:, 0, n], ALU.mult).then_inc(sem("hC0"), 1)
            rsqrt("x5")

        @block.scalar
        def _(act):
            A = act.activation
            fills = iter(range(CHUNKS))

            def fill(n=1):
                for _ in range(n):
                    c = next(fills)
                    act.wait_ge(sem("fill"), c + 1)
                    A(v_parts[:, c * CHUNK:c * CHUNK + width(c) // D, :, 0:HD1], PS[:, F_BANKS[c % 2], 0:width(c)].rearrange("p (t h d) -> p t h d", h=H1, d=HD1),
                      ACT.Copy).then_inc(sem("fill_out"), 1)

            act.wait_ge(sem("nmax0"), 1)
            for j in range(7):
                P, w = (D, 512) if j < 6 else (T, D)
                s = scoresA[0:P, 512 * j:512 * j + w]
                A(s, s, ACT.Exp, bias=nmax0[0:P], accum_out=lsum[0:P, j:j + 1]).then_inc(sem("exp0"), 1)
            act.wait_ge(sem("nmaxM"), 1)
            A(w0[:], nmax0[:], ACT.Exp, scale=-1.0, bias=nmaxM[:]).then_inc(sem("w0"), 1)
            fill(2)
            act.wait_ge(sem("qkT"), 1)
            A(tanh_qk[:], PS[:, 0, 0:2 * T].rearrange("p (a n) -> p a n", a=2), ACT.Tanh, scale=0.5).then_inc(sem("tanh_qk"), 1)
            act.wait_ge(sem("g1"), 1)
            A(g1T[:], PS[0:HD0, 1, 0:T], ACT.Copy).then_inc(sem("g1T"), 1)
            act.wait_ge(sem("v0"), 1)
            act.wait_ge(sem("constants"), CONSTANTS)
            for h in range(2):
                P = slice(T * h, T * h + T)
                A(v_halves[P, h, :], PS[P, 2, T * h:T * h + T], ACT.Copy).then_inc(sem("v_halves"), 1)
            act.wait_ge(sem("gate"), 1)
            A(tanh_gate[:], PS[0:T, 7, 256:256 + D], ACT.Tanh, scale=0.5).then_inc(sem("tanh_gate"), 1)
            fill(6)
            act.wait_ge(sem("v1"), 1)
            A(vT[:], PS[:, 1, 0:T], ACT.Identity, bias=of("mats", "sa_bv")).then_inc(sem("vT"), 1)
            fill(5)
            act.wait_ge(sem("late_in"), 16)
            A(expA[:].rearrange("p b n -> p (b n)"), of("late", "A_log"), ACT.Exp).then_inc(sem("expA"), 1)

            act.wait_ge(sem("b_turned"), 1)
            A(b_hi[0], PS[0:32, 7, 384:400], ACT.Copy).then_inc(sem("b_hi"), 1)

            for n in range(STEPS1 + LAG + 1):
                if n < STEPS1:
                    act.wait_ge(sem("s1"), n + 1)
                    if n >= 2 * CHUNKS:
                        act.wait_ge(sem("pv"), n - 2 * CHUNKS + 1)
                    A(chunk1(n), PS[:, S_BANKS[n % 4], 0:width(n % CHUNKS)], ACT.Copy).then_inc(sem("s1_out"), 1)
                if n > LAG:
                    m = n - LAG - 1
                    by_dve, pooled = shifts(m)
                    if by_pool(m):
                        act.wait_ge(sem("shifted_pool"), pooled)
                    else:
                        act.wait_ge(sem("shifted"), by_dve)
                    A(chunk1(m), chunk1(m), ACT.Exp).then_inc(sem("exp1"), 1)

            act.wait_ge(sem("lin1_b"), 1)
            for b in (2, 3):
                A(hT[:, b, :], PS[:, 1, T * (b - 2):T * (b - 1)], ACT.Relu, bias=of("late", "lin1_b", b, b + 1)).then_inc(sem("h_act"), 1)
            act.wait_ge(sem("gate1"), 1)
            for b in range(2):
                A(gT[:, b, :], PS[:, 1, T * b:T * b + T], ACT.Identity, bias=of("late", "in_b", 2 + b, 3 + b)).then_inc(sem("gT"), 1)
            act.wait_ge(sem("gT"), 2)
            A(tanh_g[:], gT[:], ACT.Tanh, scale=0.5).then_inc(sem("tanh_g"), 1)
            act.wait_ge(sem("xc"), 1)
            A(tanh_xc[:], xc[:], ACT.Tanh, scale=0.5).then_inc(sem("tanh_xc"), 1)
            act.wait_ge(sem("dt_low"), 1)
            A(dtT[:], PS[0:N, 2, 0:T], ACT.Identity, scale=0.5, bias=sm("dt_b", N)).then_inc(sem("dtT"), 1)
            act.preload_act_table_set("natural_log_exp_and_others")
            act.wait_ge(sem("zneg"), 1)
            A(ez[:], zneg[:], ACT.Exp).then_inc(sem("ez"), 1)
            act.wait_ge(sem("ez"), 1)
            A(lz[:], ez[:], ACT.Ln, bias=1.0).then_inc(sem("lz"), 1)
            for h in range(2):
                act.wait_ge(sem("b_wide"), h + 1)
                A(b_rows[:, h * N // 2:(h + 1) * N // 2, :], PS[:, h, :].rearrange("p (n t) -> p n t", t=T), ACT.Copy).then_inc(sem("b_rows"), 1)
                act.wait_ge(sem(f"dA{h}"), 1)
                A(decay[:, h, :, 1:T], dA[:, h, :, 1:T], ACT.Exp, scale=-1.0).then_inc(sem("decay"), 1)
            for h in range(2):
                act.wait_ge(sem("c_wide"), h + 1)
                A(c_rows[:, h * N // 2:(h + 1) * N // 2, :], PS[:, 2 + h, :].rearrange("p (n t) -> p n t", t=T), ACT.Copy).then_inc(sem("c_rows"), 1)
            act.wait_ge(sem("dn_turned"), 1)
            A(wdn[:, :, :], PS[:, 7, :].rearrange("p (b c) -> p b c", b=FB), ACT.Copy).then_inc(sem("wdn"), 1)
            act.preload_act_table(ACT.Gelu)
            act.wait_ge(sem("beff"), 1)
            act.wait_ge(sem("h6"), 1)
            for b in range(FB):
                A(gl6[:, b, :], PS[:, 0, T * b:T * b + T], ACT.Gelu, bias=beff[:, b:b + 1]).then_inc(sem("gelu"), 1)

        @block.vector
        def _(dve):
            steps = [0]

            def link(ins):
                steps[0] += 1
                ins.then_inc(sem("dve_step"), 1)
                dve.wait_ge(sem("dve_step"), steps[0])

            def variance(name, src, scale=1.0, eps=EPS):
                i = NORMS.index(name)
                link(dve.bn_stats(stats[:, 6 * i:6 * i + 6], src))
                link(dve.bn_aggr(mv[:, 2 * i:2 * i + 2], stats[:, 6 * i:6 * i + 6]))
                dve.tensor_scalar(var_eps[:, i:i + 1], mv[:, 2 * i + 1:2 * i + 2], scale, eps, ALU.mult, ALU.add).then_inc(sem("var_ready"), 1)

            def normalise(name, src, mean_of=None):
                i, m = NORMS.index(name), NORMS.index(mean_of or name)
                dve.wait_ge(sem("rstd_ready"), i + 1)
                dve.tensor_scalar(nm(name), src, mv[:, 2 * m:2 * m + 1], rstd[:, i:i + 1], ALU.subtract, ALU.mult).then_inc(sem("normed"), 1)

            def layer_norm(name, src):
                variance(name, src)
                normalise(name, src)

            def norm_onto(name, dst, src, gain, base):
                i = NORMS.index(name)
                link(dve.scalar_tensor_tensor(nm(name), src, mv[:, 2 * i:2 * i + 1], gain, ALU.subtract, ALU.mult))
                dve.wait_ge(sem("rstd_ready"), i + 1)
                link(dve.scalar_tensor_tensor(dst, nm(name), rstd[:, i:i + 1], base, ALU.mult, ALU.add))

            dve.memset(v_parts[:, :, :, HD1:HV], 1.0).then_inc(sem("constants"), 1)
            dve.memset(V[:, TILES * H1 * HV:], 0.0).then_inc(sem("constants"), 1)
            dve.memset(scoresA[T:D, 3072:3200], 0.0).then_inc(sem("constants"), 1)
            dve.memset(cmax[T:D, 6:7], -3.0e38).then_inc(sem("constants"), 1)
            dve.memset(lsum[T:D, 6:7], 0.0).then_inc(sem("constants"), 1)
            dve.memset(v_halves[:], 0.0).then_inc(sem("constants"), 1)
            dve.memset(pad[:, :, 0:3], 0.0).then_inc(sem("constants"), 1)

            dve.wait_ge(sem("x_in"), 16)
            layer_norm("x", x[:])
            dve.wait_ge(sem("norm_turned"), 1)
            dve.tensor_copy(xnT[:], PS[:, 7, 0:T].unsqueeze(1).to_broadcast([D, 2, T])).then_inc(sem("norm_columns"), 1)
            dve.wait_ge(sem("qW"), 1)
            dve.tensor_copy(qWT[:], PS[:, 7, 64:64 + T]).then_inc(sem("qWT"), 1)
            link(dve.tensor_copy(cp[:], PS[:, 7, 128:129]))
            for j in range(7):
                P, w = (D, 512) if j < 6 else (T, D)
                dve.wait_ge(sem("s0"), j + 1)
                dve.tensor_scalar(scoresA[0:P, 512 * j:512 * j + w], PS[0:P, S_BANKS[j % 2], 0:w], cp[0:P], None,
                                  ALU.add, ALU.max, accum_out=cmax[0:P, j:j + 1]).then_inc(sem("s0_out"), 1)
            dve.wait_ge(sem("s0_out"), 7)
            dve.wait_ge(sem("constants"), CONSTANTS)
            dve.tensor_reduce(nmax0[:], cmax[:, 0:7], X, ALU.max, negate=True).then_inc(sem("nmax0"), 1)
            dve.wait_ge(sem("nmax_other"), 1)
            dve.tensor_tensor(nmaxM[:], PS[:, 7, 130:131], nmax0[:], ALU.min).then_inc(sem("nmaxM"), 1)
            for c in range(7):
                w = 512 if c < 6 else D
                dve.wait_ge(sem("turned0"), c + 1)
                if c >= 3:
                    dve.wait_ge(sem("pv0"), c - 2)
                dve.tensor_copy(pT[:, c % 3, 0:w], PS[:, T_BANKS[c % 2], 0:w]).then_inc(sem("pT0"), 1)
            dve.wait_ge(sem("exp0"), 7)
            dve.wait_ge(sem("constants"), CONSTANTS)
            link(dve.reduce_sum(l0[:], lsum[:, 0:7], X))
            dve.wait_ge(sem("w0"), 1)
            dve.tensor_tensor(wl[:], w0[:], l0[:], ALU.mult).then_inc(sem("wl"), 1)
            dve.wait_ge(sem("l_both"), 1)
            link(dve.reciprocal(rL[:], PS[:, 7, 132:133]))
            link(dve.tensor_tensor(fac[:], w0[:], rL[:], ALU.mult))
            dve.wait_ge(sem("pv0"), 7)
            dve.tensor_scalar(o_sc[:], PS[:, 4, 0:D], fac[:], None, ALU.mult).then_inc(sem("o_sc"), 1)
            dve.wait_ge(sem("att"), 1)
            dve.tensor_copy(attT[:], PS[:, 7, 192:192 + T]).then_inc(sem("attT"), 1)
            dve.wait_ge(sem("xattn"), 1)
            link(dve.scalar_tensor_tensor(x1[:], PS[0:T, 3, 256:256 + D], 0.0, x[:], ALU.max, ALU.add))

            layer_norm("x1", x1[:])
            dve.wait_ge(sem("norm_turned"), 2)
            dve.tensor_copy(xn1T[:], PS[:, 4, 0:T].unsqueeze(1).to_broadcast([D, 2, T])).then_inc(sem("norm_columns"), 1)
            dve.wait_ge(sem("tanh_qk"), 1)
            dve.scalar_tensor_tensor(s2[:], tanh_qk[:], 1.0, PS[:, 0, 0:2 * T].rearrange("p (a n) -> p a n", a=2), ALU.add, ALU.mult).then_inc(sem("s2"), 1)
            dve.wait_ge(sem("s2"), 1)
            link(dve.tensor_tensor(s2cos[:], s2[:], of("mats", "cosT").unsqueeze(1).to_broadcast([D, 2, T]), ALU.mult))
            dve.wait_ge(sem("rotated"), 1)
            link(dve.tensor_tensor(s2sin[:], PS[:, 3, 0:2 * T].rearrange("p (a n) -> p a n", a=2), of("mats", "sinT").unsqueeze(1).to_broadcast([D, 2, T]), ALU.mult))
            link(dve.tensor_tensor(qk[:], s2cos[:], s2sin[:], ALU.add))
            for h in range(2):
                dve.tensor_tensor(q_heads[:, 8 * h:8 * h + 8, :], qk[:, 0:1, :].to_broadcast([D, 8, T]),
                                  of("mats", "head", 8 * h, 8 * h + 8).unsqueeze(2).to_broadcast([D, 8, T]), ALU.mult).then_inc(sem("q_heads"), 1)
            dve.wait_ge(sem("energy"), 1)
            dve.tensor_tensor(energy[:, :, :], PS[:, 0, :].rearrange("p (h n) -> p h n", h=8),
                              of("mats", "causal").unsqueeze(1).to_broadcast([D, 8, T]), ALU.mult).then_inc(sem("masked"), 1)
            dve.wait_ge(sem("tanh_gate"), 1)
            dve.wait_ge(sem("lin_att"), 1)
            link(dve.scalar_tensor_tensor(gated[:], tanh_gate[:], 1.0, PS[0:T, 1, 128:128 + D], ALU.add, ALU.mult))
            layer_norm("gated", gated[:])
            dve.wait_ge(sem("norm_turned"), 3)
            dve.tensor_scalar(yT[:], PS[:, 4, 64:64 + T], of("mats", "ln_w"), of("mats", "ln_b"), ALU.mult, ALU.add).then_inc(sem("norm_columns"), 1)
            dve.wait_ge(sem("attn_out"), 1)
            dve.tensor_tensor(x2[:], PS[0:T, 4, 128:128 + D], x1[:], ALU.add).then_inc(sem("x2"), 1)
            dve.wait_ge(sem("x2"), 1)

            variance("ffn", x2[:], 1.0 + EPS, EPS * EPS)
            dve.wait_ge(sem("wide_in"), 16)
            dve.wait_ge(sem("x2b"), 1)
            norm_onto("ffn", x3[:], x2[:], wd("ffn_g"), x2b[:])

            layer_norm("tgt", x3[:])
            dve.wait_ge(sem("norm_turned"), 4)
            dve.tensor_copy(tgtT[:], PS[:, 0, 0:T]).then_inc(sem("norm_columns"), 1)
            dve.wait_ge(sem("sa"), 1)
            link(dve.tensor_tensor(t1[:], PS[0:T, 2, 128:128 + D], nm("tgt"), ALU.add))
            layer_norm("t1", t1[:])
            dve.wait_ge(sem("norm_turned"), 5)
            dve.tensor_scalar(z6T[:], PS[:, 0, 64:64 + T], of("mats", "ln1_g"), of("mats", "ln1_b"), ALU.mult, ALU.add).then_inc(sem("norm_columns"), 1)
            dve.wait_ge(sem("q1"), 1)
            for p in range(2):
                dve.tensor_scalar(q_wide[:, p, :], PS[:, 4, 256:256 + T], of("mats", "bq"), of("mats", "head1", p, p + 1), ALU.add, ALU.mult).then_inc(sem("q_wide"), 1)
            link(dve.tensor_scalar(q_all[:], PS[:, 4, 256:256 + T], of("mats", "bq"), None, ALU.add))
            dve.tensor_tensor(q_wide[:, 2:H1, :], q_all[:].unsqueeze(1).to_broadcast([D, H1 - 2, T]),
                              of("mats", "head1", 2, H1).unsqueeze(2).to_broadcast([D, H1 - 2, T]), ALU.mult).then_inc(sem("q_wide"), 1)
            def queries(h):
                dve.wait_ge(sem("qk1"), h + 1)
                cols = slice(0, 2) if h == 0 else slice(2, H1)
                dve.tensor_copy(qk1[:, cols, :], PS[:, 2 + h, 0:(2 if h == 0 else 6) * T].rearrange("p (h n) -> p h n", n=T)).then_inc(sem("qk1_out"), 1)
                dve.tensor_copy(cp1[:, 0:1] if h == 0 else cp1[:, 1:PAIRS], PS[:, 2 + h, 480:481] if h == 0 else PS[:, 2 + h, 481:484]).then_inc(sem("cp1"), 1)

            queries(0)
            dve.wait_ge(sem("cp1"), 1)

            for n in range(STEPS1 + LAG + 6):
                m = n - LAG
                if 0 <= m < STEPS1 and not by_pool(m):
                    dve.wait_ge(sem("shift"), m // CHUNKS + 1)
                    t = by_tile(chunk1(m))
                    dve.tensor_tensor(t, t, shift_of(m), ALU.add).then_inc(sem("shifted"), 1)
                g, c = divmod(n - 1, CHUNKS)
                if 1 <= n <= STEPS1:
                    dve.wait_ge(sem("s1_out"), n)
                    w = width(c) // D
                    m, s = run_max[:, g % 2, 0:w, :], by_tile(chunk1(n - 1))
                    if c == 0:
                        dve.tensor_copy(m, s).then_inc(sem("run_max"), 1)
                    else:
                        dve.wait_ge(sem("run_max"), n - 1)
                        dve.tensor_tensor(m, m, s, ALU.max).then_inc(sem("run_max"), 1)
                    if c == CHUNKS - 1:
                        dve.wait_ge(sem("run_max"), n)
                        dve.tensor_reduce(tile_max[:], run_max[:, g % 2].rearrange("p t q -> p q t"), X, ALU.max).then_inc(sem("tile_max"), 1)
                if n == 6:
                    queries(1)
                    dve.wait_ge(sem("cp1"), 2)
                if c == 0 and 1 <= g <= PAIRS:
                    dve.wait_ge(sem("max_turned"), g)
                    link(dve.tensor_reduce(max1[:, g - 1:g], PS[:, 3, 0:D], X, ALU.max))
                    link(dve.tensor_scalar(minus1[:, g - 1:g], max1[:, g - 1:g], cp1[:, g - 1:g], -1.0, ALU.add, ALU.mult))
                    dve.tensor_scalar(shift_cols[:], minus1[:, g - 1:g].to_broadcast([D, D]), cp1[:, g - 1:g], None, ALU.add).then_inc(sem("shift_cols"), 1)
                if c == 1 and 1 <= g <= PAIRS:
                    dve.wait_ge(sem("shift_rows"), g)
                    dve.tensor_copy(shift[:, (g - 1) % 2, :], PS[:, 3, D:2 * D]).then_inc(sem("shift"), 1)
                done, late = divmod(n - LAG - CHUNKS - 2, CHUNKS)
                if 0 <= done < PAIRS and late == 1:
                    dve.wait_ge(sem("pv"), (done + 1) * CHUNKS)
                    dve.tensor_copy(oS[:, done % 2, :], PS[:, O_BANKS[done % 2], 0:D]).then_inc(sem("oS"), 1)
                if 0 <= done < PAIRS and late == 3:
                    dve.wait_ge(sem("heads"), done + 1)
                    link(dve.reciprocal(rl1[:, done:done + 1], PS[:, 5, HD1:HV]))
                    for p in range(2):
                        P = slice(T * p, T * p + T)
                        a = 2 * HD1 * done + HD1 * p
                        dve.tensor_scalar(ca[:, a:a + HD1], PS[P, 5, 0:HD1], rl1[P, done:done + 1], None, ALU.mult).then_inc(sem("ca"), 1)
            dve.wait_ge(sem("caT"), 1)
            dve.tensor_scalar(caT[:], PS[:, 0, 0:T], of("mats", "bv"), None, ALU.add).then_inc(sem("caT_out"), 1)
            dve.wait_ge(sem("mha"), 1)
            dve.wait_ge(sem("x_q"), 1)
            link(dve.tensor_tensor(t2[:], PS[0:T, 1, 256:256 + D], x_q[:], ALU.add))
            layer_norm("t2", t2[:])
            dve.wait_ge(sem("late_in"), 16)
            dve.wait_ge(sem("b_columns"), 1)
            dve.tensor_tensor(beff[:], PS[:, 6, 0:FB], of("late", "up_bias"), ALU.add).then_inc(sem("beff"), 1)
            dve.wait_ge(sem("norm_turned"), 6)
            dve.tensor_scalar(z7T[:], PS[:, 2, 0:T], of("mats", "ln2_g"), of("mats", "ln2_b"), ALU.mult, ALU.add).then_inc(sem("norm_columns"), 1)
            dve.wait_ge(sem("lin1_a"), 1)
            for b in (0, 1):
                dve.tensor_scalar(hT[:, b, :], PS[:, 0, T * b:T * b + T], of("late", "lin1_b", b, b + 1), 0.0, ALU.add, ALU.max).then_inc(sem("h_dve"), 1)
            dve.wait_ge(sem("ff"), 1)
            dve.wait_ge(sem("x7"), 1)
            link(dve.tensor_tensor(t3[:], PS[0:T, 2, 128:128 + D], x7[:], ALU.add))
            variance("t3", t3[:])
            dve.wait_ge(sem("x3b"), 1)
            norm_onto("t3", x4[:], t3[:], wd("ln3_g"), x3b[:])

            variance("rms", x4[:], 1.0 + RMS_EPS, EPS * RMS_EPS)
            i, j = NORMS.index("rms"), NORMS.index("x4")
            dve.tensor_scalar(var_eps[:, j:j + 1], mv[:, 2 * i + 1:2 * i + 2], 1.0, EPS, ALU.mult, ALU.add).then_inc(sem("var_ready"), 1)
            normalise("rms", x4[:])
            normalise("x4", x4[:], mean_of="rms")
            dve.wait_ge(sem("rmsT"), 1)
            dve.tensor_scalar(hmT[:], PS[:, 2, 256:256 + T], of("late", "rms_w"), None, ALU.mult).then_inc(sem("hmT"), 1)
            dve.wait_ge(sem("x_in1"), 1)
            dve.wait_ge(sem("constants"), CONSTANTS)
            for b in range(2):
                dve.tensor_scalar(pad[:, b, 3:3 + T], PS[:, 0, T * b:T * b + T], of("late", "in_b", b, b + 1), None, ALU.add).then_inc(sem("pad"), 1)
            dve.wait_ge(sem("pad"), 2)
            for k in range(4):
                for b in range(2):
                    w = of("late", "conv_w", 4 * b + k, 4 * b + k + 1)
                    if k == 0:
                        ins = dve.tensor_scalar(xc[:, b, :], pad[:, b, 0:T], w, of("late", "conv_b", b, b + 1), ALU.mult, ALU.add)
                    else:
                        ins = dve.scalar_tensor_tensor(xc[:, b, :], pad[:, b, k:k + T], w, xc[:, b, :], ALU.mult, ALU.add)
                    ins.then_inc(sem("taps"), 1)
                dve.wait_ge(sem("taps"), 2 * k + 2)
            dve.sem_inc(sem("xc"), 1)
            dve.wait_ge(sem("tanh_g"), 1)
            dve.scalar_tensor_tensor(gs2[:], tanh_g[:], 1.0, gT[:], ALU.add, ALU.mult).then_inc(sem("gs2"), 1)
            dve.wait_ge(sem("tanh_xc"), 1)
            dve.scalar_tensor_tensor(xs2[:], tanh_xc[:], 1.0, xc[:], ALU.add, ALU.mult).then_inc(sem("xs2"), 1)
            dve.memset(decay[:, :, :, 0:1], 0.0).then_inc(sem("decay_zero"), 1)
            dve.wait_ge(sem("bc"), 1)
            link(dve.tensor_scalar(bcT[:], PS[0:2 * N, 3, 0:T], 0.5, sm("bc_b", 2 * N), ALU.mult, ALU.add))
            def bc_half(h):
                n = slice(h * N // 2, (h + 1) * N // 2)
                dve.tensor_tensor(bc_own[:, n, :], bcT[:].unsqueeze(1).to_broadcast([2 * N, N // 2, T]),
                                  sm("own", 2 * N)[:, n].unsqueeze(2).to_broadcast([2 * N, N // 2, T]), ALU.mult).then_inc(sem("bc_own"), 1)

            bc_half(0)
            dve.wait_ge(sem("dt"), 1)
            for b in range(2):
                dve.tensor_scalar(z[:, b, :], PS[:, 4, T * b:T * b + T], of("late", "dup_b", b, b + 1), None, ALU.add).then_inc(sem("z"), 1)
            dve.wait_ge(sem("z"), 2)
            dve.scalar_tensor_tensor(zneg[:], z[:], -1.0, z[:], ALU.mult, ALU.min).then_inc(sem("zneg"), 1)
            bc_half(1)
            link(dve.tensor_scalar(zpos[:], z[:], 0.0, None, ALU.max))
            dve.wait_ge(sem("xs2"), 1)
            dve.wait_ge(sem("lz"), 1)
            dve.tensor_tensor(delta[:], zpos[:], lz[:], ALU.add).then_inc(sem("delta"), 1)
            dve.wait_ge(sem("delta"), 1)
            dve.wait_ge(sem("expA"), 1)
            dve.tensor_tensor(dA[:, 0], delta[:, 0:1, :].to_broadcast([D, N, T]), expA[:, 0, :].unsqueeze(2).to_broadcast([D, N, T]), ALU.mult).then_inc(sem("dA0"), 1)
            dve.scalar_tensor_tensor(dx[:], delta[:], 0.5, xs2[:], ALU.mult, ALU.mult).then_inc(sem("dx"), 1)
            dve.wait_ge(sem("dx"), 1)
            for b in range(2):
                if b == 1:
                    dve.wait_ge(sem("Bx1"), 2)
                else:
                    for h in range(2):
                        n = slice(h * N // 2, (h + 1) * N // 2)
                        dve.wait_ge(sem("b_rows"), h + 1)
                        link(dve.tensor_tensor(Bx[:, b, n], b_rows[:, n], dx[:, b:b + 1, :].to_broadcast([D, N // 2, T]), ALU.mult))
                    dve.wait_ge(sem("decay_zero"), 1)
                dve.wait_ge(sem("decay"), b + 1)
                flat = [a[:, b].rearrange("p n t -> p (n t)") for a in (hs, decay, Bx)]
                dve.tensor_tensor_scan(flat[0], flat[1], flat[2], 0.0, ALU.mult, ALU.add).then_inc(sem("scanned"), 1)
            dve.wait_ge(sem("gs2"), 1)
            for b in (1, 0):
                if b == 0:
                    dve.wait_ge(sem("hC0"), 2)
                else:
                    dve.wait_ge(sem("scanned"), 2)
                    dve.wait_ge(sem("c_rows"), 2)
                    link(dve.tensor_tensor(hC[:, b], c_rows, hs[:, b], ALU.mult))
                link(dve.reduce_sum(y[:, b, :], hC[:, b].rearrange("p n t -> p t n"), X))
                dve.scalar_tensor_tensor(yg[:, b, :], y[:, b, :], 0.5, gs2[:, b, :], ALU.mult, ALU.mult).then_inc(sem("yg"), 1)
            dve.wait_ge(sem("ssm"), 1)
            dve.wait_ge(sem("xr"), 1)
            dve.tensor_tensor(x5[:], PS[0:T, 4, 256:256 + D], xr[:], ALU.add).then_inc(sem("x5"), 1)
            dve.wait_ge(sem("x5"), 1)

            layer_norm("x5", x5[:])
            dve.wait_ge(sem("norm_turned"), 7)
            dve.tensor_copy(x6T[:], PS[:, 1, 0:T]).then_inc(sem("norm_columns"), 1)
            dve.wait_ge(sem("ff6"), 1)
            dve.tensor_copy(x6[:], PS[:, 2, 128:128 + T]).then_inc(sem("x6"), 1)

        @block.tensor
        def _(pe):
            mm = pe.matmul

            def turn(out_, in_):
                return pe.transpose(out_, in_, ident[0:T, 0:T])

            fills = iter(range(CHUNKS))

            def fill(n=1):
                for _ in range(n):
                    c = next(fills)
                    if c >= 2:
                        pe.wait_ge(sem("fill_out"), c - 1)
                    if c == 0:
                        for j in range(4):
                            pe.wait_ge(sem(f"ctxT_in{j}"), 32)
                    for t in range(width(c) // D):
                        tile = CHUNK * c + t
                        ins = mm(PS[:, F_BANKS[c % 2], D * t:D * t + D], ctxT[:, D * tile:D * tile + D], of("second", "WvT"), start=True, stop=True)
                    ins.then_inc(sem("fill"), 1)

            pe.wait_ge(sem("first_in"), 16)
            pe.wait_ge(sem("normed"), nth("x"))
            turn(PS[:, 7, 0:T], nm("x")).then_inc(sem("norm_turned"), 1)
            pe.wait_ge(sem("norm_columns"), 1)
            mm(PS[:, 7, 64:64 + T], of("first", "W0"), xnT[:, 0, :], start=True, stop=True)
            mm(PS[:, 7, 128:129], xnT[:].rearrange("p a n -> p (a n)"), of("first", "b0"), start=True, stop=True).then_inc(sem("qW"), 1)
            pe.wait_ge(sem("qWT"), 1)
            for j in range(7):
                piece = [lo <= j < hi for lo, hi in PIECES].index(True)
                pe.wait_ge(sem(f"ctxT_in{piece}"), 32)
                if j >= 2:
                    pe.wait_ge(sem("s0_out"), j - 1)
                bank = PS[:, S_BANKS[j % 2], :]
                if j < 6:
                    a = HALF0 * D + 512 * j
                    mm(bank[0:T, :], qWT[:], ctxT[:, 512 * j:512 * j + 512], start=True, stop=True)
                    mm(bank[T:D, :], qWT[:], ctxT[:, a:a + 512], start=True, stop=True).then_inc(sem("s0"), 1)
                else:
                    mm(bank[0:T, 0:D], qWT[:], ctxT[:, 512 * j:512 * j + D], start=True, stop=True).then_inc(sem("s0"), 1)
            pe.wait_ge(sem("nmax0"), 1)
            pe.wait_ge(sem("second_in"), 16)
            mm(PS[:, 7, 130:131], of("second", "swap"), nmax0[:], start=True, stop=True).then_inc(sem("nmax_other"), 1)
            pe.wait_ge(sem("constants"), CONSTANTS)
            for c in range(8):
                if c < 7:
                    pe.wait_ge(sem("exp0"), c + 1)
                    if c >= 2:
                        pe.wait_ge(sem("pT0"), c - 1)
                    for t in range(CHUNK * c, min(CHUNK * c + CHUNK, HALF0)):
                        ins = pe.transpose(PS[:, T_BANKS[c % 2], (t % CHUNK) * D:(t % CHUNK + 1) * D], scoresA[:, D * t:D * t + D], ident)
                    ins.then_inc(sem("turned0"), 1)
                if c >= 1:
                    pe.wait_ge(sem("pT0"), c)
                    j = (c - 1) // 2
                    pe.wait_ge(sem(f"ctxN_in{j}"), 32 if j < 3 else 16)
                    for t in range(CHUNK * (c - 1), min(CHUNK * c, HALF0)):
                        w = pT[:, (c - 1) % 3, (t % CHUNK) * D:(t % CHUNK + 1) * D]
                        ins = mm(PS[0:T, 4, 0:D], w[:, 0:T], ctxN[:, t, :], start=(t == 0), stop=(t == HALF0 - 1))
                        if t < HALF1:
                            ins = mm(PS[T:D, 4, 0:D], w[:, T:D], ctxN[:, HALF0 + t, :], start=(t == 0), stop=(t == HALF1 - 1))
                    ins.then_inc(sem("pv0"), 1)
            pe.wait_ge(sem("wl"), 1)
            mm(PS[:, 7, 132:133], of("second", "pair_sum"), wl[:], start=True, stop=True).then_inc(sem("l_both"), 1)
            pe.wait_ge(sem("o_sc"), 1)
            mm(PS[:, 7, 192:192 + T], o_sc[:], of("second", "stack"), start=True, stop=True).then_inc(sem("att"), 1)
            pe.wait_ge(sem("rows_in"), 16)
            pe.wait_ge(sem("ones_ready"), 1)
            mm(PS[0:T, 3, 256:256 + D], ones[:], row("b0"), start=True, stop=False)
            pe.wait_ge(sem("attT"), 1)
            mm(PS[0:T, 3, 256:256 + D], attT[:], of("second", "W0T"), start=False, stop=True).then_inc(sem("xattn"), 1)
            fill(2)

            pe.wait_ge(sem("mats_in"), 16)
            pe.wait_ge(sem("normed"), nth("x1"))
            turn(PS[:, 4, 0:T], nm("x1")).then_inc(sem("norm_turned"), 1)
            pe.wait_ge(sem("norm_columns"), 2)
            mm(PS[:, 0, 0:T], of("mats", "Wq"), xn1T[:, 0, :], start=True, stop=True)
            mm(PS[:, 0, T:2 * T], of("mats", "Wk"), xn1T[:, 0, :], start=True, stop=True).then_inc(sem("qkT"), 1)
            mm(PS[0:HD0, 1, 0:T], of("mats", "Wg1"), xn1T[:, 0, :], start=True, stop=True).then_inc(sem("g1"), 1)
            mm(PS[:, 2, 0:D], xn1T[:].rearrange("p a n -> p (a n)"), of("mats", "Wv"), start=True, stop=True).then_inc(sem("v0"), 1)
            pe.wait_ge(sem("s2"), 1)
            mm(PS[:, 3, 0:2 * T], of("mats", "rotT"), s2[:].rearrange("p a n -> p (a n)"), start=True, stop=True).then_inc(sem("rotated"), 1)
            pe.wait_ge(sem("small_in"), 16)
            pe.wait_ge(sem("g1T"), 1)
            mm(PS[0:T, 7, 256:256 + D], g1T[:], sm("Wg2", HD0), start=True, stop=True).then_inc(sem("gate"), 1)
            fill(1)
            pe.wait_ge(sem("q_heads"), 1)
            mm(PS[0:T, 0, :], qk[:, 1, :], q_heads[:, 0:8, :].rearrange("p h n -> p (h n)"), start=True, stop=True)
            pe.wait_ge(sem("q_heads"), 2)
            mm(PS[T:D, 0, :], qk[:, 1, :], q_heads[:, 8:16, :].rearrange("p h n -> p (h n)"), start=True, stop=True).then_inc(sem("energy"), 1)
            fill(1)
            pe.wait_ge(sem("v_halves"), 2)
            pe.wait_ge(sem("masked"), 1)
            v4 = v_halves[:].rearrange("p a (h d) -> p a h d", d=HD0)
            o4 = PS[0:T, 1, 128:128 + D].rearrange("p (a h d) -> p a h d", a=2, d=HD0)
            for h in range(8):
                ins = mm(o4[:, :, h, :], energy[:, h, :], v4[:, :, h, :], start=True, stop=True)
            ins.then_inc(sem("lin_att"), 1)
            fill(2)
            pe.wait_ge(sem("normed"), nth("gated"))
            turn(PS[:, 4, 64:64 + T], nm("gated")).then_inc(sem("norm_turned"), 1)
            pe.wait_ge(sem("norm_columns"), 3)
            mm(PS[0:T, 4, 128:128 + D], yT[:], of("mats", "Wo"), start=True, stop=True).then_inc(sem("attn_out"), 1)
            fill(2)

            pe.wait_ge(sem("normed"), nth("tgt"))
            turn(PS[:, 0, 0:T], nm("tgt")).then_inc(sem("norm_turned"), 1)
            pe.wait_ge(sem("norm_columns"), 4)
            mm(PS[:, 1, 0:T], of("mats", "saWvT"), tgtT[:], start=True, stop=True).then_inc(sem("v1"), 1)
            mm(PS[0:T, 2, 128:128 + D], ones[:], row("sa_out_b"), start=True, stop=False)
            pe.wait_ge(sem("vT"), 1)
            mm(PS[0:T, 2, 128:128 + D], vT[:], of("mats", "sa_outT"), start=False, stop=True).then_inc(sem("sa"), 1)
            fill(3)
            pe.wait_ge(sem("normed"), nth("t1"))
            turn(PS[:, 0, 64:64 + T], nm("t1")).then_inc(sem("norm_turned"), 1)
            pe.wait_ge(sem("norm_columns"), 5)
            mm(PS[:, 4, 256:256 + T], of("mats", "WqT"), z6T[:], start=True, stop=True).then_inc(sem("q1"), 1)
            fill(2)

            qw = q_wide[:].rearrange("p h n -> p (h n)")
            pe.wait_ge(sem("q_wide"), 2)
            mm(PS[:, 2, 0:2 * T], of("mats", "Wk1"), qw[:, 0:2 * T], start=True, stop=True)
            mm(PS[:, 2, 480:481], qw[:, 0:2 * T], of("mats", "bk"), start=True, stop=True).then_inc(sem("qk1"), 1)
            pe.wait_ge(sem("qk1_out"), 1)

            def score(n):
                g, c = divmod(n, CHUNKS)
                if n == 3:
                    pe.wait_ge(sem("cp1"), 1)
                if n == CHUNKS:
                    pe.wait_ge(sem("qk1_out"), 2)
                if n >= 4:
                    pe.wait_ge(sem("s1_out"), n - 3)
                for t in range(width(c) // D):
                    a = 512 * c + D * t
                    ins = mm(PS[:, S_BANKS[n % 4], D * t:D * t + D], ctxT[:, a:a + D], qk1[:, 2 * g:2 * g + 2, :].rearrange("p a n -> p (a n)"), start=True, stop=True)
                ins.then_inc(sem("s1"), 1)

            def apply_weights(n):
                g, c = divmod(n, CHUNKS)
                pe.wait_ge(sem("exp1"), n + 1)
                if g >= 2 and c == 0:
                    pe.wait_ge(sem("oS"), g - 1)
                for p in range(2):
                    for t in range(width(c) // D):
                        tile = CHUNK * c + t
                        a = (tile * H1 + 2 * g + p) * HV
                        ins = mm(PS[32 * t:32 * t + 32, O_BANKS[g % 2], T * p:T * p + T], V[:, a:a + 32], chunk1(n)[:, D * t + T * p:D * t + T * p + T],
                                 start=(c == 0 and p == 0), stop=(p == 1 and tile + CHUNK >= TILES))
                ins.then_inc(sem("pv"), 1)

            pe.wait_ge(sem("b_lo"), 1)
            pe.transpose(PS[0:32, 7, 384:400], b_lo[LO % 2], ident[0:16, 0:16]).then_inc(sem("b_turned"), 1)
            pe.wait_ge(sem("fill_out"), CHUNKS)
            pe.wait_ge(sem("constants"), CONSTANTS)
            for n in range(STEPS1 + LAG + 6):
                g, c = divmod(n - 1, CHUNKS)
                if n < STEPS1:
                    score(n)
                if n == 5:
                    pe.wait_ge(sem("q_wide"), 3)
                    mm(PS[:, 3, 0:6 * T], of("mats", "Wk1"), qw[:, 2 * T:], start=True, stop=True)
                    for p in range(1, PAIRS):
                        ins = mm(PS[:, 3, 480 + p:481 + p], qw[:, 2 * T * p:2 * T * p + 2 * T], of("mats", "bk"), start=True, stop=True)
                    ins.then_inc(sem("qk1"), 1)
                if LAG + 3 <= n < STEPS1 + LAG + 3:
                    apply_weights(n - LAG - 3)
                if c == 0 and 1 <= g <= PAIRS:
                    pe.wait_ge(sem("tile_max"), g)
                    if g >= 2:
                        pe.wait_ge(sem("shift"), g - 1)
                    pe.transpose(PS[:, 3, 0:D], tile_max[:], ident).then_inc(sem("max_turned"), 1)
                if c == 1 and 1 <= g <= PAIRS:
                    pe.wait_ge(sem("shift_cols"), g)
                    mm(PS[:, 3, D:2 * D], shift_cols[:], ident, start=True, stop=True).then_inc(sem("shift_rows"), 1)
                done, late = divmod(n - LAG - CHUNKS - 2, CHUNKS)
                if 0 <= done < PAIRS and late == 2:
                    pe.wait_ge(sem("oS"), done + 1)
                    if done:
                        pe.wait_ge(sem("ca"), 2 * done)
                    mm(PS[:, 5, 0:32], oS[:, done % 2, :], of("mats", "sumsel"), start=True, stop=True).then_inc(sem("heads"), 1)
            pe.wait_ge(sem("ca"), 2 * PAIRS)
            turn(PS[:, 0, 0:T], ca[:]).then_inc(sem("caT"), 1)
            mm(PS[0:T, 1, 256:256 + D], ones[:], row("mha_out_b"), start=True, stop=False)
            pe.wait_ge(sem("caT_out"), 1)
            mm(PS[0:T, 1, 256:256 + D], caT[:], of("mats", "mha_outT"), start=False, stop=True).then_inc(sem("mha"), 1)
            pe.wait_ge(sem("b_up"), 1)
            b_up = b_hi[(STAGES - LO) % 2]
            for q in range(4):
                ins = mm(PS[32 * q:32 * q + 32, 6, 0:FB], ident[0:32, 0:32], b_up.rearrange("p (b q) -> p b q", q=4)[:, :, q], start=True, stop=True)
            ins.then_inc(sem("b_columns"), 1)
            pe.wait_ge(sem("normed"), nth("t2"))
            turn(PS[:, 2, 0:T], nm("t2")).then_inc(sem("norm_turned"), 1)
            pe.wait_ge(sem("late_in"), 16)
            pe.wait_ge(sem("norm_columns"), 6)
            for b in (2, 3, 0, 1):
                ins = mm(PS[:, b // 2, T * (b % 2):T * (b % 2) + T], of("late", "lin1T", D * b, D * b + D), z7T[:], start=True, stop=True)
                if b % 2:
                    ins.then_inc(sem("lin1_b" if b == 3 else "lin1_a"), 1)
            mm(PS[0:T, 2, 128:128 + D], ones[:], row("lin2_b"), start=True, stop=False)
            pe.wait_ge(sem("h_act"), 2)
            pe.wait_ge(sem("h_dve"), 2)
            for b in range(FB):
                ins = mm(PS[0:T, 2, 128:128 + D], hT[:, b, :], of("late", "lin2T", D * b, D * b + D), start=False, stop=(b == FB - 1))
            ins.then_inc(sem("ff"), 1)
            pe.wait_ge(sem("normed"), nth("rms"))
            turn(PS[:, 2, 256:256 + T], nm("rms")).then_inc(sem("rmsT"), 1)
            pe.wait_ge(sem("hmT"), 1)
            for b in range(4):
                ins = mm(PS[:, b // 2, T * (b % 2):T * (b % 2) + T], of("late", "in_W", D * b, D * b + D), hmT[:], start=True, stop=True)
                if b % 2:
                    ins.then_inc(sem("x_in1" if b == 1 else "gate1"), 1)
            pe.wait_ge(sem("xs2"), 1)
            dbc = of("late", "dbc_W").rearrange("p (b j) -> p b j", b=2)
            for b in range(2):
                ins = mm(PS[0:N, 2, 0:T], dbc[:, b, 0:N], xs2[:, b, :], start=(b == 0), stop=(b == 1))
            ins.then_inc(sem("dt_low"), 1)
            for b in range(2):
                ins = mm(PS[0:2 * N, 3, 0:T], dbc[:, b, N:3 * N], xs2[:, b, :], start=(b == 0), stop=(b == 1))
            ins.then_inc(sem("bc"), 1)
            pe.wait_ge(sem("dtT"), 1)
            for b in range(2):
                ins = mm(PS[:, 4, T * b:T * b + T], sm("dup_W", N)[:, D * b:D * b + D], dtT[:], start=True, stop=True)
            ins.then_inc(sem("dt"), 1)
            own = bc_own.rearrange("p n t -> p (n t)")
            for name, bank, done in (("onesB", 0, "b_wide"), ("onesC", 2, "c_wide")):
                for h in range(2):
                    pe.wait_ge(sem("bc_own"), h + 1 if bank == 0 else 2)
                    mm(PS[:, bank + h, :], sm(name, 2 * N), own[:, 512 * h:512 * h + 512], start=True, stop=True).then_inc(sem(done), 1)
            pe.wait_ge(sem("dn_done"), 1)
            for b in range(FB):
                ins = pe.transpose(PS[:, 7, D * b:D * b + D], hidden["dn"][STAGES % 2][:, D * b:D * b + D], ident)
            ins.then_inc(sem("dn_turned"), 1)
            pe.wait_ge(sem("z"), 2)
            mm(PS[0:T, 4, 256:256 + D], ones[:], row("out_b"), start=True, stop=False)
            for b in (1, 0):
                pe.wait_ge(sem("yg"), 2 - b)
                ins = mm(PS[0:T, 4, 256:256 + D], yg[:, b, :], of("late", "out_W", D * b, D * b + D), start=False, stop=(b == 0))
            ins.then_inc(sem("ssm"), 1)

            pe.wait_ge(sem("c_rows"), 2)
            result = [(PS[T * h:T * h + T, 2, 128:128 + T], slice(T * h, T * h + T)) for h in range(2)]
            for o, cols in result:
                mm(o, ones[:], row("b_con")[:, cols], start=True, stop=False)
                mm(o, ones[:], row("down_bias")[:, cols], start=False, stop=False)
            pe.wait_ge(sem("normed"), nth("x5"))
            turn(PS[:, 1, 0:T], nm("x5")).then_inc(sem("norm_turned"), 1)
            pe.wait_ge(sem("up_done"), 1)
            pe.wait_ge(sem("norm_columns"), 7)
            for b in range(FB):
                ins = mm(PS[:, 0, T * b:T * b + T], wup[:, D * b:D * b + D], x6T[:], start=True, stop=True)
            ins.then_inc(sem("h6"), 1)
            for o, cols in result:
                mm(o, ident[0:T, 0:T], x5[:, cols], start=False, stop=False)
            pe.wait_ge(sem("wdn"), 1)
            for b in range(FB):
                pe.wait_ge(sem("gelu"), b + 1)
                for o, cols in result:
                    ins = mm(o, gl6[:, b, :], wdn[:, b, cols], start=False, stop=(b == FB - 1))
            ins.then_inc(sem("ff6"), 1)


def shape_constants():
    eye = np.eye(D, dtype=np.float32)
    c = {"ident": eye, "swap": np.roll(eye, T, axis=0)}
    c["pair_sum"] = np.tile(np.eye(T, dtype=np.float32), (2, 2))
    c["stack"] = np.tile(np.eye(T, dtype=np.float32), (2, 1))
    inv = 1.0 / np.float32(10000.0) ** (np.arange(0, HD0, 2, dtype=np.float32) / np.float32(HD0))
    ang = np.arange(T, dtype=np.float32)[:, None] * inv[None, :].astype(np.float32)
    c["cosT"] = np.tile(np.cos(ang).T, (2 * H0, 1))
    c["sinT"] = np.tile(np.sin(ang).T, (2 * H0, 1))
    rot = np.zeros((D, D), np.float32)
    for i in range(D):
        rot[i, i + 4 if i % 8 < 4 else i - 4] = -1.0 if i % 8 < 4 else 1.0
    c["rotT"] = rot.T
    r = np.arange(D)
    c["head"] = (r[:, None] // HD0 == np.arange(H0)[None, :]).astype(np.float32)
    c["causal"] = (r[:, None] % T <= np.arange(T)[None, :]).astype(np.float32) * np.float32(0.125)
    c["head1"] = (r[:, None] // HD1 == np.arange(H1)[None, :]).astype(np.float32) * np.float32(HD1 ** -0.5)
    c["sumsel"] = np.tile(np.eye(32, dtype=np.float32), (4, 1))
    n = np.arange(2 * N)
    c["own"] = (n[:, None] % N == np.arange(N)[None, :]).astype(np.float32)
    c["onesB"] = np.repeat((n[:, None] < N).astype(np.float32), D, axis=1)
    c["onesC"] = np.repeat((n[:, None] >= N).astype(np.float32), D, axis=1)
    return c


def stage_weights(w, turned):
    f = np.arange(FF)
    out = np.empty((STAGES, 2, FF), w.dtype)
    for k in range(STAGES):
        s = 1 << k
        pair, second = (f // (2 * s)) * s + f % s, (f // s) % 2
        out[k, 0] = w[k, pair, second, second]
        i, j = (1 - second, second) if turned else (second, 1 - second)
        out[k, 1] = w[k, pair, i, j]
    return out


def kernel(**inputs):
    import concourse.bacc as bacc
    from concourse.bass_utils import run_bass_kernel_spmd as run

    a = {k: np.asarray(v) for k, v in inputs.items()}
    c = shape_constants()

    def col(v):
        return v.reshape(-1, D).T

    def blocks(w):
        return w.reshape(-1, D, w.shape[1]).transpose(1, 0, 2).reshape(D, -1)

    in_proj, in_proj_b = a["L1_xattn_in_proj_w"], a["L1_xattn_in_proj_b"]
    up_w, dn_w = stage_weights(a["L1_ffn_up_weights"], False), stage_weights(a["L1_ffn_down_weights"], True)
    coef_lo = up_w[:LO].reshape(LO, 2, 16, 32).transpose(2, 0, 1, 3).reshape(16, -1)
    coef_hi = up_w[LO:].reshape(STAGES - LO, 2, 16, 32).transpose(3, 0, 1, 2).reshape(32, -1)
    conv = a["L1_attn_conv_w"]
    values = dict(c)
    values.update({
        "W0": a["L0_xattn_W"], "W0T": a["L0_xattn_W"].T, "b0": col(a["L0_xattn_b"]),
        "Wk1": in_proj[D:2 * D], "WvT": in_proj[2 * D:].T, "bk": col(in_proj_b[D:2 * D]),
        "Wq": a["L0_attn_Wq"], "Wk": a["L0_attn_Wk"], "Wv": a["L0_attn_Wv"], "Wg1": a["L0_attn_Wg1"], "Wo": a["L0_attn_Wo"],
        "ln_w": col(a["L0_attn_ln_w"]), "ln_b": col(a["L0_attn_ln_b"]),
        "saWvT": a["L1_xattn_qkv_w"][2 * D:].T, "sa_bv": col(a["L1_xattn_qkv_b"][2 * D:]), "sa_outT": a["L1_xattn_sa_out_w"].T,
        "ln1_g": col(a["L1_xattn_ln1_g"]), "ln1_b": col(a["L1_xattn_ln1_b"]),
        "WqT": in_proj[:D].T, "bq": col(in_proj_b[:D]), "bv": col(in_proj_b[2 * D:]), "mha_outT": a["L1_xattn_mha_out_w"].T,
        "ln2_g": col(a["L1_xattn_ln2_g"]), "ln2_b": col(a["L1_xattn_ln2_b"]),
        "lin1T": a["L1_xattn_lin1_w"].T, "lin1_b": col(a["L1_xattn_lin1_b"]), "lin2T": blocks(a["L1_xattn_lin2_w"].T),
        "rms_w": col(a["L1_attn_rms_w"]), "in_W": a["L1_attn_in_W"], "in_b": col(a["L1_attn_in_b"]),
        "conv_w": blocks(conv), "conv_b": col(a["L1_attn_conv_b"]), "A_log": blocks(a["L1_attn_A_log"]),
        "dbc_W": blocks(a["L1_attn_dbc_W"]), "dup_b": col(a["L1_attn_dup_b"]), "out_W": blocks(a["L1_attn_out_W"]),
        "up_bias": col(a["L1_ffn_up_bias"]),
        "exp": a["L1_ffn_W_exp"], "conT": a["L1_ffn_W_con"].T,
    })
    small_at, small_w = offsets(SMALL)
    small = np.zeros((32, small_w), np.float32)
    dbc_b = a["L1_attn_dbc_b"][:, None]
    for name, v in (("Wg2", a["L0_attn_Wg2"]), ("dup_W", a["L1_attn_dup_W"]), ("dt_b", dbc_b[:N]), ("bc_b", dbc_b[N:]),
                    ("own", c["own"]), ("onesB", c["onesB"]), ("onesC", c["onesC"]),
                    ("b_exp", a["L1_ffn_b_exp"].reshape(16, 32)), ("coef_lo", coef_lo), ("coef_hi", coef_hi)):
        small[0:v.shape[0], small_at[name][0]:small_at[name][1]] = v
    ctx = a["ctx_1024"][0]
    row_values = {"b0": "L0_xattn_b", "sa_out_b": "L1_xattn_sa_out_b", "mha_out_b": "L1_xattn_mha_out_b", "lin2_b": "L1_xattn_lin2_b",
                  "out_b": "L1_attn_out_b", "b_con": "L1_ffn_b_con", "down_bias": "L1_ffn_down_bias"}
    wide_values = {n: "L1_xattn_" + n for n in WIDE}
    wide_values.update({"ffn_g": "L0_ffn_ln_g", "ffn_b": "L0_ffn_ln_b"})
    arrays = {
        "x_in": a["x"][0], "ctxT_in": ctx.T, "ctxN_in": ctx.reshape(TILES, D, D).transpose(1, 0, 2),
        **{f"{p}_in": np.concatenate([values[n] for n, _ in entries], axis=1) for p, entries in PACKS.items()},
        "rows_in": np.concatenate([a[row_values[n]] for n in ROWS])[None, :],
        "wide_in": np.broadcast_to(np.concatenate([a[wide_values[n]] for n in WIDE]), (T, len(WIDE) * D)),
        "small_in": small, "coef_in": np.concatenate([up_w, dn_w[::-1]]).reshape(2 * STAGES, -1),
    }
    nc = bacc.Bacc("TRN2", target_bir_lowering=False, num_devices=1)
    arrays = {k: np.ascontiguousarray(v) for k, v in arrays.items()}
    aps = {k: nc.dram_tensor(k, v.shape, mybir.dt.from_np(v.dtype), kind="ExternalInput").ap() for k, v in arrays.items()}
    out = nc.dram_tensor("out", (T, D), mybir.dt.float32, kind="ExternalOutput").ap()
    build(nc, out=out, **aps)
    r = run(nc, [arrays], core_ids=[0])
    return r.results[0]["out"].reshape(1, T, D)
```
